# Optimizing a Trainium2 kernel written in Bass

```python
import numpy as np
import jax
import jax.numpy as jnp

def _softmax(x, axis=-1):
    return jax.nn.softmax(x, axis=axis)

def _gelu(x):
    return jax.nn.gelu(x, approximate=True)

def _silu(x):
    return jax.nn.silu(x)

def _sigmoid(x):
    return jax.nn.sigmoid(x)

def _layernorm(x, axis=-1, eps=1e-05):
    m = jnp.mean(x, axis=axis, keepdims=True)
    v = jnp.var(x, axis=axis, keepdims=True)
    return (x - m) / jnp.sqrt(v + eps)

def _scatter_add(tgt, idx, src, axis=0):
    return tgt.at[idx].add(src)

def _segment_sum(src, seg, n):
    return jax.ops.segment_sum(src, seg, n)
kernel_name = 'mk_lm_tower_d2_tok_ids1024_r4_fd500e'

def setup_inputs(seed: int=0):
    np.random.seed(seed)
    _w = jnp.asarray

    def _rec_inputs():
        import jax
        import jax.numpy as jnp
        _rk = jax.random.key(seed)
        x = jax.random.randint(jax.random.fold_in(_rk, 1), (4, 512), 0, 31993, jnp.int32)
        return x
    x = _rec_inputs()

    def _L0_tok_setup():
        import jax, jax.numpy as jnp
        import numpy as np
        V, D, CTX, NL = (8000, 256, 512, 2)
        B, T = (4, 512)
        EPS = 1e-05

        def _layer_norm(x, gamma, beta):
            mu = jnp.mean(x, axis=-1, keepdims=True)
            var = jnp.var(x, axis=-1, keepdims=True)
            return gamma * (x - mu) / jnp.sqrt(var + EPS) + beta
        key = jax.random.key(seed)
        ks = jax.random.split(key, 12)
        s = 0.02
        return {'x': jax.random.randint(ks[0], (B, T), 0, V), 'emb': jax.random.normal(ks[1], (V, D), jnp.float32) * s, 'pos': jax.random.normal(ks[2], (CTX, D), jnp.float32) * s, 'wq': jax.random.normal(ks[3], (NL, D, D), jnp.float32) * s, 'wk': jax.random.normal(ks[4], (NL, D, D), jnp.float32) * s, 'wv': jax.random.normal(ks[5], (NL, D, D), jnp.float32) * s, 'wo': jax.random.normal(ks[6], (NL, D, D), jnp.float32) * s, 'wup': jax.random.normal(ks[7], (NL, D, 4 * D), jnp.float32) * s, 'bup': jnp.zeros((NL, 4 * D), jnp.float32), 'wdown': jax.random.normal(ks[8], (NL, 4 * D, D), jnp.float32) * s, 'bdown': jnp.zeros((NL, D), jnp.float32), 'ga': jnp.ones((NL, D), jnp.float32), 'ba': jnp.zeros((NL, D), jnp.float32), 'gm': jnp.ones((NL, D), jnp.float32), 'bm': jnp.zeros((NL, D), jnp.float32)}
    _L0_tok_all = _L0_tok_setup()
    _L0_tok_in = {k: v for k, v in _L0_tok_all.items() if k in ('emb', 'pos', 'wq', 'wk', 'wv', 'wo', 'wup', 'bup', 'wdown', 'bdown', 'ga', 'ba', 'gm', 'bm')}
    del _L0_tok_all

    def _L0_attn_setup():
        import jax, jax.numpy as jnp
        import numpy as np
        B, T, C = (4, 512, 256)
        NUM_HEADS = 16
        OUT_DIM = 256
        HEAD_DIM = OUT_DIM // NUM_HEADS
        key = jax.random.key(seed)
        kx, kk, kq, kv, kp = jax.random.split(key, 5)
        return {'x': jax.random.normal(kx, (B, T, C), dtype=jnp.float32), 'W_key': jax.random.normal(kk, (OUT_DIM, C), dtype=jnp.float32), 'W_query': jax.random.normal(kq, (OUT_DIM, C), dtype=jnp.float32), 'W_value': jax.random.normal(kv, (OUT_DIM, C), dtype=jnp.float32), 'W_proj': jax.random.normal(kp, (OUT_DIM, OUT_DIM), dtype=jnp.float32)}
    _L0_attn_all = _L0_attn_setup()
    _L0_attn_in = {k: v for k, v in _L0_attn_all.items() if k in ('W_key', 'W_query', 'W_value', 'W_proj')}
    del _L0_attn_all

    def _L0_ffn_setup():
        import jax, jax.numpy as jnp
        import numpy as np
        B, S, D, E = (2, 512, 256, 8)
        key = jax.random.key(seed)
        ks = jax.random.split(key, 5)
        x = jax.random.normal(ks[0], (B, S, D), dtype=jnp.float32)
        router_w = jax.random.normal(ks[1], (E, D), dtype=jnp.float32) * 0.02
        router_b = jnp.zeros((E,), dtype=jnp.float32)
        expert_w = jax.random.normal(ks[2], (E, D, D), dtype=jnp.float32) * 0.02
        expert_b = jnp.zeros((E, D), dtype=jnp.float32)
        return {'x': x, 'router_w': router_w, 'router_b': router_b, 'expert_w': expert_w, 'expert_b': expert_b}
    _L0_ffn_all = _L0_ffn_setup()
    _L0_ffn_in = {k: v for k, v in _L0_ffn_all.items() if k in ('router_w', 'router_b', 'expert_w', 'expert_b')}
    del _L0_ffn_all

    def _L1_attn_setup():
        import math
        import jax, jax.numpy as jnp
        import numpy as np
        EMB = 256
        HEADS = 16
        HEAD_DIM = EMB // HEADS

        def _srms_norm(x, eps=1e-12):
            dtype = x.dtype
            xf = x.astype(jnp.float32)
            scale = 1.0 / math.sqrt(x.shape[-1])
            n = jnp.linalg.norm(xf * scale, axis=-1, keepdims=True)
            return (xf / jnp.maximum(n, eps)).astype(dtype)
        key = jax.random.key(seed)
        ks = jax.random.split(key, 6)
        b, l = (4, 1024)
        x = jax.random.normal(ks[0], (b, l, EMB), dtype=jnp.float32)
        std = math.sqrt(2.0 / (EMB + EMB))
        Wq = jax.random.normal(ks[1], (EMB, EMB), dtype=jnp.float32) * std
        Wk = jax.random.normal(ks[2], (EMB, EMB), dtype=jnp.float32) * std
        Wv = jax.random.normal(ks[3], (EMB, EMB), dtype=jnp.float32) * std
        Wu = jax.random.normal(ks[4], (EMB, EMB), dtype=jnp.float32) * std
        Wo = jax.random.normal(ks[5], (EMB, EMB), dtype=jnp.float32) * std
        return {'x': x, 'Wq': Wq, 'Wk': Wk, 'Wv': Wv, 'Wu': Wu, 'Wo': Wo}
    _L1_attn_all = _L1_attn_setup()
    _L1_attn_in = {k: v for k, v in _L1_attn_all.items() if k in ('Wq', 'Wk', 'Wv', 'Wu', 'Wo')}
    del _L1_attn_all

    def _L1_ffn_setup():
        import jax, jax.numpy as jnp
        import numpy as np
        D_MODEL = 256
        D_FF = 512
        NUM_EXPERTS = 16
        TOP_K = 2
        CAPACITY_FACTOR = 1.25
        BATCH, SEQ = (4, 512)
        key = jax.random.key(seed)
        k0, k1, k2, k3 = jax.random.split(key, 4)
        x = jax.random.normal(k0, (BATCH, SEQ, D_MODEL), jnp.float32)
        gate_w = jax.random.normal(k1, (NUM_EXPERTS, D_MODEL), jnp.float32) / np.float32(np.sqrt(D_MODEL))
        w1 = jax.random.normal(k2, (NUM_EXPERTS, D_MODEL, D_FF), jnp.float32) / np.float32(np.sqrt(D_MODEL))
        w2 = jax.random.normal(k3, (NUM_EXPERTS, D_FF, D_MODEL), jnp.float32) / np.float32(np.sqrt(D_FF))
        return {'x': x, 'gate_w': gate_w, 'w1': w1, 'w2': w2}
    _L1_ffn_all = _L1_ffn_setup()
    _L1_ffn_in = {k: v for k, v in _L1_ffn_all.items() if k in ('gate_w', 'w1', 'w2')}
    del _L1_ffn_all
    return {'x': x, 'L0_tok_emb': _L0_tok_in['emb'], 'L0_tok_pos': _L0_tok_in['pos'], 'L0_tok_wq': _L0_tok_in['wq'], 'L0_tok_wk': _L0_tok_in['wk'], 'L0_tok_wv': _L0_tok_in['wv'], 'L0_tok_wo': _L0_tok_in['wo'], 'L0_tok_wup': _L0_tok_in['wup'], 'L0_tok_bup': _L0_tok_in['bup'], 'L0_tok_wdown': _L0_tok_in['wdown'], 'L0_tok_bdown': _L0_tok_in['bdown'], 'L0_tok_ga': _L0_tok_in['ga'], 'L0_tok_ba': _L0_tok_in['ba'], 'L0_tok_gm': _L0_tok_in['gm'], 'L0_tok_bm': _L0_tok_in['bm'], 'L0_attn_W_key': _L0_attn_in['W_key'], 'L0_attn_W_query': _L0_attn_in['W_query'], 'L0_attn_W_value': _L0_attn_in['W_value'], 'L0_attn_W_proj': _L0_attn_in['W_proj'], 'L0_ffn_router_w': _L0_ffn_in['router_w'], 'L0_ffn_router_b': _L0_ffn_in['router_b'], 'L0_ffn_expert_w': _L0_ffn_in['expert_w'], 'L0_ffn_expert_b': _L0_ffn_in['expert_b'], 'L1_attn_Wq': _L1_attn_in['Wq'], 'L1_attn_Wk': _L1_attn_in['Wk'], 'L1_attn_Wv': _L1_attn_in['Wv'], 'L1_attn_Wu': _L1_attn_in['Wu'], 'L1_attn_Wo': _L1_attn_in['Wo'], 'L1_ffn_gate_w': _L1_ffn_in['gate_w'], 'L1_ffn_w1': _L1_ffn_in['w1'], 'L1_ffn_w2': _L1_ffn_in['w2']}

def reference(x, L0_tok_emb, L0_tok_pos, L0_tok_wq, L0_tok_wk, L0_tok_wv, L0_tok_wo, L0_tok_wup, L0_tok_bup, L0_tok_wdown, L0_tok_bdown, L0_tok_ga, L0_tok_ba, L0_tok_gm, L0_tok_bm, L0_attn_W_key, L0_attn_W_query, L0_attn_W_value, L0_attn_W_proj, L0_ffn_router_w, L0_ffn_router_b, L0_ffn_expert_w, L0_ffn_expert_b, L1_attn_Wq, L1_attn_Wk, L1_attn_Wv, L1_attn_Wu, L1_attn_Wo, L1_ffn_gate_w, L1_ffn_w1, L1_ffn_w2):
    import jax
    import jax.numpy as jnp

    def _L0_tok_ref(x, emb, pos, wq, wk, wv, wo, wup, bup, wdown, bdown, ga, ba, gm, bm):
        import jax, jax.numpy as jnp
        import numpy as np
        V, D, CTX, NL = (8000, 256, 512, 2)
        B, T = (4, 512)
        EPS = 1e-05

        def _layer_norm(x, gamma, beta):
            mu = jnp.mean(x, axis=-1, keepdims=True)
            var = jnp.var(x, axis=-1, keepdims=True)
            return gamma * (x - mu) / jnp.sqrt(var + EPS) + beta
        Bx, Tx = x.shape
        d_model = emb.shape[-1]
        inv_sqrt_d = 1.0 / jnp.sqrt(jnp.asarray(d_model, jnp.float32))
        h = emb[x] + pos[:Tx][None, :, :]
        causal = jnp.tril(jnp.ones((Tx, Tx), bool))
        neg_inf = jnp.asarray(-jnp.inf, h.dtype)
        n_layers = wq.shape[0]
        for l in range(n_layers):
            residual = h
            q = h @ wq[l]
            k = h @ wk[l]
            v = h @ wv[l]
            wei = jnp.einsum('btd,bsd->bts', q, k) * inv_sqrt_d
            wei = jnp.where(causal[None], wei, neg_inf)
            attn = jax.nn.softmax(wei, axis=-1)
            out = jnp.einsum('bts,bsd->btd', attn, v)
            z = out @ wo[l]
            h = _layer_norm(residual + z, ga[l], ba[l])
            m = jax.nn.relu(h @ wup[l] + bup[l]) @ wdown[l] + bdown[l]
            h = _layer_norm(h + m, gm[l], bm[l])
        return h

    def _L0_attn_ref(x, W_key, W_query, W_value, W_proj):
        import jax, jax.numpy as jnp
        import numpy as np
        B, T, C = (4, 512, 256)
        NUM_HEADS = 16
        OUT_DIM = 256
        HEAD_DIM = OUT_DIM // NUM_HEADS
        b, t, c = x.shape
        h, hd = (NUM_HEADS, HEAD_DIM)
        inv_sqrt_c = c ** (-0.5)

        def proj(W):
            return jnp.einsum('btc,oc->bto', x, W).reshape(b, t, h, hd).transpose(0, 2, 1, 3) * inv_sqrt_c
        k = proj(W_key)
        q = proj(W_query)
        v = proj(W_value)
        scores = jnp.einsum('bhqd,bhkd->bhqk', q, k) * hd ** (-0.5)
        causal = jnp.tril(jnp.ones((t, t), dtype=bool))
        scores = jnp.where(causal, scores, -jnp.inf)
        weight = jax.nn.softmax(scores, axis=-1)
        out = jnp.einsum('bhqk,bhkd->bhqd', weight, v)
        out = out.transpose(0, 2, 1, 3).reshape(b, t, h * hd)
        out = jnp.einsum('bto,po->btp', out, W_proj) * W_proj.shape[-1] ** (-0.5)
        return out

    def _L0_ffn_ref(x, router_w, router_b, expert_w, expert_b):
        import jax, jax.numpy as jnp
        import numpy as np
        B, S, D, E = (2, 512, 256, 8)
        logits = jnp.einsum('bsd,ed->bse', x, router_w) + router_b
        probs = jax.nn.softmax(logits, axis=-1)
        weights = jnp.max(probs, axis=-1)
        top1 = jnp.argmax(probs, axis=-1)
        y_all = jnp.einsum('bsd,eod->bseo', x, expert_w) + expert_b
        y = jnp.take_along_axis(y_all, top1[:, :, None, None], axis=2)[:, :, 0, :]
        out = y * weights[:, :, None]
        return out

    def _L1_attn_ref(x, Wq, Wk, Wv, Wu, Wo):
        import math
        import jax, jax.numpy as jnp
        import numpy as np
        EMB = 256
        HEADS = 16
        HEAD_DIM = EMB // HEADS

        def _srms_norm(x, eps=1e-12):
            dtype = x.dtype
            xf = x.astype(jnp.float32)
            scale = 1.0 / math.sqrt(x.shape[-1])
            n = jnp.linalg.norm(xf * scale, axis=-1, keepdims=True)
            return (xf / jnp.maximum(n, eps)).astype(dtype)
        b, l, d = x.shape
        h, hd = (HEADS, HEAD_DIM)
        scale = math.sqrt(hd)

        def proj(W):
            return jnp.einsum('bld,ed->ble', x, W).reshape(b, l, h, hd).transpose(0, 2, 1, 3)
        q = jax.nn.relu(proj(Wq)) / scale
        k = jax.nn.relu(proj(Wk)) / scale
        v = proj(Wv)
        u = jax.nn.silu(proj(Wu))
        kv = jnp.einsum('bhlk,bhlv->bhkv', k, v)
        out = jnp.einsum('bhlk,bhkv->bhlv', q, kv)
        out = _srms_norm(out) * u
        out = out.transpose(0, 2, 1, 3).reshape(b, l, d)
        return jnp.einsum('bld,ed->ble', out, Wo)

    def _L1_ffn_ref(x, gate_w, w1, w2):
        import jax, jax.numpy as jnp
        import numpy as np
        D_MODEL = 256
        D_FF = 512
        NUM_EXPERTS = 16
        TOP_K = 2
        CAPACITY_FACTOR = 1.25
        BATCH, SEQ = (4, 512)
        B, S, d = x.shape
        T = B * S
        E, K = (NUM_EXPERTS, TOP_K)
        capacity = int(CAPACITY_FACTOR * T * K / E)
        xf = x.reshape(T, d)
        logits = xf @ gate_w.T
        probs = jax.nn.sigmoid(logits)
        top_vals, sel = jax.lax.top_k(probs, K)
        weights = top_vals / (top_vals.sum(-1, keepdims=True) + 1e-06)
        flat_sel = sel.reshape(-1)
        onehot = jax.nn.one_hot(flat_sel, E, dtype=jnp.int32)
        ranks = jnp.take_along_axis(jnp.cumsum(onehot, axis=0), flat_sel[:, None], axis=1)[:, 0] - 1
        valid = ranks < capacity
        sentinel = E * capacity
        slot = jnp.where(valid, flat_sel * capacity + ranks, sentinel)
        x_rep = jnp.repeat(xf, K, axis=0)
        padded = jnp.zeros((sentinel + 1, d), xf.dtype).at[slot].set(x_rep)
        padded = padded[:sentinel].reshape(E, capacity, d)
        h = jax.nn.gelu(jnp.einsum('ecd,edf->ecf', padded, w1), approximate=False)
        out_padded = jnp.einsum('ecf,efd->ecd', h, w2).reshape(sentinel, d)
        gathered = out_padded[jnp.minimum(slot, sentinel - 1)]
        gathered = jnp.where(valid[:, None], gathered, jnp.zeros((), xf.dtype))
        out = (gathered * weights.reshape(-1)[:, None]).reshape(T, K, d).sum(axis=1)
        return out.reshape(B, S, d)
    h = _L0_tok_ref(x, L0_tok_emb, L0_tok_pos, L0_tok_wq, L0_tok_wk, L0_tok_wv, L0_tok_wo, L0_tok_wup, L0_tok_bup, L0_tok_wdown, L0_tok_bdown, L0_tok_ga, L0_tok_ba, L0_tok_gm, L0_tok_bm)
    h = h + _L0_attn_ref(_layernorm(h, axis=-1), L0_attn_W_key, L0_attn_W_query, L0_attn_W_value, L0_attn_W_proj)
    h = h + _L0_ffn_ref(_layernorm(h, axis=-1), L0_ffn_router_w, L0_ffn_router_b, L0_ffn_expert_w, L0_ffn_expert_b)
    h = h + _L1_attn_ref(_layernorm(h, axis=-1), L1_attn_Wq, L1_attn_Wk, L1_attn_Wv, L1_attn_Wu, L1_attn_Wo)
    h = h + _L1_ffn_ref(_layernorm(h, axis=-1), L1_ffn_gate_w, L1_ffn_w1, L1_ffn_w2)
    return h

_drawn_inputs = setup_inputs


def setup_inputs(seed=0):
    import zlib

    import numpy as np

    out = dict(_drawn_inputs(seed))
    spreads = {'L0_tok_bup': (0.0, 0.1),
     'L0_tok_bdown': (0.0, 0.1),
     'L0_tok_ga': (1.0, 0.2),
     'L0_tok_ba': (0.0, 0.1),
     'L0_tok_gm': (1.0, 0.2),
     'L0_tok_bm': (0.0, 0.1),
     'L0_ffn_router_b': (0.0, 0.1),
     'L0_ffn_expert_b': (0.0, 0.1)}
    factors = {'L0_tok_wq': 3.809, 'L0_tok_wk': 3.368}
    for name, (base, spread) in spreads.items():
        noise = np.random.default_rng([zlib.crc32(name.encode()), seed]).standard_normal(out[name].shape)
        drawn = base * np.exp(spread * noise) if base else spread * noise
        out[name] = jnp.asarray(drawn.astype(out[name].dtype))
    for name, factor in factors.items():
        out[name] = (out[name] * factor).astype(out[name].dtype)
    return out
```

```python
from contextlib import ExitStack

import concourse.bass as bass
from concourse import mybir

F32 = mybir.dt.float32
BF16 = mybir.dt.bfloat16
I32 = mybir.dt.int32
U32 = mybir.dt.uint32
ALU = mybir.AluOpType
ACT = mybir.ActivationFunctionType
AX = mybir.AxisListType

P = 128
B, T, D = 4, 512, 256
TT = T // P
NT = B * TT
KD = D // P
VOCAB = 8000
LAYERS = 2
FF = 4 * D
KF = FF // P
HEADS, HD = 16, 16
E8 = 8
E16, TOPK, DFF = 16, 2, 512
KE = DFF // P
CAP = int(1.25 * B * T * TOPK / E16)
SLOTS = E16 * CAP
CAP_TILES = [(0, 128), (128, 128), (256, CAP - 256)]
EPS = 1e-5
FAR = 1e30

STAGES = ["attn", "mlp", "attn", "mlp", "heads", "top1", "linear", "route"]
STEPS = len(STAGES) * B
ITEMS = {"attn": TT, "heads": HEADS * TT}


def stage_of(u):
    return STAGES[u // B]


def layer_of(u):
    return u // (2 * B)


def prep_keys(u):
    if u >= STEPS:
        return []
    s = stage_of(u)
    keys = ["T0", "T1"]
    if s in ("attn", "heads"):
        keys += ["q0", "q1", "k0", "k1", "v0", "v1"]
    if s == "linear":
        keys += ["q0", "q1"] + [f"kv{t}" for t in range(TT)] + ["g0", "g1"]
    return [(u, k) for k in keys]


def step_keys(u):
    s = stage_of(u)
    own = lambda *names: [(u, n) for n in names]
    nxt = prep_keys(u + 1)
    if s in ("attn", "heads"):
        return nxt + own("z0", "z1")
    if s == "mlp":
        return own(*[f"up{m}" for m in range(KF)]) + nxt + own("z0", "z1")
    if s == "top1":
        return own("gate") + nxt + own("mT", "b0", "b1") + own(*[f"y{t}{e}" for t in range(TT) for e in range(E8 // 2)])
    if s == "linear":
        return own("kvm", "o0", "o1") + nxt + own("T2", "T3", "z0", "z1")
    return own("gate") + nxt + own("rank")


RING = {key: g for g, key in enumerate(prep_keys(0) + [k for u in range(STEPS) for k in step_keys(u)])}


def first_item(u):
    return sum(ITEMS.get(stage_of(x), 0) for x in range(u))


def groups_of(u):
    if stage_of(u) == "attn":
        return [(0, 0, qt, [0]) for qt in range(TT)]
    return [(g, e, qt, [0, 1, 2, 3]) for g in range(KD) for qt in range(TT) for e in range(2)]


def items_of(u):
    return [(i, g, e, qt, j) for i, (g, e, qt, js) in enumerate(groups_of(u)) for j in js]


def first_group(u):
    return sum(len(groups_of(x)) for x in range(u) if stage_of(x) in ITEMS)


def norms_of(u):
    return 0 if u < B else 2 if stage_of(u) == "heads" else 1


def first_norm(u):
    return sum(norms_of(x) for x in range(u))


def last_key(u):
    return (u, f"y{TT - 1}{E8 // 2 - 1}") if stage_of(u) == "top1" else (u, "z1")


def tower_kernel(nc, a):
    ctx = ExitStack()
    with ctx:
        def sb(name, shape, dt=F32):
            return ctx.enter_context(nc.sbuf_tensor(name, shape, dt))

        def sem(name):
            return ctx.enter_context(nc.semaphore(name))

        attn_w = sb("attn_w", [P, LAYERS, 4, KD, D])
        up_w = sb("up_w", [P, LAYERS, KD, FF])
        down_w = sb("down_w", [P, LAYERS, KF, D])
        rows = sb("rows", [P, LAYERS, 5, D])
        up_b = sb("up_b", [P, LAYERS, KF])
        heads_w = sb("heads_w", [P, 4, KD, D])
        lin_q = sb("lin_q", [P, KD, D])
        lin_kvu = sb("lin_kvu", [P, KD, 3 * D])
        lin_o = sb("lin_o", [P, KD, D])
        gate8 = sb("gate8", [P, KD, E8])
        gate8_b = sb("gate8_b", [P, E8])
        expert_b = sb("expert_b", [E8, D])
        gate16 = sb("gate16", [P, KD, E16])
        top1_w = up_w[:, :, :, :].rearrange("p l k f -> p (l k f)").rearrange("p (k n) -> p k n", k=KD)
        moe_w = down_w[:, :, :, :].rearrange("p l k d -> p (l k d)")
        W1 = [moe_w[:, x * 1024:(x + 1) * 1024].rearrange("p (k f) -> p k f", k=KD) for x in range(2)]
        W2 = [moe_w[:, 2048 + x * 1024:2048 + (x + 1) * 1024].rearrange("p (m d) -> p m d", m=KE) for x in range(2)]
        h = sb("h", [P, NT, D])
        xn = sb("xn", [P, 2, TT, D])
        xT = sb("xT", [P, 2, KD, T])
        qk = sb("qk", [P, 2, 2, KD, T])
        kodd = sb("kodd", [P, 2, KD, T])
        v = sb("v", [P, 2, TT, D])
        vodd = sb("vodd", [P, 2, TT, D])
        oT = sb("oT", [P, 2, KD, T])
        hid = sb("hid", [P, KF, T])
        prob = sb("prob", [P, 4, T])
        probT = sb("probT", [P, 2, 4, T])
        pos = kodd[:, :, :, :].rearrange("p a k t -> p (a k t)")[:, 0:TT * D].rearrange("p (t d) -> p t d", t=TT)
        zeros = vodd[:, :, :, :].rearrange("p a t d -> p (a t d)")
        gate_u = kodd[:, :, :, :].rearrange("p a k t -> p a (k t)").rearrange("p a (t d) -> p a t d", t=TT)
        lin_k = qk[:, 1, :, :, :].rearrange("p a k t -> p a (k t)").rearrange("p a (t d) -> p a t d", t=TT)
        lin_y = vodd
        lin_t = hid[:, :, :].rearrange("p m t -> p (m t)").rearrange("p (x t d) -> p x t d", x=4, t=TT)
        xf = qk[:, :, :, :, :].rearrange("p a b k t -> p (a b k t)").rearrange("p (n d) -> p n d", n=NT)
        got = [xf, attn_w[:, :, :, :, :].rearrange("p a b k t -> p (a b k t)").rearrange("p (n d) -> p n d", n=NT)]
        flatT = probT[:, :, :, :].rearrange("p a b t -> p (a b t)")
        xe = [flatT[:, x * 768:(x + 1) * 768].rearrange("p (t d) -> p t d", t=3) for x in range(2)]
        ye = [flatT[:, 1536 + x * 768:1536 + (x + 1) * 768].rearrange("p (t d) -> p t d", t=3) for x in range(2)]
        xeT = [xT[:, :, :, :].rearrange("p a k t -> p (a k t)")[:, x * 640:(x + 1) * 640]
               .rearrange("p (k t) -> p k t", k=KD) for x in range(2)]
        heT = [hid[:, 4 * x:4 * x + 4, 0:CAP] for x in range(2)]
        kvm = sb("kvm", [P, 2, KD, P])
        ident = sb("ident", [P, P])
        ones_f = sb("ones_f", [P, P])
        blockdiag = sb("blockdiag", [P, P])
        causal = sb("causal", [P, T])
        evenrow = sb("evenrow", [P, 2])
        before = sb("before", [P, P], BF16)
        ones_b = sb("ones_b", [P, P], BF16)
        tmp_b = prob[:, 0, 0:P]
        eps_c = sb("eps_c", [P, 1])
        iota16 = sb("iota16", [P, E16])
        iota_i = sb("iota_i", [P, E16], I32)
        first16 = sb("first16", [P, E16])
        base16 = sb("base16", [P, E16])
        ids = sb("ids", [P, NT], I32)
        idf = sb("idf", [P, 2, NT])
        idu = sb("idu", [P, NT], U32)
        stats = sb("stats", [P, 2, TT, 6])
        mv = sb("mv", [P, 2, TT, 2])
        sd = sb("sd", [P, 2, TT])
        rstd = sb("rstd", [P, 2, TT])
        negmax = sb("negmax", [P, 8])
        rsum = sb("rsum", [P, 8])
        rinv = sb("rinv", [P, 8])
        lg = sb("lg", [P, 2, TT, E16])
        ga_ = sb("ga_", [P, 6, TT, E16])
        small = sb("small", [P, 12, TT])
        mw = sb("mw", [P, TT, E8])
        mwT = hid[0:E8, 7, :]
        cnt = sb("cnt", [P, NT, E16], BF16)
        wk = sb("wk", [P, TOPK, NT])
        slot_s = sb("slot_s", [P, TOPK, NT], U32)
        slot_g = sb("slot_g", [P, TOPK, NT], U32)
        srms = hid[:, 6, 0:3 * TT * HEADS].rearrange("p (x t h) -> p x t h", x=3, t=TT)

        ring = [ctx.enter_context(nc.psum_tensor(f"ring{i}", [P, T], F32)) for i in range(2)]
        s_bank = [ctx.enter_context(nc.psum_tensor(f"s_bank{i}", [P, T], F32)) for i in range(3)]
        pt_bank = [ctx.enter_context(nc.psum_tensor(f"pt_bank{i}", [P, T], F32)) for i in range(2)]
        o_bank = ctx.enter_context(nc.psum_tensor("o_bank", [P, T], F32))

        up_bank = [s_bank[0], s_bank[1], s_bank[2], o_bank]

        slots_x = nc.dram_tensor("slots_x", (SLOTS, D), F32, kind="Internal").ap()
        slots_y = nc.dram_tensor("slots_y", (SLOTS, D), F32, kind="Internal").ap()

        ids_in, pos_in, id_ready, const_p, const_v = sem("ids_in"), sem("pos_in"), sem("id_ready"), sem("const_p"), sem("const_v")
        emb_in = [sem(f"emb_in{b}") for b in range(B)]
        w_in = {n: sem(f"w_{n}") for n in ("attn0", "attn1", "up0", "up1", "down0", "down1", "rows", "upb",
                                           "heads", "lin", "gates", "top1")}
        zeroed = sem("zeroed")
        stats_ready, sd_ready, dve_step, norm_mid = sem("stats_ready"), sem("sd_ready"), sem("dve_step"), sem("norm_mid")
        xn_dve, xn_pool = sem("xn_dve"), sem("xn_pool")
        xn_turned = sem("xn_turned")
        pool_step = sem("pool_step")
        ring_full = sem("ring_full")
        ring_drained = [sem("ring_drained0"), sem("ring_drained1")]
        xT_read = sem("xT_read")
        qk_read = sem("qk_read")
        s_full, masked, exped, inverted, normed = sem("s_full"), sem("masked"), sem("exped"), sem("inverted"), sem("normed")
        pt_full = sem("pt_full")
        pt_drained = [sem("pt_drained0"), sem("pt_drained1")]
        av_done, o_full, o_drained, z_done = sem("av_done"), sem("o_full"), sem("o_drained"), sem("z_done")
        resid = sem("resid")
        odd_cleared = sem("odd_cleared")
        gates, gexp, gmask = sem("gates"), sem("gexp"), sem("gmask")
        lin_step, lin_sd, lin_out, lin_act = sem("lin_step"), sem("lin_sd"), sem("lin_out"), sem("lin_act")
        counts = sem("counts")
        slots_set, kept = sem("slots_set"), sem("kept")
        scattered = sem("scattered")
        w1_in, w2_in, xe_in, ye_out = ([sem(f"w1_in{i}") for i in range(2)], [sem(f"w2_in{i}") for i in range(2)],
                                       [sem(f"xe_in{i}") for i in range(2)], [sem(f"ye_out{i}") for i in range(2)])
        e_turned, e_xT, e_up, e_gelu, e_down, e_y = (sem("e_turned"), sem("e_xT"), sem("e_up"), sem("e_gelu"),
                                                     sem("e_down"), sem("e_y"))
        got_in = [sem(f"got_in{b}") for b in range(B)]
        mixed, mixed0, out_sent = sem("mixed"), sem("mixed0"), sem("out_sent")

        block = ctx.enter_context(nc.Block())

        def ring_free(eng, key):
            g = RING[key]
            if g >= 2:
                eng.wait_ge(ring_drained[g % 2], g // 2)
            return ring[g % 2]

        def ring_ready(eng, key):
            eng.wait_ge(ring_full, RING[key] + 1)
            return ring[RING[key] % 2]

        def ring_empty(key):
            return ring_drained[RING[key] % 2]

        def drained(eng, key):
            g = RING[key]
            eng.wait_ge(ring_drained[g % 2], g // 2 + 1)

        def grid(t):
            return t.rearrange("(n p) d -> p n d", p=P)

        @block.sync
        def _(sync):
            sync.dma_start(ids[:, :], a["x_cols"]).then_inc(ids_in, 16)
            sync.dma_start(pos, grid(a["L0_tok_pos"])).then_inc(pos_in, 16)
            for l in range(LAYERS):
                for i, n in enumerate(("wq", "wk", "wv", "wo")):
                    sync.dma_start(attn_w[:, l, i, :, :], a[f"L0_tok_{n}"][l].rearrange("(k p) n -> p k n", p=P))\
                        .then_inc(w_in[f"attn{l}"], 16)
                if l == 0:
                    for m in range(LAYERS):
                        for i, n in enumerate(("bdown", "ga", "ba", "gm", "bm")):
                            sync.dma_start(rows[:, m, i, :], a[f"L0_tok_{n}"][m:m + 1, :].to_broadcast([P, D]))\
                                .then_inc(w_in["rows"], 16)
                    sync.dma_start(up_b[:, :, :], a["bup_cols"]).then_inc(w_in["upb"], 16)
                sync.dma_start(up_w[:, l, :, :], a["L0_tok_wup"][l].rearrange("(k p) n -> p k n", p=P))\
                    .then_inc(w_in[f"up{l}"], 16)
                sync.dma_start(down_w[:, l, :, :], a["L0_tok_wdown"][l].rearrange("(k p) n -> p k n", p=P))\
                    .then_inc(w_in[f"down{l}"], 16)
            for i, n in enumerate(("query", "key", "value", "proj")):
                sync.dma_start(heads_w[:, i, :, :], a[f"heads_{n}"].rearrange("(k p) n -> p k n", p=P))\
                    .then_inc(w_in["heads"], 16)
            sync.dma_start(gate8[:, :, :], a["router_t"].rearrange("(k p) n -> p k n", p=P)).then_inc(w_in["gates"], 16)
            sync.dma_start(gate16[:, :, :], a["gate_t"].rearrange("(k p) n -> p k n", p=P)).then_inc(w_in["gates"], 16)
            sync.dma_start(gate8_b[:, :], a["router_b"].to_broadcast([P, E8])).then_inc(w_in["gates"], 16)
            sync.dma_start(expert_b[:, :], a["L0_ffn_expert_b"]).then_inc(w_in["gates"], 16)
            sync.dma_start(lin_q[:, :, :], a["lin_q_t"].rearrange("(k p) n -> p k n", p=P)).then_inc(w_in["lin"], 16)
            sync.dma_start(lin_kvu[:, :, :], a["lin_kvu_t"].rearrange("(k p) n -> p k n", p=P)).then_inc(w_in["lin"], 16)
            sync.dma_start(lin_o[:, :, :], a["lin_o_t"].rearrange("(k p) n -> p k n", p=P)).then_inc(w_in["lin"], 16)
            sync.wait_ge(const_p, 1)
            for i in range(5):
                sync.dma_start(slots_x[i * 1024:(i + 1) * 1024, :].rearrange("(p r) d -> p (r d)", p=P), zeros)\
                    .then_inc(zeroed, 16)
            sync.wait_ge(ring_full, RING[(4 * B - 1, "up7")] + 1)
            sync.dma_start(top1_w, a["top1_t"].rearrange("(k p) n -> p k n", p=P)).then_inc(w_in["top1"], 16)
            sync.wait_ge(ring_full, RING[(4 * B - 1, "z1")] + 1)

            def weights1(e, x):
                sync.dma_start(W1[x], a["w1_rows"][bass.ds(e * D, D), :].rearrange("(k p) f -> p k f", p=P)).then_inc(w1_in[x], 16)

            def weights2(e, x):
                sync.dma_start(W2[x], a["w2_rows"][bass.ds(e * DFF, DFF), :].rearrange("(m p) d -> p m d", p=P)).then_inc(w2_in[x], 16)

            def tokens(e, x):
                src = slots_x[bass.ds(e * CAP, CAP), :]
                sync.dma_start(xe[x][:, 0:2, :], src[0:256, :].rearrange("(t p) d -> p t d", p=P)).then_inc(xe_in[x], 16)
                sync.dma_start(xe[x][0:CAP - 256, 2, :], src[256:CAP, :]).then_inc(xe_in[x], 16)

            def results(e, x):
                dst = slots_y[bass.ds(e * CAP, CAP), :]
                sync.wait_ge(e_y, 2 * e + 2)
                sync.dma_start(dst[0:256, :].rearrange("(t p) d -> p t d", p=P), ye[x][:, 0:2, :]).then_inc(ye_out[x], 16)
                sync.dma_start(dst[256:CAP, :], ye[x][0:CAP - 256, 2, :]).then_inc(ye_out[x], 16)

            for e in range(2):
                weights1(e, e)
                weights2(e, e)
            sync.wait_ge(scattered, 16 * TOPK * NT)
            for e in range(2):
                tokens(e, e)
            with sync.Fori(0, E16 // 2 - 1) as j:
                for x in range(2):
                    e = 2 * j + x
                    sync.wait_ge(e_up, KE * e + KE)
                    weights1(e + 2, x)
                    tokens(e + 2, x)
                    results(e, x)
                    weights2(e + 2, x)
            for x in range(2):
                results(E16 - 2 + x, x)
            out_v = a["out"].rearrange("b (t p) d -> b p t d", p=P)
            for b in range(B):
                sync.wait_ge(mixed, TT * (b + 1))
                sync.dma_start(out_v[b], h[:, b * TT:(b + 1) * TT, :]).then_inc(out_sent, 16)
            sync.wait_ge(out_sent, 16 * B)

        @block.gpsimd
        def _(pool):
            done = {}

            def step(ins):
                ins.then_inc(pool_step, 1)
                done["n"] = done.get("n", 0) + 1

            def settle():
                pool.wait_ge(pool_step, done["n"])

            pool.memset(zeros, 0.0).then_inc(const_p, 1)
            step(pool.memset(ident[:, :], 0.0))
            step(pool.memset(ones_f[:, :], 1.0))
            step(pool.memset(causal[:, :], 0.0))
            step(pool.memset(ones_b[:, :], 1.0))
            step(pool.iota(iota_i[:, :], pattern=[[1, E16]], base=0, channel_multiplier=0))
            settle()
            step(pool.affine_select(out=ident[:, :], in_=ident[:, :], compare_op=ALU.not_equal, fill=1.0, base=0,
                                    pattern=[[-1, P]], channel_multiplier=1))
            step(pool.affine_select(out=causal[:, T - P:T], in_=causal[:, T - P:T], compare_op=ALU.is_ge, fill=FAR, base=0,
                                    pattern=[[-1, P]], channel_multiplier=1))
            step(pool.affine_select(out=tmp_b, in_=ones_f[:, :], compare_op=ALU.is_gt, fill=0.0, base=0,
                                    pattern=[[1, P]], channel_multiplier=-1))
            step(pool.affine_select(out=blockdiag[:, :], in_=ones_f[:, :], compare_op=ALU.is_ge, fill=0.0, base=0,
                                    pattern=[[-HD, P // HD], [0, HD]], channel_multiplier=1))
            step(pool.tensor_copy(iota16[:, :], iota_i[:, :]))
            settle()
            step(pool.affine_select(out=blockdiag[:, :], in_=blockdiag[:, :], compare_op=ALU.is_ge, fill=0.0, base=HD - 1,
                                    pattern=[[HD, P // HD], [0, HD]], channel_multiplier=-1))
            settle()
            pool.tensor_copy(before[:, :], tmp_b).then_inc(const_p, 1)

            pool.wait_ge(id_ready, 4)
            for t in range(NT):
                pool.indirect_dma_start(out=h[:, t, :], out_offset=None, in_=a["L0_tok_emb"],
                                        in_offset=bass.IndirectOffsetOnAxis(ap=idu[:, t:t + 1], axis=0))\
                    .then_inc(emb_in[t // TT], 16)

            def affine(u):
                p = u % 2
                l, r = ((u // B - 1) // 2, 1 if u // B % 2 == 1 else 3)
                if u == B:
                    pool.wait_ge(w_in["rows"], 160)
                pool.wait_ge(norm_mid, u - B + 1)
                row = lambda i: rows[:, l, i:i + 1, :].to_broadcast([P, TT, D])
                step(pool.tensor_tensor(out=xn[:, p, :, :], in0=xn[:, p, :, :], in1=row(r), op=ALU.mult))
                settle()
                pool.tensor_tensor(out=xn[:, p, :, :], in0=xn[:, p, :, :], in1=row(r + 1), op=ALU.add).then_inc(xn_pool, 1)

            for u in range(STEPS):
                n0, items = first_item(u), items_of(u) if stage_of(u) in ITEMS else []
                for i, item in enumerate(items):
                    n, w = n0 + i, (item[3] + 1) * P
                    pool.wait_ge(inverted, n + 1)
                    pool.tensor_scalar(prob[:, n % 4, 0:w], prob[:, n % 4, 0:w], rinv[:, n % 8:n % 8 + 1], None, ALU.mult)\
                        .then_inc(normed, 1)
                if u == 3 * B:
                    pool.wait_ge(av_done, first_group(4 * B))
                    pool.memset(v[:, :, :, :], 0.0).then_inc(odd_cleared, 1)
                if B <= u + 2 < 4 * B:
                    affine(u + 2)
                if stage_of(u) == "route":
                    b, p = u % B, u % 2
                    pool.wait_ge(xn_dve, u - 3 * B + 1)
                    pool.wait_ge(ring_full, RING[(7 * B - 1, "o1")] + 1)
                    pool.tensor_copy(xf[:, b * TT:(b + 1) * TT, :], xn[:, p, :, :]).then_inc(kept, 1)
                    pool.wait_ge(kept, b + 1)
                    pool.wait_ge(slots_set, 2 * TOPK * (b + 1))
                    if b == 0:
                        pool.wait_ge(zeroed, 80)
                    for t in range(b * TT, (b + 1) * TT):
                        for k in range(TOPK):
                            pool.indirect_dma_start(out=slots_x,
                                                    out_offset=bass.IndirectOffsetOnAxis(ap=slot_s[:, k, t:t + 1], axis=0),
                                                    in_=xf[:, t, :], in_offset=None,
                                                    bounds_check=SLOTS - 1, oob_is_err=False).then_inc(scattered, 16)
            for x in range(2):
                pool.wait_ge(ye_out[x], 16 * E16)
            pool.wait_ge(scattered, 16 * TOPK * NT)
            for b in range(B):
                for t in range(b * TT, (b + 1) * TT):
                    for k in range(TOPK):
                        pool.indirect_dma_start(out=got[k][:, t, :], out_offset=None, in_=slots_y,
                                                in_offset=bass.IndirectOffsetOnAxis(ap=slot_g[:, k, t:t + 1], axis=0))\
                            .then_inc(got_in[b], 16)

        @block.tensor
        def _(pe):
            def mm(out, lhsT, rhs, start, stop, **kw):
                return pe.matmul(out, lhsT, rhs, start=start, stop=stop, **kw)

            def chain(out, pairs):
                for i, (l, r) in enumerate(pairs):
                    ins = mm(out, l, r, i == 0, i == len(pairs) - 1)
                return ins

            def project(u, key):
                p, s, l = u % 2, stage_of(u), layer_of(u)
                k = key[1]
                bank = ring_free(pe, key)
                if k[0] == "T":
                    c = int(k[1])
                    if c == 0:
                        if B <= u < 4 * B:
                            pe.wait_ge(xn_pool, u - B + 1)
                        else:
                            pe.wait_ge(xn_dve, u + 1 if u < B else u - 3 * B + 1)
                    for t in range(TT):
                        ins = pe.transpose(bank[:, t * P:(t + 1) * P], xn[:, p, t, c * P:(c + 1) * P], ident[:, :])
                    ins.then_inc(ring_full, 1)
                    return
                if k == "q0":
                    drained(pe, (u, "T0"))
                    drained(pe, (u, "T1"))
                    if s == "attn" and u % B == 0:
                        pe.wait_ge(w_in[f"attn{l}"], 64)
                    if s == "heads" and u % B == 0:
                        pe.wait_ge(w_in["heads"], 64)
                    if s == "linear" and u % B == 0:
                        pe.wait_ge(w_in["lin"], 48)
                if k[0] in "qk" and k[1] != "v":
                    c = int(k[1])
                    i = "qk".index(k[0])
                    w = attn_w[:, l, i] if s == "attn" else heads_w[:, i] if s == "heads" else lin_q
                    chain(bank[:, :], [(w[:, kk, c * P:(c + 1) * P], xT[:, p, kk, :]) for kk in range(KD)])\
                        .then_inc(ring_full, 1)
                elif k[0] == "v":
                    w = attn_w[:, l, 2] if s == "attn" else heads_w[:, 2]
                    for t in range(2):
                        tt = 2 * int(k[1]) + t
                        ins = chain(bank[:, t * D:(t + 1) * D],
                                    [(xT[:, p, kk, tt * P:(tt + 1) * P], w[:, kk, :]) for kk in range(KD)])
                    ins.then_inc(ring_full, 1)
                elif k[:2] == "kv":
                    t = int(k[2])
                    chain(bank[:, :], [(xT[:, p, kk, t * P:(t + 1) * P], lin_kvu[:, kk, 0:2 * D]) for kk in range(KD)])\
                        .then_inc(ring_full, 1)
                else:
                    for t in range(2):
                        tt = 2 * int(k[1]) + t
                        ins = chain(bank[:, t * D:(t + 1) * D],
                                    [(xT[:, p, kk, tt * P:(tt + 1) * P], lin_kvu[:, kk, 2 * D:3 * D]) for kk in range(KD)])
                    ins.then_inc(ring_full, 1)

            def prep(u):
                for key in prep_keys(u):
                    project(u, key)

            def scores(u, n, item):
                _, g, e, qt, j = item
                p, w = u % 2, (qt + 1) * P
                if n >= 3:
                    pe.wait_ge(masked, n - 2)
                bank = s_bank[n % 3]
                if stage_of(u) == "attn":
                    ins = chain(bank[:, 0:w], [(qk[:, 0, p, kk, qt * P:w], qk[:, 1, p, kk, 0:w]) for kk in range(KD)])
                else:
                    r = slice(32 * j, 32 * j + 32)
                    keys = kodd if e else qk[:, 1]
                    ins = mm(bank[:, 0:w], qk[r, 0, p, g, qt * P:w], keys[r, p, g, 0:w], True, True,
                             tile_position=(32 * j, 0))
                ins.then_inc(s_full, 1)

            def turn(n, item):
                qt = item[3]
                pe.wait_ge(normed, n + 1)
                if n >= 2:
                    pe.wait_ge(pt_drained[n % 2], n // 2)
                for kt in range(qt + 1):
                    ins = pe.transpose(pt_bank[n % 2][:, kt * P:(kt + 1) * P], prob[:, n % 4, kt * P:(kt + 1) * P], ident[:, :])
                ins.then_inc(pt_full, 1)

            def weigh(u, m, last_n, o_use):
                p = u % 2
                g, e, qt, js = groups_of(u)[m - first_group(u)]
                for x in range(2):
                    count = (last_n - x) // 2 + 1 if last_n >= x else 0
                    if count > 0:
                        pe.wait_ge(pt_drained[x], count)
                if stage_of(u) == "attn":
                    if o_use:
                        pe.wait_ge(o_drained, o_use)
                    for c in range(KD):
                        for kt in range(qt + 1):
                            ins = mm(o_bank[:, c * P:(c + 1) * P], v[:, p, kt, c * P:(c + 1) * P],
                                     probT[:, m % 2, 0, kt * P:(kt + 1) * P], kt == 0, kt == qt)
                    ins.then_inc(av_done, 1)
                else:
                    if qt == 0 and e == 0:
                        pe.wait_ge(o_drained, o_use)
                    vals = vodd if e else v
                    for kt in range(qt + 1):
                        for j in range(4):
                            c0 = g * P + 32 * j
                            ins = mm(o_bank[32 * j:32 * j + 32, qt * P:(qt + 1) * P], vals[:, p, kt, c0:c0 + 32],
                                     probT[:, m % 2, j, kt * P:(kt + 1) * P], e == 0 and kt == 0, e == 1 and kt == qt,
                                     tile_position=(0, 32 * j))
                    ins.then_inc(av_done, 1)

            def out_proj(u, w):
                p = u % 2
                for x in range(2):
                    bank = ring_free(pe, (u, f"z{x}"))
                    for t in range(2):
                        tt = 2 * x + t
                        ins = chain(bank[:, t * D:(t + 1) * D], [(oT[:, p, c, tt * P:(tt + 1) * P], w[:, c, :]) for c in range(KD)])
                    ins.then_inc(ring_full, 1)

            o_uses = 0
            pe.wait_ge(const_p, 2)
            prep(0)
            for u in range(STEPS):
                s, p, l = stage_of(u), u % 2, layer_of(u)
                n0, m0 = first_item(u), first_group(u)
                if s == "attn":
                    items = items_of(u)
                    for k in ("q0", "q1", "k0", "k1", "v0", "v1"):
                        drained(pe, (u, k))
                    for i in range(TT):
                        scores(u, n0 + i, items[i])
                    prep(u + 1)
                    for i in range(TT):
                        turn(n0 + i, items[i])
                        if i:
                            weigh(u, m0 + i - 1, n0 + i - 1, o_uses)
                            o_uses += 1
                    weigh(u, m0 + TT - 1, n0 + TT - 1, o_uses)
                    o_uses += 1
                    pe.wait_ge(o_drained, o_uses)
                    out_proj(u, attn_w[:, l, 3])
                elif s == "heads":
                    items = items_of(u)
                    for k in ("q0", "q1", "k0", "k1", "v0", "v1"):
                        drained(pe, (u, k))
                    nxt = prep_keys(u + 1)
                    for i in range(3):
                        scores(u, n0 + i, items[i])
                    for i in range(len(items)):
                        turn(n0 + i, items[i])
                        if i + 3 < len(items):
                            scores(u, n0 + i + 3, items[i + 3])
                        if i % 4 == 3 and i > 3:
                            m = i // 4 - 1
                            weigh(u, m0 + m, n0 + i - 4, o_uses)
                            if m % 8 == 7:
                                o_uses += 1
                        if i % 7 == 5 and nxt:
                            project(u + 1, nxt.pop(0))
                    for key in nxt:
                        project(u + 1, key)
                    weigh(u, m0 + 15, n0 + 63, o_uses)
                    o_uses += 1
                    pe.wait_ge(o_drained, o_uses)
                    out_proj(u, heads_w[:, 3])
                elif s == "mlp":
                    drained(pe, (u, "T0"))
                    drained(pe, (u, "T1"))
                    if u % B == 0:
                        pe.wait_ge(w_in[f"up{l}"], 16)
                    for m in range(KF):
                        bank = ring_free(pe, (u, f"up{m}"))
                        chain(bank[:, :], [(up_w[:, l, kk, m * P:(m + 1) * P], xT[:, p, kk, :]) for kk in range(KD)])\
                            .then_inc(ring_full, 1)
                    prep(u + 1)
                    if u % B == 0:
                        pe.wait_ge(w_in[f"down{l}"], 16)
                    drained(pe, (u, "up6"))
                    drained(pe, (u, "up7"))
                    for x in range(2):
                        bank = ring_free(pe, (u, f"z{x}"))
                        for t in range(2):
                            tt = 2 * x + t
                            ins = chain(bank[:, t * D:(t + 1) * D],
                                        [(hid[:, m, tt * P:(tt + 1) * P], down_w[:, l, m, :]) for m in range(KF)])
                        ins.then_inc(ring_full, 1)
                elif s == "top1":
                    drained(pe, (u, "T0"))
                    drained(pe, (u, "T1"))
                    if u % B == 0:
                        pe.wait_ge(w_in["gates"], 64)
                        pe.wait_ge(w_in["top1"], 16)
                    bank = ring_free(pe, (u, "gate"))
                    for t in range(TT):
                        ins = chain(bank[:, t * E8:(t + 1) * E8],
                                    [(xT[:, p, kk, t * P:(t + 1) * P], gate8[:, kk, :]) for kk in range(KD)])
                    ins.then_inc(ring_full, 1)
                    prep(u + 1)
                    bank = ring_free(pe, (u, "mT"))
                    pe.wait_ge(gmask, u % B + 1)
                    for t in range(TT):
                        ins = pe.transpose(bank[0:E8, t * P:(t + 1) * P], mw[:, t, :], ident[:, :])
                    ins.then_inc(ring_full, 1)
                    drained(pe, (u, "mT"))
                    for x in range(2):
                        bank = ring_free(pe, (u, f"b{x}"))
                        for t in range(2):
                            tt = 2 * x + t
                            ins = mm(bank[:, t * D:(t + 1) * D], mwT[:, tt * P:(tt + 1) * P], expert_b[:, :], True, True)
                        ins.then_inc(ring_full, 1)
                    for t in range(TT):
                        for e in range(E8 // 2):
                            bank = ring_free(pe, (u, f"y{t}{e}"))
                            chain(bank[:, :], [(xT[:, p, kk, t * P:(t + 1) * P], top1_w[:, kk, e * 2 * D:(e + 1) * 2 * D])
                                               for kk in range(KD)]).then_inc(ring_full, 1)
                elif s == "linear":
                    for k in ("q0", "q1", "kv0", "kv1", "kv2", "kv3", "g0", "g1"):
                        drained(pe, (u, k))
                    bank = ring_free(pe, (u, "kvm"))
                    for c in range(KD):
                        ins = chain(bank[:, c * P:(c + 1) * P],
                                    [(lin_k[:, p, t, c * P:(c + 1) * P], v[:, p, t, c * P:(c + 1) * P]) for t in range(TT)])
                    ins.then_inc(ring_full, 1)
                    drained(pe, (u, "kvm"))
                    for x in range(2):
                        bank = ring_free(pe, (u, f"o{x}"))
                        for t in range(2):
                            tt = 2 * x + t
                            for c in range(KD):
                                ins = mm(bank[:, t * D + c * P:t * D + (c + 1) * P], qk[:, 0, p, c, tt * P:(tt + 1) * P],
                                         kvm[:, p, c, :], True, True)
                        ins.then_inc(ring_full, 1)
                    prep(u + 1)
                    for c in range(KD):
                        bank = ring_free(pe, (u, f"T{2 + c}"))
                        pe.wait_ge(lin_out, u % B + 1)
                        for t in range(TT):
                            ins = pe.transpose(bank[:, t * P:(t + 1) * P], lin_y[:, p, t, c * P:(c + 1) * P], ident[:, :])
                        ins.then_inc(ring_full, 1)
                    drained(pe, (u, "T2"))
                    drained(pe, (u, "T3"))
                    out_proj(u, lin_o)
                else:
                    drained(pe, (u, "T0"))
                    drained(pe, (u, "T1"))
                    bank = ring_free(pe, (u, "gate"))
                    for t in range(TT):
                        ins = chain(bank[:, t * E16:(t + 1) * E16],
                                    [(xT[:, p, kk, t * P:(t + 1) * P], gate16[:, kk, :]) for kk in range(KD)])
                    ins.then_inc(ring_full, 1)
                    prep(u + 1)
                    bank = ring_free(pe, (u, "rank"))
                    b = u % B
                    pe.wait_ge(counts, b + 1)
                    for t in range(TT):
                        tt = b * TT + t
                        ins = chain(bank[:, t * E16:(t + 1) * E16],
                                    [(before[:, :], cnt[:, tt, :])] + [(ones_b[:, :], cnt[:, y, :]) for y in range(tt)])
                    ins.then_inc(ring_full, 1)
            for i in range(2):
                pe.wait_ge(ring_drained[i], (len(RING) - i + 1) // 2)

            def first(j, x, begin=False):
                e = 2 * j + x
                pe.wait_ge(xe_in[x], 32 * j + 32)
                for c in range(KD):
                    if not begin:
                        pe.wait_ge(e_xT, 2 * e - 1 + c)
                    for i, (t0, w) in enumerate(CAP_TILES):
                        ins = pe.transpose(pt_bank[c][:, t0:t0 + w], xe[x][0:w, i, c * P:(c + 1) * P], ident[0:w, 0:w])
                    ins.then_inc(e_turned, 1)
                pe.wait_ge(w1_in[x], 16 * j + 16)
                pe.wait_ge(e_xT, 2 * e + 2)
                for m in range(KE):
                    if not begin:
                        pe.wait_ge(e_gelu, KE * e - KE + m + 1)
                    chain(up_bank[m][:, 0:CAP], [(W1[x][:, kk, m * P:(m + 1) * P], xeT[x][:, kk, :]) for kk in range(KD)])\
                        .then_inc(e_up, 1)

            def second(j, x, begin=False):
                e = 2 * j + x
                pe.wait_ge(w2_in[x], 16 * j + 16)
                pe.wait_ge(e_gelu, KE * e + KE)
                for i, (t0, w) in enumerate(CAP_TILES):
                    bank = ring[i // 2]
                    if not begin and i != 1:
                        pe.wait_ge(e_y, 2 * e - 1 + i // 2)
                    ins = chain(bank[0:w, (i % 2) * D:(i % 2 + 1) * D],
                                [(heT[x][:, m, t0:t0 + w], W2[x][:, m, :]) for m in range(KE)])
                    if i:
                        ins.then_inc(e_down, 1)

            first(0, 0, True)
            first(0, 1)
            second(0, 0, True)
            with pe.Fori(1, E16 // 2) as j:
                first(j, 0)
                second(j - 1, 1)
                first(j, 1)
                second(j, 0)
            second(E16 // 2 - 1, 1)

        @block.scalar
        def _(act):
            def turned(u, dst, key):
                bank = ring_ready(act, key)
                act.activation(dst, bank[:, :], ACT.Copy).then_inc(ring_empty(key), 1)

            def root(u):
                for w in range(norms_of(u)):
                    n = first_norm(u) + w
                    act.wait_ge(stats_ready, n + 1)
                    act.activation(sd[:, n % 2, :], mv[:, n % 2, :, 1], ACT.Sqrt, bias=eps_c[:, 0:1]).then_inc(sd_ready, 1)

            def take(u, key):
                p, s, k = u % 2, stage_of(u), key[1]
                if k[0] == "T":
                    turned(u, xT[:, p, int(k[1]), :], key)
                elif k[0] == "q":
                    bank = ring_ready(act, key)
                    dst = qk[:, 0, p, int(k[1]), :]
                    if s == "linear":
                        act.activation(dst, bank[:, :], ACT.Relu, scale=HD ** -0.5).then_inc(ring_empty(key), 1)
                    else:
                        scale = -D ** -0.5 if s == "attn" else -(D ** -1.0) * HD ** -0.5
                        act.activation(dst, bank[:, :], ACT.Copy, scale=scale).then_inc(ring_empty(key), 1)
                elif k in ("k0", "k1"):
                    bank = ring_ready(act, key)
                    c = int(k[1])
                    if s == "attn":
                        act.activation(qk[:, 1, p, c, :], bank[:, :], ACT.Copy).then_inc(ring_empty(key), 1)
                    else:
                        act.activation(qk[:, 1, p, c, :], bank[:, :], ACT.Copy, scale=evenrow[:, 0:1])
                        act.activation(kodd[:, p, c, :], bank[:, :], ACT.Copy, scale=evenrow[:, 1:2]).then_inc(ring_empty(key), 1)
                elif k[:2] == "kv":
                    t = int(k[2])
                    bank = ring_ready(act, key)
                    act.activation(lin_k[:, p, t, :], bank[:, 0:D], ACT.Relu, scale=HD ** -0.5)
                    act.activation(v[:, p, t, :], bank[:, D:2 * D], ACT.Copy).then_inc(ring_empty(key), 1)
                elif k[0] == "g":
                    x = int(k[1])
                    bank = ring_ready(act, key)
                    act.activation(gate_u[:, p, 2 * x:2 * x + 2, :].rearrange("p t d -> p (t d)"), bank[:, :], ACT.Silu)\
                        .then_inc(ring_empty(key), 1)

            def prep(u):
                for key in prep_keys(u):
                    take(u, key)

            def exp_item(n, item):
                w = (item[3] + 1) * P
                act.wait_ge(masked, n + 1)
                act.activation(prob[:, n % 4, 0:w], prob[:, n % 4, 0:w], ACT.Exp, scale=-1.0, bias=negmax[:, n % 8:n % 8 + 1],
                               accum_out=rsum[:, n % 8:n % 8 + 1]).then_inc(exped, 1)

            def copy_item(u, n, item):
                m, _, _, qt, j = item
                mm = first_group(u) + m
                act.wait_ge(pt_full, n + 1)
                if mm >= 2:
                    act.wait_ge(av_done, mm - 1)
                act.activation(probT[:, mm % 2, j, 0:(qt + 1) * P], pt_bank[n % 2][:, 0:(qt + 1) * P], ACT.Copy)\
                    .then_inc(pt_drained[n % 2], 1)

            act.wait_ge(const_v, 2)
            prep(0)
            for u in range(STEPS):
                s, p, l = stage_of(u), u % 2, layer_of(u)
                n0 = first_item(u)
                if s == "attn":
                    items = items_of(u)
                    for i in range(TT):
                        exp_item(n0 + i, items[i])
                    prep(u + 1)
                    for i in range(0, TT, 2):
                        copy_item(u, n0 + i, items[i])
                elif s == "heads":
                    items = items_of(u)
                    nxt = prep_keys(u + 1)
                    for i in range(3):
                        exp_item(n0 + i, items[i])
                    for i in range(len(items)):
                        if i % 2 == 0:
                            copy_item(u, n0 + i, items[i])
                        if i + 3 < len(items):
                            exp_item(n0 + i + 3, items[i + 3])
                        if i % 7 == 5 and nxt:
                            take(u + 1, nxt.pop(0))
                    for key in nxt:
                        take(u + 1, key)
                elif s == "mlp":
                    if u == B:
                        act.wait_ge(w_in["upb"], 16)
                    for m in range(0, KF):
                        key = (u, f"up{m}")
                        if RING[key] % 2 == 0:
                            bank = ring_ready(act, key)
                            act.activation(hid[:, m, :], bank[:, :], ACT.Relu, bias=up_b[:, l, m:m + 1]).then_inc(ring_empty(key), 1)
                    prep(u + 1)
                elif s == "top1":
                    act.wait_ge(gates, u % B + 1)
                    act.activation(ga_[:, 1, :, 0:E8], ga_[:, 0, :, 0:E8], ACT.Exp).then_inc(gexp, 1)
                    prep(u + 1)
                    key = (u, "mT")
                    bank = ring_ready(act, key)
                    act.activation(mwT, bank[0:E8, :], ACT.Copy).then_inc(ring_empty(key), 1)
                elif s == "linear":
                    for x in range(2):
                        key = (u, f"o{x}")
                        bank = ring_ready(act, key)
                        act.activation(lin_t[:, 0, 2 * x:2 * x + 2, :].rearrange("p t d -> p (t d)"), bank[:, :], ACT.Copy)\
                            .then_inc(ring_empty(key), 1)
                    act.wait_ge(lin_step, u % B + 1)
                    act.activation(srms[:, 1, :, :], srms[:, 0, :, :], ACT.Sqrt, scale=1.0 / HD).then_inc(lin_sd, 1)
                    prep(u + 1)
                    for c in range(KD):
                        turned(u, oT[:, p, c, :], (u, f"T{2 + c}"))
                else:
                    act.wait_ge(gates, B + u % B + 1)
                    act.activation(small[:, 2:4, :], small[:, 0:2, :], ACT.Exp, scale=-1.0).then_inc(gexp, 1)
                    prep(u + 1)
                if u + 2 < STEPS:
                    root(u + 2)

            def first(j, x):
                e = 2 * j + x
                for c in range(KD):
                    act.wait_ge(e_turned, 2 * e + c + 1)
                    act.activation(xeT[x][:, c, :], pt_bank[c][:, 0:CAP], ACT.Copy).then_inc(e_xT, 1)
                for m in range(KE):
                    act.wait_ge(e_up, KE * e + m + 1)
                    act.activation(heT[x][:, m, :], up_bank[m][:, 0:CAP], ACT.Gelu).then_inc(e_gelu, 1)

            with act.Fori(0, E16 // 2) as j:
                for x in range(2):
                    first(j, x)

        @block.vector
        def _(dve):
            steps = [0]

            def step(ins):
                ins.then_inc(dve_step, 1)
                steps[0] += 1

            def settle():
                dve.wait_ge(dve_step, steps[0])

            dve.wait_ge(ids_in, 16)
            dve.tensor_scalar(idf[:, 0, :], ids[:, :], 0.0, float(VOCAB), ALU.is_lt, ALU.mult).then_inc(id_ready, 1)
            dve.wait_ge(id_ready, 1)
            dve.tensor_tensor(out=idf[:, 1, :], in0=ids[:, :], in1=idf[:, 0, :], op=ALU.add).then_inc(id_ready, 1)
            dve.wait_ge(id_ready, 2)
            dve.tensor_scalar(idf[:, 0, :], idf[:, 1, :], 0.0, float(VOCAB - 1), ALU.max, ALU.min).then_inc(id_ready, 1)
            dve.wait_ge(id_ready, 3)
            dve.tensor_copy(idu[:, :], idf[:, 0, :]).then_inc(id_ready, 1)
            dve.memset(eps_c[:, :], EPS).then_inc(const_v, 1)
            dve.wait_ge(const_p, 2)
            dve.wait_ge(const_v, 1)
            step(dve.tensor_scalar(first16[:, :], iota16[:, :], -1.0, float(E16), ALU.mult, ALU.add))
            step(dve.tensor_scalar(base16[:, :], iota16[:, :], float(CAP), None, ALU.mult))
            bd = blockdiag[:, :].rearrange("p (n two d) -> p two n d", two=2, d=HD)
            step(dve.tensor_reduce(evenrow[:, 0:1], bd[:, 0, :, 0:1], AX.XY, ALU.add))
            settle()
            dve.tensor_reduce(evenrow[:, 1:2], bd[:, 1, :, 0:1], AX.XY, ALU.add).then_inc(const_v, 1)

            def normalise(u, w):
                n, b, p = first_norm(u) + w, u % B, u % 2
                into_h = norms_of(u) == 2 and w == 0
                for t in range(TT):
                    step(dve.bn_stats(stats[:, n % 2, t, :], h[:, b * TT + t, :]))
                settle()
                for t in range(TT):
                    ins = dve.bn_aggr(mv[:, n % 2, t, :], stats[:, n % 2, t, :])
                    if t < TT - 1:
                        step(ins)
                    else:
                        ins.then_inc(stats_ready, 1)
                return n

            def scale_rows(u, w):
                n, b, p = first_norm(u) + w, u % B, u % 2
                into_h = norms_of(u) == 2 and w == 0
                dve.wait_ge(sd_ready, n + 1)
                step(dve.reciprocal(rstd[:, n % 2, :], sd[:, n % 2, :]))
                settle()
                for t in range(TT):
                    dst = h[:, b * TT + t, :] if into_h else xn[:, p, t, :]
                    ins = dve.tensor_scalar(dst, h[:, b * TT + t, :], mv[:, n % 2, t, 0:1], rstd[:, n % 2, t:t + 1],
                                            ALU.subtract, ALU.mult)
                    if t < TT - 1 or into_h:
                        step(ins)
                    elif u < 4 * B:
                        ins.then_inc(norm_mid, 1)
                    else:
                        ins.then_inc(xn_dve, 1)

            def front(u):
                if u >= STEPS:
                    return
                b, p = u % B, u % 2
                if u >= 2:
                    dve.wait_ge(ring_full, RING[(u - 2, "T1")] + 1)
                    if stage_of(u - 2) == "route":
                        dve.wait_ge(kept, (u - 2) % B + 1)
                    else:
                        drained(dve, last_key(u - 2))
                if u < B:
                    dve.wait_ge(emb_in[b], 16 * TT)
                    if u == 0:
                        dve.wait_ge(pos_in, 16)
                    dve.tensor_tensor(out=xn[:, p, :, :], in0=h[:, b * TT:(b + 1) * TT, :], in1=pos, op=ALU.add).then_inc(xn_dve, 1)
                    return
                settle()
                drained(dve, last_key(u - B))
                for w in range(norms_of(u)):
                    normalise(u, w)
                    scale_rows(u, w)
                    if norms_of(u) == 2 and w == 0:
                        settle()
                        hb = h[:, b * TT:(b + 1) * TT, :]
                        row = lambda i: rows[:, 1, i:i + 1, :].to_broadcast([P, TT, D])
                        step(dve.tensor_tensor(out=hb, in0=hb, in1=row(3), op=ALU.mult))
                        settle()
                        step(dve.tensor_tensor(out=hb, in0=hb, in1=row(4), op=ALU.add))
                        settle()

            def take(u, key):
                p, s, k = u % 2, stage_of(u), key[1]
                if k[0] == "v" and s == "attn":
                    x = int(k[1])
                    bank = ring_ready(dve, key)
                    dve.tensor_copy(v[:, p, 2 * x:2 * x + 2, :].rearrange("p t d -> p (t d)"), bank[:, :]).then_inc(ring_empty(key), 1)
                elif k[0] == "v":
                    x = int(k[1])
                    if u == 4 * B and x == 0:
                        dve.wait_ge(odd_cleared, 1)
                        dve.wait_ge(zeroed, 80)
                    bank = ring_ready(dve, key)
                    for e, dst in enumerate((v, vodd)):
                        cut = lambda y: y.rearrange("p (n two d) -> p two n d", two=2, d=HD)[:, e]
                        ins = dve.tensor_scalar(cut(dst[:, p, 2 * x:2 * x + 2, :].rearrange("p t d -> p (t d)")),
                                                cut(bank[:, :]), D ** -1.0, None, ALU.mult)
                    ins.then_inc(ring_empty(key), 1)

            def prep(u):
                for key in prep_keys(u):
                    take(u, key)

            def mask_item(n, item):
                w = (item[3] + 1) * P
                dve.wait_ge(s_full, n + 1)
                if n >= 4:
                    dve.wait_ge(pt_full, n - 3)
                dve.tensor_tensor_reduce(out=prob[:, n % 4, 0:w], in0=s_bank[n % 3][:, 0:w], in1=causal[:, T - w:T],
                                         scale=1.0, scalar=3.0e38, op0=ALU.add, op1=ALU.min,
                                         accum_out=negmax[:, n % 8:n % 8 + 1]).then_inc(masked, 1)

            def invert(n):
                dve.wait_ge(exped, n + 1)
                dve.reciprocal(rinv[:, n % 8:n % 8 + 1], rsum[:, n % 8:n % 8 + 1]).then_inc(inverted, 1)

            def copy_item(u, n, item):
                m, _, _, qt, j = item
                mm = first_group(u) + m
                dve.wait_ge(pt_full, n + 1)
                if mm >= 2:
                    dve.wait_ge(av_done, mm - 1)
                dve.tensor_copy(probT[:, mm % 2, j, 0:(qt + 1) * P], pt_bank[n % 2][:, 0:(qt + 1) * P]).then_inc(pt_drained[n % 2], 1)

            def residual(u, base):
                b, p = u % B, u % 2
                for x in range(2):
                    key = (u, f"z{x}")
                    bank = ring_ready(dve, key)
                    r = slice(b * TT + 2 * x, b * TT + 2 * x + 2)
                    src = xn[:, p, 2 * x:2 * x + 2, :] if base == "xn" else h[:, r, :]
                    dve.tensor_tensor(out=h[:, r, :], in0=bank[:, :].rearrange("p (t d) -> p t d", t=2), in1=src, op=ALU.add)\
                        .then_inc(ring_empty(key), 1)
                    if stage_of(u) == "mlp":
                        if u == B:
                            dve.wait_ge(w_in["rows"], 160)
                        drained(dve, key)
                        step(dve.tensor_tensor(out=h[:, r, :], in0=h[:, r, :],
                                               in1=rows[:, layer_of(u), 0:1, :].to_broadcast([P, 2, D]), op=ALU.add))

            def first_of(dst, vals, top, width):
                t1 = ga_[:, 4, :, 0:width]
                m = small[:, 8, :]
                wide = lambda y: y.unsqueeze(2).to_broadcast([P, TT, width])
                order = first16[:, 0:width].unsqueeze(1).to_broadcast([P, TT, width])
                step(dve.tensor_tensor(out=t1, in0=vals, in1=wide(top), op=ALU.is_ge))
                settle()
                step(dve.tensor_tensor(out=t1, in0=t1, in1=order, op=ALU.mult))
                settle()
                step(dve.tensor_reduce(m, t1, AX.X, ALU.max))
                settle()
                step(dve.tensor_tensor(out=dst, in0=t1, in1=wide(m), op=ALU.is_equal))
                settle()

            def o_take(u, g, done):
                p = u % 2
                dve.wait_ge(av_done, done)
                if stage_of(u) == "attn":
                    dst = oT[:, p, :, g * P:(g + 1) * P]
                    dve.tensor_copy(dst, o_bank[:, 0:D].rearrange("p (c q) -> p c q", c=KD)).then_inc(o_drained, 1)
                else:
                    dve.tensor_copy(oT[:, p, g, :], o_bank[:, :]).then_inc(o_drained, 1)

            def attention(u):
                items, n0, m0 = items_of(u), first_item(u), first_group(u)
                for i in range(TT):
                    mask_item(n0 + i, items[i])
                    if i:
                        invert(n0 + i - 1)
                invert(n0 + TT - 1)
                prep(u + 1)
                for i in range(TT):
                    if i % 2 == 1:
                        copy_item(u, n0 + i, items[i])
                    if i:
                        o_take(u, i - 1, m0 + i)
                o_take(u, TT - 1, m0 + TT)
                residual(u, "xn")

            def many_heads(u):
                items, n0, m0 = items_of(u), first_item(u), first_group(u)
                nxt = prep_keys(u + 1)
                for i in range(3):
                    mask_item(n0 + i, items[i])
                    if i:
                        invert(n0 + i - 1)
                for i in range(len(items)):
                    if i % 2 == 1:
                        copy_item(u, n0 + i, items[i])
                    if i + 3 < len(items):
                        mask_item(n0 + i + 3, items[i + 3])
                    if i + 2 < len(items):
                        invert(n0 + i + 2)
                    if i == 36:
                        o_take(u, 0, m0 + 8)
                    if i % 7 == 5 and nxt:
                        take(u + 1, nxt.pop(0))
                for key in nxt:
                    take(u + 1, key)
                o_take(u, 1, m0 + 16)
                residual(u, "h")

            def feed_forward(u):
                l = layer_of(u)
                if u == B:
                    dve.wait_ge(w_in["upb"], 16)
                for m in range(KF):
                    key = (u, f"up{m}")
                    if RING[key] % 2 == 1:
                        bank = ring_ready(dve, key)
                        dve.tensor_scalar(hid[:, m, :], bank[:, :], up_b[:, l, m:m + 1], 0.0, ALU.add, ALU.max)\
                            .then_inc(ring_empty(key), 1)
                prep(u + 1)
                residual(u, "xn")

            def wide(y, n):
                return y.unsqueeze(2).to_broadcast([P, TT, n])

            def top1(u):
                b, p = u % B, u % 2
                if b == 0:
                    dve.wait_ge(w_in["gates"], 64)
                key = (u, "gate")
                bank = ring_ready(dve, key)
                lgt, z, ez, oh = lg[:, p, :, 0:E8], ga_[:, 0, :, 0:E8], ga_[:, 1, :, 0:E8], ga_[:, 2, :, 0:E8]
                dve.tensor_tensor(out=lgt, in0=bank[:, 0:TT * E8].rearrange("p (t e) -> p t e", e=E8),
                                  in1=gate8_b[:, :].unsqueeze(1).to_broadcast([P, TT, E8]), op=ALU.add).then_inc(ring_empty(key), 1)
                drained(dve, key)
                step(dve.tensor_reduce(small[:, 0, :], lgt, AX.X, ALU.max))
                settle()
                dve.tensor_tensor(out=z, in0=lgt, in1=wide(small[:, 0, :], E8), op=ALU.subtract).then_inc(gates, 1)
                first_of(oh, lgt, small[:, 0, :], E8)
                dve.wait_ge(gexp, b + 1)
                step(dve.tensor_reduce(small[:, 1, :], ez, AX.X, ALU.add))
                settle()
                step(dve.reciprocal(small[:, 2, :], small[:, 1, :]))
                settle()
                dve.tensor_tensor(out=mw[:, :, :], in0=oh, in1=wide(small[:, 2, :], E8), op=ALU.mult).then_inc(gmask, 1)
                prep(u + 1)
                for x in range(2):
                    key = (u, f"b{x}")
                    bank = ring_ready(dve, key)
                    r = slice(b * TT + 2 * x, b * TT + 2 * x + 2)
                    dve.tensor_tensor(out=h[:, r, :], in0=bank[:, :].rearrange("p (t d) -> p t d", t=2), in1=h[:, r, :], op=ALU.add)\
                        .then_inc(ring_empty(key), 1)
                    drained(dve, key)
                dve.wait_ge(gmask, b + 1)
                for t in range(TT):
                    for e in range(E8 // 2):
                        key = (u, f"y{t}{e}")
                        bank = ring_ready(dve, key)
                        ht = h[:, b * TT + t, :]
                        step(dve.scalar_tensor_tensor(out=ht, in0=bank[:, 0:D], scalar=mw[:, t, 2 * e:2 * e + 1], in1=ht,
                                                      op0=ALU.mult, op1=ALU.add))
                        settle()
                        dve.scalar_tensor_tensor(out=ht, in0=bank[:, D:2 * D], scalar=mw[:, t, 2 * e + 1:2 * e + 2], in1=ht,
                                                 op0=ALU.mult, op1=ALU.add).then_inc(ring_empty(key), 1)
                        drained(dve, key)

            def linear(u):
                b, p = u % B, u % 2
                key = (u, "kvm")
                bank = ring_ready(dve, key)
                dve.tensor_tensor(out=kvm[:, p, :, :], in0=bank[:, 0:D].rearrange("p (c n) -> p c n", c=KD),
                                  in1=blockdiag[:, :].unsqueeze(1).to_broadcast([P, KD, P]), op=ALU.mult)\
                    .then_inc(ring_empty(key), 1)
                drained(dve, (u, "o0"))
                drained(dve, (u, "o1"))
                o, sq, gated = lin_t[:, 0], lin_t[:, 1], lin_t[:, 2]
                heads = lambda y: y.rearrange("p t (h d) -> p t h d", d=HD)
                step(dve.tensor_tensor(out=sq, in0=o, in1=o, op=ALU.mult))
                settle()
                dve.tensor_reduce(srms[:, 0, :, :], heads(sq), AX.X, ALU.add).then_inc(lin_step, 1)
                step(dve.tensor_tensor(out=gated, in0=o, in1=gate_u[:, p, :, :], op=ALU.mult))
                dve.wait_ge(lin_sd, b + 1)
                step(dve.tensor_scalar(srms[:, 2, :, :], srms[:, 1, :, :], 1e-12, None, ALU.max))
                settle()
                step(dve.reciprocal(srms[:, 0, :, :], srms[:, 2, :, :]))
                settle()
                dve.tensor_tensor(out=heads(lin_y[:, p, :, :]), in0=heads(gated),
                                  in1=srms[:, 0, :, :].unsqueeze(3).to_broadcast([P, TT, HEADS, HD]), op=ALU.mult)\
                    .then_inc(lin_out, 1)
                residual(u, "h")

            def route(u):
                b, p = u % B, u % 2
                key = (u, "gate")
                bank = ring_ready(dve, key)
                lgt, rest, oh = lg[:, p, :, :], ga_[:, 0, :, :], [ga_[:, 2, :, :], ga_[:, 3, :, :]]
                dve.tensor_copy(lgt, bank[:, 0:TT * E16].rearrange("p (t e) -> p t e", e=E16)).then_inc(ring_empty(key), 1)
                drained(dve, key)
                step(dve.tensor_reduce(small[:, 0, :], lgt, AX.X, ALU.max))
                settle()
                first_of(oh[0], lgt, small[:, 0, :], E16)
                step(dve.scalar_tensor_tensor(out=rest, in0=oh[0], scalar=-FAR, in1=lgt, op0=ALU.mult, op1=ALU.add))
                settle()
                dve.tensor_reduce(small[:, 1, :], rest, AX.X, ALU.max).then_inc(gates, 1)
                dve.wait_ge(gates, B + b + 1)
                first_of(oh[1], rest, small[:, 1, :], E16)
                r = slice(b * TT, (b + 1) * TT)
                dve.tensor_tensor(out=cnt[:, r, :], in0=oh[0], in1=oh[1], op=ALU.add).then_inc(counts, 1)
                dve.wait_ge(gexp, B + b + 1)
                step(dve.tensor_scalar(small[:, 4:6, :], small[:, 2:4, :], 1.0, None, ALU.add))
                settle()
                step(dve.reciprocal(small[:, 6:8, :], small[:, 4:6, :]))
                settle()
                step(dve.tensor_tensor(out=small[:, 9, :], in0=small[:, 6, :], in1=small[:, 7, :], op=ALU.add))
                settle()
                step(dve.tensor_scalar(small[:, 10, :], small[:, 9, :], 1e-6, None, ALU.add))
                settle()
                step(dve.reciprocal(small[:, 11, :], small[:, 10, :]))
                settle()
                step(dve.tensor_tensor(out=small[:, 6:8, :], in0=small[:, 6:8, :],
                                       in1=small[:, 11:12, :].to_broadcast([P, 2, TT]), op=ALU.mult))
                key = (u, "rank")
                bank = ring_ready(dve, key)
                rk, t1 = ga_[:, 1, :, :], ga_[:, 5, :, :]
                dve.tensor_copy(rk, bank[:, 0:TT * E16].rearrange("p (t e) -> p t e", e=E16)).then_inc(ring_empty(key), 1)
                drained(dve, key)
                for k in range(TOPK):
                    rank, base, valid = small[:, 8, :], small[:, 9, :], small[:, 10, :]
                    step(dve.tensor_tensor(out=t1, in0=oh[k], in1=rk, op=ALU.mult))
                    settle()
                    step(dve.tensor_reduce(rank, t1, AX.X, ALU.add))
                    settle()
                    step(dve.tensor_tensor(out=t1, in0=oh[k], in1=base16[:, :].unsqueeze(1).to_broadcast([P, TT, E16]), op=ALU.mult))
                    settle()
                    step(dve.tensor_reduce(base, t1, AX.X, ALU.add))
                    step(dve.tensor_scalar(valid, rank, float(CAP), None, ALU.is_lt))
                    settle()
                    step(dve.tensor_tensor(out=wk[:, k, r], in0=small[:, 6 + k, :], in1=valid, op=ALU.mult))
                    step(dve.tensor_tensor(out=base, in0=base, in1=rank, op=ALU.add))
                    step(dve.tensor_scalar(small[:, 11, :], valid, -1048576.0, 1048576.0, ALU.mult, ALU.add))
                    settle()
                    dve.tensor_scalar(slot_g[:, k, r], base, float(SLOTS - 1), None, ALU.min).then_inc(slots_set, 1)
                    dve.tensor_tensor(out=slot_s[:, k, r], in0=base, in1=small[:, 11, :], op=ALU.add).then_inc(slots_set, 1)
                    dve.wait_ge(slots_set, 2 * TOPK * b + 2 * k + 2)

            bodies = {"attn": attention, "heads": many_heads, "mlp": feed_forward, "top1": top1, "linear": linear, "route": route}
            front(0)
            front(1)
            prep(0)
            for u in range(STEPS):
                bodies[stage_of(u)](u)
                front(u + 2)

            def results(j, x, begin=False):
                e = 2 * j + x
                if not begin:
                    dve.wait_ge(ye_out[x], 32 * j)
                dve.wait_ge(e_down, 2 * e + 1)
                dve.tensor_copy(ye[x][:, 0:2, :].rearrange("p t d -> p (t d)"), ring[0][:, :]).then_inc(e_y, 1)
                dve.wait_ge(e_down, 2 * e + 2)
                dve.tensor_copy(ye[x][0:CAP - 256, 2, :], ring[1][0:CAP - 256, 0:D]).then_inc(e_y, 1)

            results(0, 0, True)
            results(0, 1, True)
            with dve.Fori(1, E16 // 2) as j:
                for x in range(2):
                    results(j, x)
            for b in range(B):
                dve.wait_ge(got_in[b], 16 * TOPK * TT)
                for t in range(b * TT, (b + 1) * TT):
                    dve.scalar_tensor_tensor(out=h[:, t, :], in0=got[0][:, t, :], scalar=wk[:, 0, t:t + 1], in1=h[:, t, :],
                                             op0=ALU.mult, op1=ALU.add).then_inc(mixed0, 1)
                for t in range(b * TT, (b + 1) * TT):
                    dve.wait_ge(mixed0, t + 1)
                    dve.scalar_tensor_tensor(out=h[:, t, :], in0=got[1][:, t, :], scalar=wk[:, 1, t:t + 1], in1=h[:, t, :],
                                             op0=ALU.mult, op1=ALU.add).then_inc(mixed, 1)


def kernel(**inputs):
    import numpy as np
    import concourse.bacc as bacc
    from concourse.bass_utils import run_bass_kernel_spmd

    x = {k: np.asarray(v) for k, v in inputs.items()}
    turned = lambda w: np.ascontiguousarray(np.swapaxes(x[w], -1, -2))
    arrays = {n: x[n] for n in x if n.startswith("L0_tok_") and n not in ("L0_tok_bup",)}
    arrays["L0_ffn_expert_b"] = x["L0_ffn_expert_b"]
    arrays |= {
        "x_cols": np.ascontiguousarray(x["x"].reshape(NT, P).T),
        "bup_cols": np.ascontiguousarray(x["L0_tok_bup"].reshape(LAYERS, KF, P).transpose(2, 0, 1)),
        "heads_query": turned("L0_attn_W_query"), "heads_key": turned("L0_attn_W_key"),
        "heads_value": turned("L0_attn_W_value"), "heads_proj": turned("L0_attn_W_proj"),
        "router_t": turned("L0_ffn_router_w"), "router_b": x["L0_ffn_router_b"].reshape(1, E8),
        "top1_t": np.ascontiguousarray(x["L0_ffn_expert_w"].transpose(2, 0, 1).reshape(D, E8 * D)),
        "lin_q_t": turned("L1_attn_Wq"), "lin_o_t": turned("L1_attn_Wo"),
        "lin_kvu_t": np.concatenate([turned("L1_attn_Wk"), turned("L1_attn_Wv"), turned("L1_attn_Wu")], axis=1),
        "gate_t": turned("L1_ffn_gate_w"),
        "w1_rows": x["L1_ffn_w1"].reshape(E16 * D, DFF), "w2_rows": x["L1_ffn_w2"].reshape(E16 * DFF, D),
    }
    nc = bacc.Bacc("TRN2", target_bir_lowering=False, num_devices=1)
    a, sent = {}, {}
    for name, array in arrays.items():
        sent[f"in_{name}"] = np.ascontiguousarray(array)
        a[name] = nc.dram_tensor(f"in_{name}", array.shape, mybir.dt.from_np(array.dtype), kind="ExternalInput").ap()
    a["out"] = nc.dram_tensor("out_0_dram", (B, T, D), F32, kind="ExternalOutput").ap()
    tower_kernel(nc, a)
    got = run_bass_kernel_spmd(nc, [sent], core_ids=[0])
    return got.results[0]["out_0_dram"]
```

```python
from contextlib import ExitStack

import concourse.bass as bass
from concourse import mybir

F32 = mybir.dt.float32
BF16 = mybir.dt.bfloat16
I32 = mybir.dt.int32
U32 = mybir.dt.uint32
ALU = mybir.AluOpType
ACT = mybir.ActivationFunctionType
AX = mybir.AxisListType

P = 128
B, T, D = 4, 512, 256
TT = T // P
NT = B * TT
KD = D // P
VOCAB = 8000
LAYERS = 2
FF = 4 * D
KF = FF // P
HEADS, HD = 16, 16
E8 = 8
E16, TOPK, DFF = 16, 2, 512
KE = DFF // P
CAP = int(1.25 * B * T * TOPK / E16)
SLOTS = E16 * CAP
CAP_TILES = [(0, 128), (128, 128), (256, CAP - 256)]
EPS = 1e-5
FAR = 1e30

STAGES = ["attn", "mlp", "attn", "mlp", "heads", "top1", "linear", "route"]
SEQ = [(s, b) for s in range(6) for b in range(B)] + [(6, 0), (6, 1), (7, 0), (6, 2), (7, 1), (6, 3), (7, 2), (7, 3)]
STEPS = len(SEQ)
ITEMS = {"attn": TT, "heads": HEADS * TT}


def stage_of(u):
    return STAGES[SEQ[u][0]]


def batch_of(u):
    return SEQ[u][1]


def layer_of(u):
    return SEQ[u][0] // 2


def last_step(u):
    return SEQ.index((SEQ[u][0] - 1, batch_of(u)))


def prep_keys(u):
    if u >= STEPS:
        return []
    s = stage_of(u)
    keys = ["T0", "T1"]
    if s in ("attn", "heads"):
        keys += ["q0", "q1", "k0", "k1", "v0", "v1"]
    if s == "linear":
        keys += ["q0", "q1"] + [f"kv{t}" for t in range(TT)] + ["g0", "g1"]
    return [(u, k) for k in keys]


def step_keys(u):
    s = stage_of(u)
    own = lambda *names: [(u, n) for n in names]
    nxt = prep_keys(u + 1)
    if s == "attn":
        return nxt + own("z0", "z1")
    if s == "heads":
        return nxt[:5] + own("r0") + nxt[5:] + own("r1", "z0", "z1")
    if s == "mlp":
        return own(*[f"up{m}" for m in range(KF)]) + nxt + own("z0", "z1")
    if s == "top1":
        return own("gate") + nxt + own("mT", "b0", "b1") + own(*[f"y{t}{e}" for t in range(TT) for e in range(E8 // 2)])
    if s == "linear":
        return own("kvm", "o0", "o1") + nxt + own("T2", "T3", "z0", "z1")
    return own("gate") + nxt + own("rank")


def ring_plan():
    plan, used, bank = {}, [0, 0], 1
    for u in range(-1, STEPS):
        for key in prep_keys(0) if u < 0 else step_keys(u):
            bank = int(key[1] == "z1") if u >= 0 and stage_of(u) == "heads" else 1 - bank
            plan[key] = (len(plan), bank, used[bank])
            used[bank] += 1
    return plan, used


RING, RING_USES = ring_plan()


def first_item(u):
    return sum(ITEMS.get(stage_of(x), 0) for x in range(u))


def groups_of(u):
    if stage_of(u) == "attn":
        return [(0, 0, qt, [0]) for qt in range(TT)]
    return [(g, e, qt, [0, 1, 2, 3]) for g in range(KD) for qt in range(TT) for e in range(2)]


def items_of(u):
    return [(i, g, e, qt, j) for i, (g, e, qt, js) in enumerate(groups_of(u)) for j in js]


def first_group(u):
    return sum(len(groups_of(x)) for x in range(u) if stage_of(x) in ITEMS)


def norms_of(u):
    return 0 if u < B else 2 if stage_of(u) == "heads" else 1


def first_norm(u):
    return sum(norms_of(x) for x in range(u))


def last_key(u):
    return (u, f"y{TT - 1}{E8 // 2 - 1}") if stage_of(u) == "top1" else (u, "z1")


PAIRS = HEADS * TT // 2
AHEAD = 3


def tower_kernel(nc, a):
    ctx = ExitStack()
    with ctx:
        def sb(name, shape, dt=F32):
            return ctx.enter_context(nc.sbuf_tensor(name, shape, dt))

        def sem(name):
            return ctx.enter_context(nc.semaphore(name))

        attn_w = sb("attn_w", [P, LAYERS, 4, KD, D])
        up_w = sb("up_w", [P, LAYERS, KD, FF])
        down_w = sb("down_w", [P, LAYERS, KF, D])
        rows = sb("rows", [P, LAYERS, 5, D])
        up_b = sb("up_b", [P, LAYERS, KF])
        heads_w = sb("heads_w", [P, 4, KD, D])
        lin_q = sb("lin_q", [P, KD, D])
        lin_kvu = sb("lin_kvu", [P, KD, 3 * D])
        lin_o = sb("lin_o", [P, KD, D])
        gate8 = sb("gate8", [P, KD, E8])
        gate8_b = sb("gate8_b", [P, E8])
        expert_b = sb("expert_b", [E8, D])
        gate16 = sb("gate16", [P, KD, E16])
        top1_w = up_w[:, :, :, :].rearrange("p l k f -> p (l k f)").rearrange("p (k n) -> p k n", k=KD)
        moe_w = down_w[:, :, :, :].rearrange("p l k d -> p (l k d)")
        W1 = [moe_w[:, x * 1024:(x + 1) * 1024].rearrange("p (k f) -> p k f", k=KD) for x in range(2)]
        W2 = [moe_w[:, 2048 + x * 1024:2048 + (x + 1) * 1024].rearrange("p (m d) -> p m d", m=KE) for x in range(2)]
        h = sb("h", [P, NT, D])
        xn = sb("xn", [P, 2, TT, D])
        xT = sb("xT", [P, 2, KD, T])
        qk = sb("qk", [P, 2, 2, KD, T])
        kodd = sb("kodd", [P, 2, KD, T])
        v = sb("v", [P, 2, TT, D])
        vodd = sb("vodd", [P, 2, TT, D])
        oT = sb("oT", [P, 2, KD, T])
        hid = sb("hid", [P, KF, T])
        prob = sb("prob", [P, 4, T])
        probT = sb("probT", [P, 2, 4, T])
        pos = kodd[:, :, :, :].rearrange("p a k t -> p (a k t)")[:, 0:TT * D].rearrange("p (t d) -> p t d", t=TT)
        zeros = vodd[:, :, :, :].rearrange("p a t d -> p (a t d)")
        gate_u = kodd[:, :, :, :].rearrange("p a k t -> p a (k t)").rearrange("p a (t d) -> p a t d", t=TT)
        lin_k = qk[:, 1, :, :, :].rearrange("p a k t -> p a (k t)").rearrange("p a (t d) -> p a t d", t=TT)
        lin_y = vodd
        lin_t = hid[:, :, :].rearrange("p m t -> p (m t)").rearrange("p (x t d) -> p x t d", x=4, t=TT)
        xf = attn_w[:, :, :, :, :].rearrange("p a b k t -> p (a b k t)").rearrange("p (n d) -> p n d", n=NT)
        got = [xf, qk[:, :, :, :, :].rearrange("p a b k t -> p (a b k t)").rearrange("p (n d) -> p n d", n=NT)]
        flatT = probT[:, :, :, :].rearrange("p a b t -> p (a b t)")
        xe = [flatT[:, x * 768:(x + 1) * 768].rearrange("p (t d) -> p t d", t=3) for x in range(2)]
        ye = [flatT[:, 1536 + x * 768:1536 + (x + 1) * 768].rearrange("p (t d) -> p t d", t=3) for x in range(2)]
        xeT = [xT[:, :, :, :].rearrange("p a k t -> p (a k t)")[:, x * 640:(x + 1) * 640]
               .rearrange("p (k t) -> p k t", k=KD) for x in range(2)]
        heT = [hid[:, 4 * x:4 * x + 4, 0:CAP] for x in range(2)]
        kvm = sb("kvm", [P, 2, KD, P])
        ident = sb("ident", [P, P])
        ones_f = sb("ones_f", [P, P])
        blockdiag = sb("blockdiag", [P, P])
        causal = sb("causal", [P, T])
        evenrow = sb("evenrow", [P, 2])
        before = sb("before", [P, P], BF16)
        ones_b = sb("ones_b", [P, P], BF16)
        tmp_b = prob[:, 0, 0:P]
        eps_c = sb("eps_c", [P, 1])
        iota16 = sb("iota16", [P, E16])
        iota_i = sb("iota_i", [P, E16], I32)
        first16 = sb("first16", [P, E16])
        base16 = sb("base16", [P, E16])
        ids = sb("ids", [P, NT], I32)
        idf = sb("idf", [P, 2, NT])
        idu = sb("idu", [P, NT], U32)
        stats = sb("stats", [P, 2, TT, 6])
        mv = sb("mv", [P, 2, TT, 2])
        sd = sb("sd", [P, 2, TT])
        rstd = sb("rstd", [P, 2, TT])
        negmax = sb("negmax", [P, 16])
        rsum = sb("rsum", [P, 2, TT])
        rinv = sb("rinv", [P, 2, TT])
        hsum = sb("hsum", [P, 2, TT * 8])
        hinv = sb("hinv", [P, 2, TT * 8])
        hinv_wide = prob
        lg = causal[:, 0:2 * TT * E16].rearrange("p (x t e) -> p x t e", x=2, t=TT)
        ga_ = sb("ga_", [P, 6, TT, E16])
        small = sb("small", [P, 12, TT])
        mw = sb("mw", [P, TT, E8])
        mwT = hid[0:E8, 7, :]
        cnt = sb("cnt", [P, NT, E16], BF16)
        wk = sb("wk", [P, TOPK, NT])
        slot_s = sb("slot_s", [P, TOPK, NT], U32)
        slot_g = idf[:, :, :].bitcast(U32)
        srms = hid[:, 6, 0:3 * TT * HEADS].rearrange("p (x t h) -> p x t h", x=3, t=TT)

        ring = [ctx.enter_context(nc.psum_tensor(f"ring{i}", [P, T], F32)) for i in range(2)]
        s_bank = [ctx.enter_context(nc.psum_tensor(f"s_bank{i}", [P, T], F32)) for i in range(3)] + [ring[1]]
        pt_bank = [ctx.enter_context(nc.psum_tensor(f"pt_bank{i}", [P, T], F32)) for i in range(2)]
        o_bank = ctx.enter_context(nc.psum_tensor("o_bank", [P, T], F32))

        up_bank = [s_bank[0], s_bank[1], s_bank[2], o_bank]

        slots_x = nc.dram_tensor("slots_x", (SLOTS, D), F32, kind="Internal").ap()
        slots_y = nc.dram_tensor("slots_y", (SLOTS, D), F32, kind="Internal").ap()

        ids_in, pos_in, id_ready, const_p, const_v = sem("ids_in"), sem("pos_in"), sem("id_ready"), sem("const_p"), sem("const_v")
        emb_in = [sem(f"emb_in{b}") for b in range(B)]
        w_in = {n: sem(f"w_{n}") for n in ("attn0", "attn1", "up0", "up1", "down0", "down1", "rows", "upb",
                                           "heads", "lin", "gates", "top1")}
        zeroed = sem("zeroed")
        stats_ready, sd_ready, dve_step, norm_mid = sem("stats_ready"), sem("sd_ready"), sem("dve_step"), sem("norm_mid")
        xn_dve, xn_pool = sem("xn_dve"), sem("xn_pool")
        xn_turned = sem("xn_turned")
        pool_step = sem("pool_step")
        ring_full = sem("ring_full")
        ring_drained = [sem("ring_drained0"), sem("ring_drained1")]
        xT_read = sem("xT_read")
        qk_read = sem("qk_read")
        s_full, masked, exped, inverted, widened = sem("s_full"), sem("masked"), sem("exped"), sem("inverted"), sem("widened")
        pt_full = sem("pt_full")
        pt_drained = [sem("pt_drained0"), sem("pt_drained1")]
        av_done, o_full, o_drained, z_done = sem("av_done"), sem("o_full"), sem("o_drained"), sem("z_done")
        resid = sem("resid")
        odd_cleared = sem("odd_cleared")
        gates, gexp, gmask = sem("gates"), sem("gexp"), sem("gmask")
        lin_step, lin_sd, lin_out, lin_act = sem("lin_step"), sem("lin_sd"), sem("lin_out"), sem("lin_act")
        counts = sem("counts")
        slots_set, kept = sem("slots_set"), sem("kept")
        scattered = sem("scattered")
        w1_in, w2_in, xe_in, ye_out = ([sem(f"w1_in{i}") for i in range(2)], [sem(f"w2_in{i}") for i in range(2)],
                                       [sem(f"xe_in{i}") for i in range(2)], [sem(f"ye_out{i}") for i in range(2)])
        e_turned, e_xT, e_up, e_gelu, e_down, e_y = (sem("e_turned"), sem("e_xT"), sem("e_up"), sem("e_gelu"),
                                                     sem("e_down"), sem("e_y"))
        got_in = [sem(f"got_in{b}") for b in range(B)]
        mixed, mixed0, out_sent = sem("mixed"), sem("mixed0"), sem("out_sent")

        block = ctx.enter_context(nc.Block())

        def ring_free(eng, key):
            _, bank, before_it = RING[key]
            if before_it:
                eng.wait_ge(ring_drained[bank], before_it)
            return ring[bank]

        def filled(eng, key):
            eng.wait_ge(ring_full, RING[key][0] + 1)

        def ring_ready(eng, key):
            filled(eng, key)
            return ring[RING[key][1]]

        def ring_empty(key):
            return ring_drained[RING[key][1]]

        def drained(eng, key):
            eng.wait_ge(ring_drained[RING[key][1]], RING[key][2] + 1)

        def item_slot(u, i):
            return prob[:, i, :] if stage_of(u) == "attn" else hid[:, i % 8, :]

        def grid(t):
            return t.rearrange("(n p) d -> p n d", p=P)

        @block.sync
        def _(sync):
            sync.dma_start(ids[:, :], a["x_cols"]).then_inc(ids_in, 16)
            sync.dma_start(pos, grid(a["L0_tok_pos"])).then_inc(pos_in, 16)
            for l in range(LAYERS):
                for i, n in enumerate(("wq", "wk", "wv", "wo")):
                    sync.dma_start(attn_w[:, l, i, :, :], a[f"L0_tok_{n}"][l].rearrange("(k p) n -> p k n", p=P))\
                        .then_inc(w_in[f"attn{l}"], 16)
                if l == 0:
                    for m in range(LAYERS):
                        for i, n in enumerate(("bdown", "ga", "ba", "gm", "bm")):
                            sync.dma_start(rows[:, m, i, :], a[f"L0_tok_{n}"][m:m + 1, :].to_broadcast([P, D]))\
                                .then_inc(w_in["rows"], 16)
                    sync.dma_start(up_b[:, :, :], a["bup_cols"]).then_inc(w_in["upb"], 16)
                sync.dma_start(up_w[:, l, :, :], a["L0_tok_wup"][l].rearrange("(k p) n -> p k n", p=P))\
                    .then_inc(w_in[f"up{l}"], 16)
                sync.dma_start(down_w[:, l, :, :], a["L0_tok_wdown"][l].rearrange("(k p) n -> p k n", p=P))\
                    .then_inc(w_in[f"down{l}"], 16)
            for i, n in enumerate(("query", "key", "value", "proj")):
                sync.dma_start(heads_w[:, i, :, :], a[f"heads_{n}"].rearrange("(k p) n -> p k n", p=P))\
                    .then_inc(w_in["heads"], 16)
            sync.dma_start(gate8[:, :, :], a["router_t"].rearrange("(k p) n -> p k n", p=P)).then_inc(w_in["gates"], 16)
            sync.dma_start(gate16[:, :, :], a["gate_t"].rearrange("(k p) n -> p k n", p=P)).then_inc(w_in["gates"], 16)
            sync.dma_start(gate8_b[:, :], a["router_b"].to_broadcast([P, E8])).then_inc(w_in["gates"], 16)
            sync.dma_start(expert_b[:, :], a["L0_ffn_expert_b"]).then_inc(w_in["gates"], 16)
            sync.dma_start(lin_q[:, :, :], a["lin_q_t"].rearrange("(k p) n -> p k n", p=P)).then_inc(w_in["lin"], 16)
            sync.dma_start(lin_kvu[:, :, :], a["lin_kvu_t"].rearrange("(k p) n -> p k n", p=P)).then_inc(w_in["lin"], 16)
            sync.dma_start(lin_o[:, :, :], a["lin_o_t"].rearrange("(k p) n -> p k n", p=P)).then_inc(w_in["lin"], 16)
            sync.wait_ge(const_p, 1)
            for i in range(5):
                sync.dma_start(slots_x[i * 1024:(i + 1) * 1024, :].rearrange("(p r) d -> p (r d)", p=P), zeros)\
                    .then_inc(zeroed, 16)
            filled(sync, (4 * B - 1, "up7"))
            sync.dma_start(top1_w, a["top1_t"].rearrange("(k p) n -> p k n", p=P)).then_inc(w_in["top1"], 16)
            filled(sync, (4 * B - 1, "z1"))

            def weights1(e, x):
                sync.dma_start(W1[x], a["w1_rows"][bass.ds(e * D, D), :].rearrange("(k p) f -> p k f", p=P)).then_inc(w1_in[x], 16)

            def weights2(e, x):
                sync.dma_start(W2[x], a["w2_rows"][bass.ds(e * DFF, DFF), :].rearrange("(m p) d -> p m d", p=P)).then_inc(w2_in[x], 16)

            def tokens(e, x):
                src = slots_x[bass.ds(e * CAP, CAP), :]
                sync.dma_start(xe[x][:, 0:2, :], src[0:256, :].rearrange("(t p) d -> p t d", p=P)).then_inc(xe_in[x], 16)
                sync.dma_start(xe[x][0:CAP - 256, 2, :], src[256:CAP, :]).then_inc(xe_in[x], 16)

            def results(e, x):
                dst = slots_y[bass.ds(e * CAP, CAP), :]
                sync.wait_ge(e_y, 2 * e + 2)
                sync.dma_start(dst[0:256, :].rearrange("(t p) d -> p t d", p=P), ye[x][:, 0:2, :]).then_inc(ye_out[x], 16)
                sync.dma_start(dst[256:CAP, :], ye[x][0:CAP - 256, 2, :]).then_inc(ye_out[x], 16)

            for e in range(2):
                weights1(e, e)
                weights2(e, e)
            sync.wait_ge(scattered, 16 * TOPK * NT)
            for e in range(2):
                tokens(e, e)
            with sync.Fori(0, E16 // 2 - 1) as j:
                for x in range(2):
                    e = 2 * j + x
                    sync.wait_ge(e_up, KE * e + KE)
                    weights1(e + 2, x)
                    tokens(e + 2, x)
                    results(e, x)
                    weights2(e + 2, x)
            for x in range(2):
                results(E16 - 2 + x, x)
            out_v = a["out"].rearrange("b (t p) d -> b p t d", p=P)
            for b in range(B):
                sync.wait_ge(mixed, TT * (b + 1))
                sync.dma_start(out_v[b], h[:, b * TT:(b + 1) * TT, :]).then_inc(out_sent, 16)
            sync.wait_ge(out_sent, 16 * B)

        @block.gpsimd
        def _(pool):
            done = {}

            def step(ins):
                ins.then_inc(pool_step, 1)
                done["n"] = done.get("n", 0) + 1

            def settle():
                pool.wait_ge(pool_step, done["n"])

            pool.memset(zeros, 0.0).then_inc(const_p, 1)
            step(pool.memset(ident[:, :], 0.0))
            step(pool.memset(ones_f[:, :], 1.0))
            step(pool.memset(causal[:, :], 0.0))
            step(pool.memset(ones_b[:, :], 1.0))
            step(pool.iota(iota_i[:, :], pattern=[[1, E16]], base=0, channel_multiplier=0))
            settle()
            step(pool.affine_select(out=ident[:, :], in_=ident[:, :], compare_op=ALU.not_equal, fill=1.0, base=0,
                                    pattern=[[-1, P]], channel_multiplier=1))
            step(pool.affine_select(out=causal[:, T - P:T], in_=causal[:, T - P:T], compare_op=ALU.is_ge, fill=FAR, base=0,
                                    pattern=[[-1, P]], channel_multiplier=1))
            step(pool.affine_select(out=tmp_b, in_=ones_f[:, :], compare_op=ALU.is_gt, fill=0.0, base=0,
                                    pattern=[[1, P]], channel_multiplier=-1))
            step(pool.affine_select(out=blockdiag[:, :], in_=ones_f[:, :], compare_op=ALU.is_ge, fill=0.0, base=0,
                                    pattern=[[-HD, P // HD], [0, HD]], channel_multiplier=1))
            step(pool.tensor_copy(iota16[:, :], iota_i[:, :]))
            settle()
            step(pool.affine_select(out=blockdiag[:, :], in_=blockdiag[:, :], compare_op=ALU.is_ge, fill=0.0, base=HD - 1,
                                    pattern=[[HD, P // HD], [0, HD]], channel_multiplier=-1))
            settle()
            pool.tensor_copy(before[:, :], tmp_b).then_inc(const_p, 1)

            pool.wait_ge(id_ready, 4)
            for t in range(NT):
                pool.indirect_dma_start(out=h[:, t, :], out_offset=None, in_=a["L0_tok_emb"],
                                        in_offset=bass.IndirectOffsetOnAxis(ap=idu[:, t:t + 1], axis=0))\
                    .then_inc(emb_in[t // TT], 16)

            def affine(u):
                p = u % 2
                l, r = ((u // B - 1) // 2, 1 if u // B % 2 == 1 else 3)
                if u == B:
                    pool.wait_ge(w_in["rows"], 160)
                pool.wait_ge(norm_mid, u - B + 1)
                row = lambda i: rows[:, l, i:i + 1, :].to_broadcast([P, TT, D])
                step(pool.tensor_tensor(out=xn[:, p, :, :], in0=xn[:, p, :, :], in1=row(r), op=ALU.mult))
                settle()
                pool.tensor_tensor(out=xn[:, p, :, :], in0=xn[:, p, :, :], in1=row(r + 1), op=ALU.add).then_inc(xn_pool, 1)

            for u in range(STEPS):
                if stage_of(u) == "heads":
                    for g in range(KD):
                        pool.wait_ge(inverted, KD * batch_of(u) + g + 1)
                        pool.tensor_copy(hinv_wide[:, g, :].rearrange("p (x d) -> p x d", d=HD),
                                         hinv[:, g, :].unsqueeze(2).to_broadcast([P, TT * 8, HD])).then_inc(widened, 1)
                if u == 3 * B:
                    pool.wait_ge(av_done, first_group(4 * B))
                    pool.memset(v[:, :, :, :], 0.0).then_inc(odd_cleared, 1)
                if B <= u + 2 < 4 * B:
                    affine(u + 2)
                if stage_of(u) == "route":
                    b, p = batch_of(u), u % 2
                    pool.wait_ge(xn_dve, u - 3 * B + 1)
                    filled(pool, (3 * B - 1, "z1"))
                    pool.tensor_copy(xf[:, b * TT:(b + 1) * TT, :], xn[:, p, :, :]).then_inc(kept, 1)
                    pool.wait_ge(kept, b + 1)
                    pool.wait_ge(slots_set, 2 * TOPK * (b + 1))
                    if b == 0:
                        pool.wait_ge(zeroed, 80)
                    for t in range(b * TT, (b + 1) * TT):
                        for k in range(TOPK):
                            pool.indirect_dma_start(out=slots_x,
                                                    out_offset=bass.IndirectOffsetOnAxis(ap=slot_s[:, k, t:t + 1], axis=0),
                                                    in_=xf[:, t, :], in_offset=None,
                                                    bounds_check=SLOTS - 1, oob_is_err=False).then_inc(scattered, 16)
            for x in range(2):
                pool.wait_ge(ye_out[x], 16 * E16)
            pool.wait_ge(scattered, 16 * TOPK * NT)
            for b in range(B):
                for t in range(b * TT, (b + 1) * TT):
                    for k in range(TOPK):
                        pool.indirect_dma_start(out=got[k][:, t, :], out_offset=None, in_=slots_y,
                                                in_offset=bass.IndirectOffsetOnAxis(ap=slot_g[:, k, t:t + 1], axis=0))\
                            .then_inc(got_in[b], 16)

        @block.tensor
        def _(pe):
            def mm(out, lhsT, rhs, start, stop, **kw):
                return pe.matmul(out, lhsT, rhs, start=start, stop=stop, **kw)

            def chain(out, pairs):
                for i, (l, r) in enumerate(pairs):
                    ins = mm(out, l, r, i == 0, i == len(pairs) - 1)
                return ins

            def project(u, key):
                p, s, l = u % 2, stage_of(u), layer_of(u)
                k = key[1]
                bank = ring_free(pe, key)
                if k[0] == "T":
                    c = int(k[1])
                    if c == 0:
                        if B <= u < 4 * B:
                            pe.wait_ge(xn_pool, u - B + 1)
                        else:
                            pe.wait_ge(xn_dve, u + 1 if u < B else u - 3 * B + 1)
                    for t in range(TT):
                        ins = pe.transpose(bank[:, t * P:(t + 1) * P], xn[:, p, t, c * P:(c + 1) * P], ident[:, :])
                    ins.then_inc(ring_full, 1)
                    return
                if k == "q0":
                    drained(pe, (u, "T0"))
                    drained(pe, (u, "T1"))
                    if s == "attn" and batch_of(u) == 0:
                        pe.wait_ge(w_in[f"attn{l}"], 64)
                    if s == "heads" and batch_of(u) == 0:
                        pe.wait_ge(w_in["heads"], 64)
                    if s == "linear" and batch_of(u) == 0:
                        pe.wait_ge(w_in["lin"], 48)
                if k[0] in "qk" and k[1] != "v":
                    c = int(k[1])
                    i = "qk".index(k[0])
                    w = attn_w[:, l, i] if s == "attn" else heads_w[:, i] if s == "heads" else lin_q
                    chain(bank[:, :], [(w[:, kk, c * P:(c + 1) * P], xT[:, p, kk, :]) for kk in range(KD)])\
                        .then_inc(ring_full, 1)
                elif k[0] == "v":
                    w = attn_w[:, l, 2] if s == "attn" else heads_w[:, 2]
                    for t in range(2):
                        tt = 2 * int(k[1]) + t
                        ins = chain(bank[:, t * D:(t + 1) * D],
                                    [(xT[:, p, kk, tt * P:(tt + 1) * P], w[:, kk, :]) for kk in range(KD)])
                    ins.then_inc(ring_full, 1)
                elif k[:2] == "kv":
                    t = int(k[2])
                    chain(bank[:, :], [(xT[:, p, kk, t * P:(t + 1) * P], lin_kvu[:, kk, 0:2 * D]) for kk in range(KD)])\
                        .then_inc(ring_full, 1)
                else:
                    for t in range(2):
                        tt = 2 * int(k[1]) + t
                        ins = chain(bank[:, t * D:(t + 1) * D],
                                    [(xT[:, p, kk, tt * P:(tt + 1) * P], lin_kvu[:, kk, 2 * D:3 * D]) for kk in range(KD)])
                    ins.then_inc(ring_full, 1)

            def prep(u):
                for key in prep_keys(u):
                    project(u, key)

            def scores(u, i):
                _, g, e, qt, j = items_of(u)[i]
                n0, p, w = first_item(u), u % 2, (qt + 1) * P
                if stage_of(u) == "attn":
                    if n0 + i >= 3:
                        pe.wait_ge(masked, n0 + max(i - 2, 0))
                    ins = chain(s_bank[i % 3][:, 0:w], [(qk[:, 0, p, kk, qt * P:w], qk[:, 1, p, kk, 0:w]) for kk in range(KD)])
                else:
                    pe.wait_ge(masked, n0 + max(i // 2 * 2 - 2, 0))
                    if i == 3:
                        pe.wait_ge(ring_drained[1], RING[(u, "z1")][2])
                    r = slice(32 * j, 32 * j + 32)
                    keys = kodd if e else qk[:, 1]
                    ins = mm(s_bank[i % 4][:, 0:w], qk[r, 0, p, g, qt * P:w], keys[r, p, g, 0:w], True, True,
                             tile_position=(32 * j, 0))
                ins.then_inc(s_full, 1)

            def turn(u, i):
                qt, n = items_of(u)[i][3], first_item(u) + i
                pe.wait_ge(exped, n + 1)
                if n >= 2:
                    pe.wait_ge(pt_drained[n % 2], n // 2)
                for kt in range(qt + 1):
                    ins = pe.transpose(pt_bank[n % 2][:, kt * P:(kt + 1) * P], item_slot(u, i)[:, kt * P:(kt + 1) * P], ident[:, :])
                ins.then_inc(pt_full, 1)

            def weigh(u, i, o_use):
                p, m = u % 2, first_group(u) + i
                g, e, qt, js = groups_of(u)[i]
                last_n = first_item(u) + (i + 1) * len(js) - 1
                for x in range(2):
                    if last_n >= x:
                        pe.wait_ge(pt_drained[x], (last_n - x) // 2 + 1)
                if o_use and qt == 0 and e == 0 or stage_of(u) == "attn" and o_use:
                    pe.wait_ge(o_drained, o_use)
                if stage_of(u) == "attn":
                    for c in range(KD):
                        for kt in range(qt + 1):
                            ins = mm(o_bank[:, c * P:(c + 1) * P], v[:, p, kt, c * P:(c + 1) * P],
                                     probT[:, m % 2, 0, kt * P:(kt + 1) * P], kt == 0, kt == qt)
                else:
                    vals = vodd if e else v
                    for kt in range(qt + 1):
                        for j in range(4):
                            c0 = g * P + 32 * j
                            ins = mm(o_bank[32 * j:32 * j + 32, qt * P:(qt + 1) * P], vals[:, p, kt, c0:c0 + 32],
                                     probT[:, m % 2, j, kt * P:(kt + 1) * P], e == 0 and kt == 0, e == 1 and kt == qt,
                                     tile_position=(0, 32 * j))
                ins.then_inc(av_done, 1)

            def widths(u, g):
                bank = ring_free(pe, (u, f"r{g}"))
                pe.wait_ge(widened, KD * batch_of(u) + g + 1)
                for qt in range(TT):
                    ins = pe.transpose(bank[:, qt * P:(qt + 1) * P], hinv_wide[:, g, qt * P:(qt + 1) * P], ident[:, :])
                ins.then_inc(ring_full, 1)

            def out_proj(u, w):
                p = u % 2
                for x in range(2):
                    bank = ring_free(pe, (u, f"z{x}"))
                    for t in range(2):
                        tt = 2 * x + t
                        ins = chain(bank[:, t * D:(t + 1) * D], [(oT[:, p, c, tt * P:(tt + 1) * P], w[:, c, :]) for c in range(KD)])
                    ins.then_inc(ring_full, 1)

            o_uses = 0
            pe.wait_ge(const_p, 2)
            prep(0)
            for u in range(STEPS):
                s, p, l = stage_of(u), u % 2, layer_of(u)
                n0, m0 = first_item(u), first_group(u)
                if s == "attn":
                    for k in ("q0", "q1", "k0", "k1", "v0", "v1"):
                        drained(pe, (u, k))
                    for i in range(TT):
                        scores(u, i)
                    prep(u + 1)
                    for i in range(TT):
                        turn(u, i)
                        if i:
                            weigh(u, i - 1, o_uses)
                            o_uses += 1
                    weigh(u, TT - 1, o_uses)
                    o_uses += 1
                    pe.wait_ge(o_drained, o_uses)
                    out_proj(u, attn_w[:, l, 3])
                elif s == "heads":
                    for k in ("q0", "q1", "k0", "k1", "v0", "v1"):
                        drained(pe, (u, k))
                    nxt = prep_keys(u + 1)
                    for i in range(2 * AHEAD):
                        scores(u, i)
                    for k in range(PAIRS):
                        for i in range(2 * (k + AHEAD), min(2 * (k + AHEAD) + 2, 2 * PAIRS)):
                            scores(u, i)
                        turn(u, 2 * k)
                        turn(u, 2 * k + 1)
                        if k >= 3 and k % 2 == 1:
                            weigh(u, (k - 3) // 2, o_uses)
                            if (k - 3) // 2 == 7:
                                o_uses += 1
                        if k % 4 == 1 and nxt:
                            project(u + 1, nxt.pop(0))
                        if k == 18:
                            widths(u, 0)
                    weigh(u, PAIRS // 2 - 1, o_uses)
                    o_uses += 1
                    widths(u, 1)
                    drained(pe, (u, "r0"))
                    drained(pe, (u, "r1"))
                    pe.wait_ge(masked, n0 + 2 * PAIRS)
                    out_proj(u, heads_w[:, 3])
                elif s == "mlp":
                    drained(pe, (u, "T0"))
                    drained(pe, (u, "T1"))
                    if batch_of(u) == 0:
                        pe.wait_ge(w_in[f"up{l}"], 16)
                    for m in range(KF):
                        bank = ring_free(pe, (u, f"up{m}"))
                        chain(bank[:, :], [(up_w[:, l, kk, m * P:(m + 1) * P], xT[:, p, kk, :]) for kk in range(KD)])\
                            .then_inc(ring_full, 1)
                    prep(u + 1)
                    if batch_of(u) == 0:
                        pe.wait_ge(w_in[f"down{l}"], 16)
                    drained(pe, (u, "up6"))
                    drained(pe, (u, "up7"))
                    for x in range(2):
                        bank = ring_free(pe, (u, f"z{x}"))
                        for t in range(2):
                            tt = 2 * x + t
                            ins = chain(bank[:, t * D:(t + 1) * D],
                                        [(hid[:, m, tt * P:(tt + 1) * P], down_w[:, l, m, :]) for m in range(KF)])
                        ins.then_inc(ring_full, 1)
                elif s == "top1":
                    drained(pe, (u, "T0"))
                    drained(pe, (u, "T1"))
                    if batch_of(u) == 0:
                        pe.wait_ge(w_in["gates"], 64)
                        pe.wait_ge(w_in["top1"], 16)
                    bank = ring_free(pe, (u, "gate"))
                    for t in range(TT):
                        ins = chain(bank[:, t * E8:(t + 1) * E8],
                                    [(xT[:, p, kk, t * P:(t + 1) * P], gate8[:, kk, :]) for kk in range(KD)])
                    ins.then_inc(ring_full, 1)
                    prep(u + 1)
                    bank = ring_free(pe, (u, "mT"))
                    pe.wait_ge(gmask, batch_of(u) + 1)
                    for t in range(TT):
                        ins = pe.transpose(bank[0:E8, t * P:(t + 1) * P], mw[:, t, :], ident[:, :])
                    ins.then_inc(ring_full, 1)
                    drained(pe, (u, "mT"))
                    for x in range(2):
                        bank = ring_free(pe, (u, f"b{x}"))
                        for t in range(2):
                            tt = 2 * x + t
                            ins = mm(bank[:, t * D:(t + 1) * D], mwT[:, tt * P:(tt + 1) * P], expert_b[:, :], True, True)
                        ins.then_inc(ring_full, 1)
                    for t in range(TT):
                        for e in range(E8 // 2):
                            bank = ring_free(pe, (u, f"y{t}{e}"))
                            chain(bank[:, :], [(xT[:, p, kk, t * P:(t + 1) * P], top1_w[:, kk, e * 2 * D:(e + 1) * 2 * D])
                                               for kk in range(KD)]).then_inc(ring_full, 1)
                elif s == "linear":
                    for k in ("q0", "q1", "kv0", "kv1", "kv2", "kv3", "g0", "g1"):
                        drained(pe, (u, k))
                    bank = ring_free(pe, (u, "kvm"))
                    for c in range(KD):
                        ins = chain(bank[:, c * P:(c + 1) * P],
                                    [(lin_k[:, p, t, c * P:(c + 1) * P], v[:, p, t, c * P:(c + 1) * P]) for t in range(TT)])
                    ins.then_inc(ring_full, 1)
                    drained(pe, (u, "kvm"))
                    for x in range(2):
                        bank = ring_free(pe, (u, f"o{x}"))
                        for t in range(2):
                            tt = 2 * x + t
                            for c in range(KD):
                                ins = mm(bank[:, t * D + c * P:t * D + (c + 1) * P], qk[:, 0, p, c, tt * P:(tt + 1) * P],
                                         kvm[:, p, c, :], True, True)
                        ins.then_inc(ring_full, 1)
                    prep(u + 1)
                    for c in range(KD):
                        bank = ring_free(pe, (u, f"T{2 + c}"))
                        pe.wait_ge(lin_out, batch_of(u) + 1)
                        for t in range(TT):
                            ins = pe.transpose(bank[:, t * P:(t + 1) * P], lin_y[:, p, t, c * P:(c + 1) * P], ident[:, :])
                        ins.then_inc(ring_full, 1)
                    drained(pe, (u, "T2"))
                    drained(pe, (u, "T3"))
                    out_proj(u, lin_o)
                else:
                    drained(pe, (u, "T0"))
                    drained(pe, (u, "T1"))
                    bank = ring_free(pe, (u, "gate"))
                    for t in range(TT):
                        ins = chain(bank[:, t * E16:(t + 1) * E16],
                                    [(xT[:, p, kk, t * P:(t + 1) * P], gate16[:, kk, :]) for kk in range(KD)])
                    ins.then_inc(ring_full, 1)
                    prep(u + 1)
                    bank = ring_free(pe, (u, "rank"))
                    b = batch_of(u)
                    pe.wait_ge(counts, b + 1)
                    for t in range(TT):
                        tt = b * TT + t
                        ins = chain(bank[:, t * E16:(t + 1) * E16],
                                    [(before[:, :], cnt[:, tt, :])] + [(ones_b[:, :], cnt[:, y, :]) for y in range(tt)])
                    ins.then_inc(ring_full, 1)
            for i in range(2):
                pe.wait_ge(ring_drained[i], RING_USES[i])

            def first(j, x, begin=False):
                e = 2 * j + x
                pe.wait_ge(xe_in[x], 32 * j + 32)
                for c in range(KD):
                    if not begin:
                        pe.wait_ge(e_xT, 2 * e - 1 + c)
                    for i, (t0, w) in enumerate(CAP_TILES):
                        ins = pe.transpose(pt_bank[c][:, t0:t0 + w], xe[x][0:w, i, c * P:(c + 1) * P], ident[0:w, 0:w])
                    ins.then_inc(e_turned, 1)
                pe.wait_ge(w1_in[x], 16 * j + 16)
                pe.wait_ge(e_xT, 2 * e + 2)
                for m in range(KE):
                    if not begin:
                        pe.wait_ge(e_gelu, KE * e - KE + m + 1)
                    chain(up_bank[m][:, 0:CAP], [(W1[x][:, kk, m * P:(m + 1) * P], xeT[x][:, kk, :]) for kk in range(KD)])\
                        .then_inc(e_up, 1)

            def second(j, x, begin=False):
                e = 2 * j + x
                pe.wait_ge(w2_in[x], 16 * j + 16)
                pe.wait_ge(e_gelu, KE * e + KE)
                for i, (t0, w) in enumerate(CAP_TILES):
                    bank = ring[i // 2]
                    if not begin and i != 1:
                        pe.wait_ge(e_y, 2 * e - 1 + i // 2)
                    ins = chain(bank[0:w, (i % 2) * D:(i % 2 + 1) * D],
                                [(heT[x][:, m, t0:t0 + w], W2[x][:, m, :]) for m in range(KE)])
                    if i:
                        ins.then_inc(e_down, 1)

            first(0, 0, True)
            first(0, 1)
            second(0, 0, True)
            with pe.Fori(1, E16 // 2) as j:
                first(j, 0)
                second(j - 1, 1)
                first(j, 1)
                second(j, 0)
            second(E16 // 2 - 1, 1)

        @block.scalar
        def _(act):
            def turned(u, dst, key):
                bank = ring_ready(act, key)
                act.activation(dst, bank[:, :], ACT.Copy).then_inc(ring_empty(key), 1)

            def root(u):
                for w in range(norms_of(u)):
                    n = first_norm(u) + w
                    act.wait_ge(stats_ready, n + 1)
                    act.activation(sd[:, n % 2, :], mv[:, n % 2, :, 1], ACT.Sqrt, bias=eps_c[:, 0:1]).then_inc(sd_ready, 1)

            def take(u, key):
                p, s, k = u % 2, stage_of(u), key[1]
                if k[0] == "T":
                    turned(u, xT[:, p, int(k[1]), :], key)
                elif k[0] == "q":
                    bank = ring_ready(act, key)
                    dst = qk[:, 0, p, int(k[1]), :]
                    if s == "linear":
                        act.activation(dst, bank[:, :], ACT.Relu, scale=HD ** -0.5).then_inc(ring_empty(key), 1)
                    else:
                        scale = -D ** -0.5 if s == "attn" else -(D ** -1.0) * HD ** -0.5
                        act.activation(dst, bank[:, :], ACT.Copy, scale=scale).then_inc(ring_empty(key), 1)
                elif k in ("k0", "k1"):
                    bank = ring_ready(act, key)
                    c = int(k[1])
                    if s == "attn":
                        act.activation(qk[:, 1, p, c, :], bank[:, :], ACT.Copy).then_inc(ring_empty(key), 1)
                    else:
                        act.activation(qk[:, 1, p, c, :], bank[:, :], ACT.Copy, scale=evenrow[:, 0:1])
                        act.activation(kodd[:, p, c, :], bank[:, :], ACT.Copy, scale=evenrow[:, 1:2]).then_inc(ring_empty(key), 1)
                elif k[:2] == "kv":
                    t = int(k[2])
                    bank = ring_ready(act, key)
                    act.activation(lin_k[:, p, t, :], bank[:, 0:D], ACT.Relu, scale=HD ** -0.5)
                    act.activation(v[:, p, t, :], bank[:, D:2 * D], ACT.Copy).then_inc(ring_empty(key), 1)
                elif k[0] == "g":
                    x = int(k[1])
                    bank = ring_ready(act, key)
                    act.activation(gate_u[:, p, 2 * x:2 * x + 2, :].rearrange("p t d -> p (t d)"), bank[:, :], ACT.Silu)\
                        .then_inc(ring_empty(key), 1)

            def prep(u):
                for key in prep_keys(u):
                    take(u, key)

            def exp_item(u, i):
                _, g, e, qt, j = items_of(u)[i]
                n, w = first_item(u) + i, (qt + 1) * P
                total = rsum[:, u % 2, qt:qt + 1] if stage_of(u) == "attn" else hsum[:, g, qt * 8 + 2 * j + e:qt * 8 + 2 * j + e + 1]
                act.wait_ge(masked, n + 1)
                act.activation(item_slot(u, i)[:, 0:w], item_slot(u, i)[:, 0:w], ACT.Exp, scale=-1.0,
                               bias=negmax[:, n % 16:n % 16 + 1], accum_out=total).then_inc(exped, 1)

            def copy_item(u, i):
                m, _, _, qt, j = items_of(u)[i]
                n, mm = first_item(u) + i, first_group(u) + m
                act.wait_ge(pt_full, n + 1)
                if mm >= 2:
                    act.wait_ge(av_done, mm - 1)
                act.activation(probT[:, mm % 2, j, 0:(qt + 1) * P], pt_bank[n % 2][:, 0:(qt + 1) * P], ACT.Copy)\
                    .then_inc(pt_drained[n % 2], 1)

            def o_take(u, g):
                act.wait_ge(av_done, first_group(u) + 8 * g + 8)
                act.activation(oT[:, u % 2, g, :], o_bank[:, :], ACT.Copy).then_inc(o_drained, 1)

            act.wait_ge(const_v, 2)
            prep(0)
            for u in range(STEPS):
                s, p, l = stage_of(u), u % 2, layer_of(u)
                n0 = first_item(u)
                if s == "attn":
                    for i in range(TT):
                        exp_item(u, i)
                    prep(u + 1)
                    for i in range(0, TT, 2):
                        copy_item(u, i)
                elif s == "heads":
                    nxt = prep_keys(u + 1)
                    for i in range(2 * AHEAD):
                        exp_item(u, i)
                    for k in range(PAIRS):
                        copy_item(u, 2 * k)
                        for i in range(2 * (k + AHEAD), min(2 * (k + AHEAD) + 2, 2 * PAIRS)):
                            exp_item(u, i)
                        if k % 4 == 1 and nxt:
                            take(u + 1, nxt.pop(0))
                        if k == 18:
                            o_take(u, 0)
                    o_take(u, 1)
                elif s == "mlp":
                    if u == B:
                        act.wait_ge(w_in["upb"], 16)
                    for m in range(0, KF):
                        key = (u, f"up{m}")
                        if RING[key][1] == 0:
                            bank = ring_ready(act, key)
                            act.activation(hid[:, m, :], bank[:, :], ACT.Relu, bias=up_b[:, l, m:m + 1]).then_inc(ring_empty(key), 1)
                    prep(u + 1)
                elif s == "top1":
                    act.wait_ge(gates, batch_of(u) + 1)
                    act.activation(ga_[:, 1, :, 0:E8], ga_[:, 0, :, 0:E8], ACT.Exp).then_inc(gexp, 1)
                    prep(u + 1)
                    key = (u, "mT")
                    bank = ring_ready(act, key)
                    act.activation(mwT, bank[0:E8, :], ACT.Copy).then_inc(ring_empty(key), 1)
                elif s == "linear":
                    for x in range(2):
                        key = (u, f"o{x}")
                        bank = ring_ready(act, key)
                        act.activation(lin_t[:, 0, 2 * x:2 * x + 2, :].rearrange("p t d -> p (t d)"), bank[:, :], ACT.Copy)\
                            .then_inc(ring_empty(key), 1)
                    act.wait_ge(lin_step, batch_of(u) + 1)
                    act.activation(srms[:, 1, :, :], srms[:, 0, :, :], ACT.Sqrt, scale=1.0 / HD).then_inc(lin_sd, 1)
                    prep(u + 1)
                    for c in range(KD):
                        turned(u, oT[:, p, c, :], (u, f"T{2 + c}"))
                else:
                    act.wait_ge(gates, B + batch_of(u) + 1)
                    act.activation(small[:, 2:4, :], small[:, 0:2, :], ACT.Exp, scale=-1.0).then_inc(gexp, 1)
                    prep(u + 1)
                if u + 2 < STEPS:
                    root(u + 2)

            def first(j, x):
                e = 2 * j + x
                for c in range(KD):
                    act.wait_ge(e_turned, 2 * e + c + 1)
                    act.activation(xeT[x][:, c, :], pt_bank[c][:, 0:CAP], ACT.Copy).then_inc(e_xT, 1)
                for m in range(KE):
                    act.wait_ge(e_up, KE * e + m + 1)
                    act.activation(heT[x][:, m, :], up_bank[m][:, 0:CAP], ACT.Gelu).then_inc(e_gelu, 1)

            with act.Fori(0, E16 // 2) as j:
                for x in range(2):
                    first(j, x)

        @block.vector
        def _(dve):
            steps = [0]

            def step(ins):
                ins.then_inc(dve_step, 1)
                steps[0] += 1

            def settle():
                dve.wait_ge(dve_step, steps[0])

            dve.wait_ge(ids_in, 16)
            dve.tensor_scalar(idf[:, 0, :], ids[:, :], 0.0, float(VOCAB), ALU.is_lt, ALU.mult).then_inc(id_ready, 1)
            dve.wait_ge(id_ready, 1)
            dve.tensor_tensor(out=idf[:, 1, :], in0=ids[:, :], in1=idf[:, 0, :], op=ALU.add).then_inc(id_ready, 1)
            dve.wait_ge(id_ready, 2)
            dve.tensor_scalar(idf[:, 0, :], idf[:, 1, :], 0.0, float(VOCAB - 1), ALU.max, ALU.min).then_inc(id_ready, 1)
            dve.wait_ge(id_ready, 3)
            dve.tensor_copy(idu[:, :], idf[:, 0, :]).then_inc(id_ready, 1)
            dve.memset(eps_c[:, :], EPS).then_inc(const_v, 1)
            dve.wait_ge(const_p, 2)
            dve.wait_ge(const_v, 1)
            step(dve.tensor_scalar(first16[:, :], iota16[:, :], -1.0, float(E16), ALU.mult, ALU.add))
            step(dve.tensor_scalar(base16[:, :], iota16[:, :], float(CAP), None, ALU.mult))
            bd = blockdiag[:, :].rearrange("p (n two d) -> p two n d", two=2, d=HD)
            step(dve.tensor_reduce(evenrow[:, 0:1], bd[:, 0, :, 0:1], AX.XY, ALU.add))
            settle()
            dve.tensor_reduce(evenrow[:, 1:2], bd[:, 1, :, 0:1], AX.XY, ALU.add).then_inc(const_v, 1)

            def normalise(u, w):
                n, b, p = first_norm(u) + w, batch_of(u), u % 2
                into_h = norms_of(u) == 2 and w == 0
                for t in range(TT):
                    step(dve.bn_stats(stats[:, n % 2, t, :], h[:, b * TT + t, :]))
                settle()
                for t in range(TT):
                    ins = dve.bn_aggr(mv[:, n % 2, t, :], stats[:, n % 2, t, :])
                    if t < TT - 1:
                        step(ins)
                    else:
                        ins.then_inc(stats_ready, 1)
                return n

            def scale_rows(u, w):
                n, b, p = first_norm(u) + w, batch_of(u), u % 2
                into_h = norms_of(u) == 2 and w == 0
                dve.wait_ge(sd_ready, n + 1)
                step(dve.reciprocal(rstd[:, n % 2, :], sd[:, n % 2, :]))
                settle()
                for t in range(TT):
                    dst = h[:, b * TT + t, :] if into_h else xn[:, p, t, :]
                    ins = dve.tensor_scalar(dst, h[:, b * TT + t, :], mv[:, n % 2, t, 0:1], rstd[:, n % 2, t:t + 1],
                                            ALU.subtract, ALU.mult)
                    if t < TT - 1 or into_h:
                        step(ins)
                    elif u < 4 * B:
                        ins.then_inc(norm_mid, 1)
                    else:
                        ins.then_inc(xn_dve, 1)

            def front(u):
                if u >= STEPS:
                    return
                b, p = batch_of(u), u % 2
                if u >= 2:
                    filled(dve, (u - 2, "T1"))
                    if stage_of(u - 2) == "route":
                        dve.wait_ge(kept, batch_of(u - 2) + 1)
                    else:
                        drained(dve, last_key(u - 2))
                if u < B:
                    dve.wait_ge(emb_in[b], 16 * TT)
                    if u == 0:
                        dve.wait_ge(pos_in, 16)
                    dve.tensor_tensor(out=xn[:, p, :, :], in0=h[:, b * TT:(b + 1) * TT, :], in1=pos, op=ALU.add).then_inc(xn_dve, 1)
                    return
                settle()
                drained(dve, last_key(last_step(u)))
                for w in range(norms_of(u)):
                    normalise(u, w)
                    scale_rows(u, w)
                    if norms_of(u) == 2 and w == 0:
                        settle()
                        hb = h[:, b * TT:(b + 1) * TT, :]
                        row = lambda i: rows[:, 1, i:i + 1, :].to_broadcast([P, TT, D])
                        step(dve.tensor_tensor(out=hb, in0=hb, in1=row(3), op=ALU.mult))
                        settle()
                        step(dve.tensor_tensor(out=hb, in0=hb, in1=row(4), op=ALU.add))
                        settle()

            def take(u, key):
                p, s, k = u % 2, stage_of(u), key[1]
                if k[0] == "v" and s == "attn":
                    x = int(k[1])
                    bank = ring_ready(dve, key)
                    dve.tensor_copy(v[:, p, 2 * x:2 * x + 2, :].rearrange("p t d -> p (t d)"), bank[:, :]).then_inc(ring_empty(key), 1)
                elif k[0] == "v":
                    x = int(k[1])
                    if u == 4 * B and x == 0:
                        dve.wait_ge(odd_cleared, 1)
                        dve.wait_ge(zeroed, 80)
                    bank = ring_ready(dve, key)
                    for e, dst in enumerate((v, vodd)):
                        cut = lambda y: y.rearrange("p (n two d) -> p two n d", two=2, d=HD)[:, e]
                        ins = dve.tensor_scalar(cut(dst[:, p, 2 * x:2 * x + 2, :].rearrange("p t d -> p (t d)")),
                                                cut(bank[:, :]), D ** -1.0, None, ALU.mult)
                    ins.then_inc(ring_empty(key), 1)

            def prep(u):
                for key in prep_keys(u):
                    take(u, key)

            def mask_item(u, i):
                n, w = first_item(u) + i, (items_of(u)[i][3] + 1) * P
                dve.wait_ge(s_full, n + 1)
                if stage_of(u) == "attn":
                    bank = s_bank[i % 3]
                    if n >= 4:
                        dve.wait_ge(pt_full, n - 3)
                else:
                    bank = s_bank[i % 4]
                    if u == 4 * B and i == 0:
                        filled(dve, (u - 1, "z1"))
                    dve.wait_ge(pt_full, max(n - 7, 0))
                dve.tensor_tensor_reduce(out=item_slot(u, i)[:, 0:w], in0=bank[:, 0:w], in1=causal[:, T - w:T],
                                         scale=1.0, scalar=3.0e38, op0=ALU.add, op1=ALU.min,
                                         accum_out=negmax[:, n % 16:n % 16 + 1]).then_inc(masked, 1)

            def copy_item(u, i):
                m, _, _, qt, j = items_of(u)[i]
                n, mm = first_item(u) + i, first_group(u) + m
                dve.wait_ge(pt_full, n + 1)
                if mm >= 2:
                    dve.wait_ge(av_done, mm - 1)
                dve.tensor_copy(probT[:, mm % 2, j, 0:(qt + 1) * P], pt_bank[n % 2][:, 0:(qt + 1) * P]).then_inc(pt_drained[n % 2], 1)

            def residual(u, base):
                b, p = batch_of(u), u % 2
                for x in range(2):
                    key = (u, f"z{x}")
                    bank = ring_ready(dve, key)
                    r = slice(b * TT + 2 * x, b * TT + 2 * x + 2)
                    if stage_of(u) == "attn":
                        step(dve.scalar_tensor_tensor(out=h[:, r.start, :], in0=bank[:, 0:D], scalar=rinv[:, p, 2 * x:2 * x + 1],
                                                      in1=xn[:, p, 2 * x, :], op0=ALU.mult, op1=ALU.add))
                        dve.scalar_tensor_tensor(out=h[:, r.start + 1, :], in0=bank[:, D:2 * D],
                                                 scalar=rinv[:, p, 2 * x + 1:2 * x + 2], in1=xn[:, p, 2 * x + 1, :],
                                                 op0=ALU.mult, op1=ALU.add).then_inc(ring_empty(key), 1)
                        continue
                    src = xn[:, p, 2 * x:2 * x + 2, :] if base == "xn" else h[:, r, :]
                    dve.tensor_tensor(out=h[:, r, :], in0=bank[:, :].rearrange("p (t d) -> p t d", t=2), in1=src, op=ALU.add)\
                        .then_inc(ring_empty(key), 1)
                    if stage_of(u) == "mlp":
                        if u == B:
                            dve.wait_ge(w_in["rows"], 160)
                        drained(dve, key)
                        step(dve.tensor_tensor(out=h[:, r, :], in0=h[:, r, :],
                                               in1=rows[:, layer_of(u), 0:1, :].to_broadcast([P, 2, D]), op=ALU.add))

            def first_of(dst, vals, top, width):
                t1 = ga_[:, 4, :, 0:width]
                m = small[:, 8, :]
                wide = lambda y: y.unsqueeze(2).to_broadcast([P, TT, width])
                order = first16[:, 0:width].unsqueeze(1).to_broadcast([P, TT, width])
                step(dve.tensor_tensor(out=t1, in0=vals, in1=wide(top), op=ALU.is_ge))
                settle()
                step(dve.tensor_tensor(out=t1, in0=t1, in1=order, op=ALU.mult))
                settle()
                step(dve.tensor_reduce(m, t1, AX.X, ALU.max))
                settle()
                step(dve.tensor_tensor(out=dst, in0=t1, in1=wide(m), op=ALU.is_equal))
                settle()

            def o_take(u, qt):
                dve.wait_ge(av_done, first_group(u) + qt + 1)
                dve.tensor_copy(oT[:, u % 2, :, qt * P:(qt + 1) * P], o_bank[:, 0:D].rearrange("p (c q) -> p c q", c=KD))\
                    .then_inc(o_drained, 1)

            def attention(u):
                for i in range(TT):
                    mask_item(u, i)
                prep(u + 1)
                dve.wait_ge(exped, first_item(u) + TT)
                step(dve.reciprocal(rinv[:, u % 2, :], rsum[:, u % 2, :]))
                for i in range(TT):
                    if i % 2 == 1:
                        copy_item(u, i)
                    if i:
                        o_take(u, i - 1)
                o_take(u, TT - 1)
                settle()
                residual(u, "xn")

            def divide(u, g):
                key = (u, f"r{g}")
                bank = ring_ready(dve, key)
                dve.wait_ge(o_drained, LAYERS * B * TT + KD * batch_of(u) + g + 1)
                dve.tensor_tensor(out=oT[:, u % 2, g, :], in0=bank[:, :], in1=oT[:, u % 2, g, :], op=ALU.mult)\
                    .then_inc(ring_empty(key), 1)

            def many_heads(u):
                nxt = prep_keys(u + 1)
                for i in range(2 * AHEAD):
                    mask_item(u, i)
                for k in range(PAIRS):
                    for i in range(2 * (k + AHEAD), min(2 * (k + AHEAD) + 2, 2 * PAIRS)):
                        mask_item(u, i)
                    copy_item(u, 2 * k + 1)
                    if k % 4 == 1 and nxt:
                        take(u + 1, nxt.pop(0))
                    if k in (14, 30):
                        g = k // 16
                        dve.wait_ge(exped, first_item(u) + 32 * g + 32)
                        if batch_of(u) or g:
                            dve.wait_ge(widened, KD * batch_of(u) + g)
                        dve.reciprocal(hinv[:, g, :], hsum[:, g, :]).then_inc(inverted, 1)
                    if k == 19:
                        divide(u, 0)
                divide(u, 1)
                residual(u, "h")

            def feed_forward(u):
                l = layer_of(u)
                if u == B:
                    dve.wait_ge(w_in["upb"], 16)
                for m in range(KF):
                    key = (u, f"up{m}")
                    if RING[key][1] == 1:
                        bank = ring_ready(dve, key)
                        dve.tensor_scalar(hid[:, m, :], bank[:, :], up_b[:, l, m:m + 1], 0.0, ALU.add, ALU.max)\
                            .then_inc(ring_empty(key), 1)
                prep(u + 1)
                residual(u, "xn")

            def wide(y, n):
                return y.unsqueeze(2).to_broadcast([P, TT, n])

            def top1(u):
                b, p = batch_of(u), u % 2
                if b == 0:
                    dve.wait_ge(w_in["gates"], 64)
                key = (u, "gate")
                bank = ring_ready(dve, key)
                lgt, z, ez, oh = lg[:, p, :, 0:E8], ga_[:, 0, :, 0:E8], ga_[:, 1, :, 0:E8], ga_[:, 2, :, 0:E8]
                dve.tensor_tensor(out=lgt, in0=bank[:, 0:TT * E8].rearrange("p (t e) -> p t e", e=E8),
                                  in1=gate8_b[:, :].unsqueeze(1).to_broadcast([P, TT, E8]), op=ALU.add).then_inc(ring_empty(key), 1)
                drained(dve, key)
                step(dve.tensor_reduce(small[:, 0, :], lgt, AX.X, ALU.max))
                settle()
                dve.tensor_tensor(out=z, in0=lgt, in1=wide(small[:, 0, :], E8), op=ALU.subtract).then_inc(gates, 1)
                first_of(oh, lgt, small[:, 0, :], E8)
                dve.wait_ge(gexp, b + 1)
                step(dve.tensor_reduce(small[:, 1, :], ez, AX.X, ALU.add))
                settle()
                step(dve.reciprocal(small[:, 2, :], small[:, 1, :]))
                settle()
                dve.tensor_tensor(out=mw[:, :, :], in0=oh, in1=wide(small[:, 2, :], E8), op=ALU.mult).then_inc(gmask, 1)
                prep(u + 1)
                for x in range(2):
                    key = (u, f"b{x}")
                    bank = ring_ready(dve, key)
                    r = slice(b * TT + 2 * x, b * TT + 2 * x + 2)
                    dve.tensor_tensor(out=h[:, r, :], in0=bank[:, :].rearrange("p (t d) -> p t d", t=2), in1=h[:, r, :], op=ALU.add)\
                        .then_inc(ring_empty(key), 1)
                    drained(dve, key)
                dve.wait_ge(gmask, b + 1)
                for t in range(TT):
                    for e in range(E8 // 2):
                        key = (u, f"y{t}{e}")
                        bank = ring_ready(dve, key)
                        ht = h[:, b * TT + t, :]
                        step(dve.scalar_tensor_tensor(out=ht, in0=bank[:, 0:D], scalar=mw[:, t, 2 * e:2 * e + 1], in1=ht,
                                                      op0=ALU.mult, op1=ALU.add))
                        settle()
                        dve.scalar_tensor_tensor(out=ht, in0=bank[:, D:2 * D], scalar=mw[:, t, 2 * e + 1:2 * e + 2], in1=ht,
                                                 op0=ALU.mult, op1=ALU.add).then_inc(ring_empty(key), 1)
                        drained(dve, key)

            def linear(u):
                b, p = batch_of(u), u % 2
                key = (u, "kvm")
                bank = ring_ready(dve, key)
                dve.tensor_tensor(out=kvm[:, p, :, :], in0=bank[:, 0:D].rearrange("p (c n) -> p c n", c=KD),
                                  in1=blockdiag[:, :].unsqueeze(1).to_broadcast([P, KD, P]), op=ALU.mult)\
                    .then_inc(ring_empty(key), 1)
                drained(dve, (u, "o0"))
                drained(dve, (u, "o1"))
                o, sq, gated = lin_t[:, 0], lin_t[:, 1], lin_t[:, 2]
                heads = lambda y: y.rearrange("p t (h d) -> p t h d", d=HD)
                step(dve.tensor_tensor(out=sq, in0=o, in1=o, op=ALU.mult))
                settle()
                dve.tensor_reduce(srms[:, 0, :, :], heads(sq), AX.X, ALU.add).then_inc(lin_step, 1)
                step(dve.tensor_tensor(out=gated, in0=o, in1=gate_u[:, p, :, :], op=ALU.mult))
                dve.wait_ge(lin_sd, b + 1)
                step(dve.tensor_scalar(srms[:, 2, :, :], srms[:, 1, :, :], 1e-12, None, ALU.max))
                settle()
                step(dve.reciprocal(srms[:, 0, :, :], srms[:, 2, :, :]))
                settle()
                dve.tensor_tensor(out=heads(lin_y[:, p, :, :]), in0=heads(gated),
                                  in1=srms[:, 0, :, :].unsqueeze(3).to_broadcast([P, TT, HEADS, HD]), op=ALU.mult)\
                    .then_inc(lin_out, 1)
                residual(u, "h")

            def route(u):
                b, p = batch_of(u), u % 2
                key = (u, "gate")
                bank = ring_ready(dve, key)
                lgt, rest, oh = lg[:, p, :, :], ga_[:, 0, :, :], [ga_[:, 2, :, :], ga_[:, 3, :, :]]
                dve.tensor_copy(lgt, bank[:, 0:TT * E16].rearrange("p (t e) -> p t e", e=E16)).then_inc(ring_empty(key), 1)
                drained(dve, key)
                step(dve.tensor_reduce(small[:, 0, :], lgt, AX.X, ALU.max))
                settle()
                first_of(oh[0], lgt, small[:, 0, :], E16)
                step(dve.scalar_tensor_tensor(out=rest, in0=oh[0], scalar=-FAR, in1=lgt, op0=ALU.mult, op1=ALU.add))
                settle()
                dve.tensor_reduce(small[:, 1, :], rest, AX.X, ALU.max).then_inc(gates, 1)
                dve.wait_ge(gates, B + b + 1)
                first_of(oh[1], rest, small[:, 1, :], E16)
                r = slice(b * TT, (b + 1) * TT)
                dve.tensor_tensor(out=cnt[:, r, :], in0=oh[0], in1=oh[1], op=ALU.add).then_inc(counts, 1)
                dve.wait_ge(gexp, B + b + 1)
                step(dve.tensor_scalar(small[:, 4:6, :], small[:, 2:4, :], 1.0, None, ALU.add))
                settle()
                step(dve.reciprocal(small[:, 6:8, :], small[:, 4:6, :]))
                settle()
                step(dve.tensor_tensor(out=small[:, 9, :], in0=small[:, 6, :], in1=small[:, 7, :], op=ALU.add))
                settle()
                step(dve.tensor_scalar(small[:, 10, :], small[:, 9, :], 1e-6, None, ALU.add))
                settle()
                step(dve.reciprocal(small[:, 11, :], small[:, 10, :]))
                settle()
                step(dve.tensor_tensor(out=small[:, 6:8, :], in0=small[:, 6:8, :],
                                       in1=small[:, 11:12, :].to_broadcast([P, 2, TT]), op=ALU.mult))
                key = (u, "rank")
                bank = ring_ready(dve, key)
                rk, t1 = ga_[:, 1, :, :], ga_[:, 5, :, :]
                dve.tensor_copy(rk, bank[:, 0:TT * E16].rearrange("p (t e) -> p t e", e=E16)).then_inc(ring_empty(key), 1)
                drained(dve, key)
                for k in range(TOPK):
                    rank, base, valid = small[:, 8, :], small[:, 9, :], small[:, 10, :]
                    step(dve.tensor_tensor(out=t1, in0=oh[k], in1=rk, op=ALU.mult))
                    settle()
                    step(dve.tensor_reduce(rank, t1, AX.X, ALU.add))
                    settle()
                    step(dve.tensor_tensor(out=t1, in0=oh[k], in1=base16[:, :].unsqueeze(1).to_broadcast([P, TT, E16]), op=ALU.mult))
                    settle()
                    step(dve.tensor_reduce(base, t1, AX.X, ALU.add))
                    step(dve.tensor_scalar(valid, rank, float(CAP), None, ALU.is_lt))
                    settle()
                    step(dve.tensor_tensor(out=wk[:, k, r], in0=small[:, 6 + k, :], in1=valid, op=ALU.mult))
                    step(dve.tensor_tensor(out=base, in0=base, in1=rank, op=ALU.add))
                    step(dve.tensor_scalar(small[:, 11, :], valid, -1048576.0, 1048576.0, ALU.mult, ALU.add))
                    settle()
                    dve.tensor_scalar(slot_g[:, k, r], base, float(SLOTS - 1), None, ALU.min).then_inc(slots_set, 1)
                    dve.tensor_tensor(out=slot_s[:, k, r], in0=base, in1=small[:, 11, :], op=ALU.add).then_inc(slots_set, 1)
                    dve.wait_ge(slots_set, 2 * TOPK * b + 2 * k + 2)

            bodies = {"attn": attention, "heads": many_heads, "mlp": feed_forward, "top1": top1, "linear": linear, "route": route}
            front(0)
            front(1)
            prep(0)
            for u in range(STEPS):
                bodies[stage_of(u)](u)
                front(u + 2)

            def results(j, x, begin=False):
                e = 2 * j + x
                if not begin:
                    dve.wait_ge(ye_out[x], 32 * j)
                dve.wait_ge(e_down, 2 * e + 1)
                dve.tensor_copy(ye[x][:, 0:2, :].rearrange("p t d -> p (t d)"), ring[0][:, :]).then_inc(e_y, 1)
                dve.wait_ge(e_down, 2 * e + 2)
                dve.tensor_copy(ye[x][0:CAP - 256, 2, :], ring[1][0:CAP - 256, 0:D]).then_inc(e_y, 1)

            results(0, 0, True)
            results(0, 1, True)
            with dve.Fori(1, E16 // 2) as j:
                for x in range(2):
                    results(j, x)
            for b in range(B):
                dve.wait_ge(got_in[b], 16 * TOPK * TT)
                for t in range(b * TT, (b + 1) * TT):
                    dve.scalar_tensor_tensor(out=h[:, t, :], in0=got[0][:, t, :], scalar=wk[:, 0, t:t + 1], in1=h[:, t, :],
                                             op0=ALU.mult, op1=ALU.add).then_inc(mixed0, 1)
                for t in range(b * TT, (b + 1) * TT):
                    dve.wait_ge(mixed0, t + 1)
                    dve.scalar_tensor_tensor(out=h[:, t, :], in0=got[1][:, t, :], scalar=wk[:, 1, t:t + 1], in1=h[:, t, :],
                                             op0=ALU.mult, op1=ALU.add).then_inc(mixed, 1)


def kernel(**inputs):
    import numpy as np
    import concourse.bacc as bacc
    from concourse.bass_utils import run_bass_kernel_spmd

    x = {k: np.asarray(v) for k, v in inputs.items()}
    turned = lambda w: np.ascontiguousarray(np.swapaxes(x[w], -1, -2))
    arrays = {n: x[n] for n in x if n.startswith("L0_tok_") and n not in ("L0_tok_bup",)}
    arrays["L0_ffn_expert_b"] = x["L0_ffn_expert_b"]
    arrays |= {
        "x_cols": np.ascontiguousarray(x["x"].reshape(NT, P).T),
        "bup_cols": np.ascontiguousarray(x["L0_tok_bup"].reshape(LAYERS, KF, P).transpose(2, 0, 1)),
        "heads_query": turned("L0_attn_W_query"), "heads_key": turned("L0_attn_W_key"),
        "heads_value": turned("L0_attn_W_value"), "heads_proj": turned("L0_attn_W_proj"),
        "router_t": turned("L0_ffn_router_w"), "router_b": x["L0_ffn_router_b"].reshape(1, E8),
        "top1_t": np.ascontiguousarray(x["L0_ffn_expert_w"].transpose(2, 0, 1).reshape(D, E8 * D)),
        "lin_q_t": turned("L1_attn_Wq"), "lin_o_t": turned("L1_attn_Wo"),
        "lin_kvu_t": np.concatenate([turned("L1_attn_Wk"), turned("L1_attn_Wv"), turned("L1_attn_Wu")], axis=1),
        "gate_t": turned("L1_ffn_gate_w"),
        "w1_rows": x["L1_ffn_w1"].reshape(E16 * D, DFF), "w2_rows": x["L1_ffn_w2"].reshape(E16 * DFF, D),
    }
    nc = bacc.Bacc("TRN2", target_bir_lowering=False, num_devices=1)
    a, sent = {}, {}
    for name, array in arrays.items():
        sent[f"in_{name}"] = np.ascontiguousarray(array)
        a[name] = nc.dram_tensor(f"in_{name}", array.shape, mybir.dt.from_np(array.dtype), kind="ExternalInput").ap()
    a["out"] = nc.dram_tensor("out_0_dram", (B, T, D), F32, kind="ExternalOutput").ap()
    tower_kernel(nc, a)
    got = run_bass_kernel_spmd(nc, [sent], core_ids=[0])
    return got.results[0]["out_0_dram"]
```

```python
from contextlib import ExitStack

import concourse.bass as bass
from concourse import mybir

F32 = mybir.dt.float32
FR = mybir.dt.float32r
BF16 = mybir.dt.bfloat16
I32 = mybir.dt.int32
U32 = mybir.dt.uint32
ALU = mybir.AluOpType
ACT = mybir.ActivationFunctionType
AX = mybir.AxisListType

P = 128
B, T, D = 4, 512, 256
TT = T // P
NT = B * TT
KD = D // P
VOCAB = 8000
LAYERS = 2
FF = 4 * D
KF = FF // P
HEADS, HD = 16, 16
E8 = 8
E16, TOPK, DFF = 16, 2, 512
KE = DFF // P
CAP = int(1.25 * B * T * TOPK / E16)
SLOTS = E16 * CAP
CAP_TILES = [(0, 128), (128, 128), (256, CAP - 256)]
ZEROINGS = SLOTS // 256
LAST = CAP - 256
EPS = 1e-5
MH_SCALE = -(D ** -1.0) * HD ** -0.5
FAR = 1e30

STAGES = ["attn", "mlp", "attn", "mlp", "heads", "top1", "linear", "route"]
SEQ = [(s, b) for s in range(6) for b in range(B)] + [(6, 0), (6, 1), (7, 0), (6, 2), (7, 1), (6, 3), (7, 2), (7, 3)]
STEPS = len(SEQ)
LAST_LINEAR = SEQ.index((6, B - 1))
ITEMS = {"attn": TT, "heads": HEADS * TT}


BESIDE = [u for u in range(STEPS - 1) if SEQ[u][0] == 7]


def norm_order():
    out = list(range(STEPS))
    for u in BESIDE[:-1]:
        out[u], out[u + 1] = out[u + 1], out[u]
    return out


NORM_ORDER = norm_order()


def linear_next(u):
    return u + 2 < STEPS and SEQ[u + 2][0] == 6


def stage_of(u):
    return STAGES[SEQ[u][0]]


def batch_of(u):
    return SEQ[u][1]


def layer_of(u):
    return SEQ[u][0] // 2


def last_step(u):
    return SEQ.index((SEQ[u][0] - 1, batch_of(u)))


def same_next(u):
    return u + 1 < STEPS and stage_of(u + 1) == stage_of(u)


def same_last(u):
    return u > 0 and stage_of(u - 1) == stage_of(u)


def late_turn(u):
    return layer_of(u) > 0 or not same_next(u)


def prep_keys(u):
    if u >= STEPS:
        return []
    s = stage_of(u)
    keys = ["T0", "T1"]
    if s == "attn":
        keys += ["q0", "q1", "k0", "k1", "v0", "v1"]
    if s == "heads":
        keys += [f"{n}{c}" for n in "qk" for c in range(HEADS // 4)] + ["v0", "v1"]
    if s == "linear":
        keys += ["q0", "q1"] + [f"kv{t}" for t in range(TT)] + ["g0", "g1"]
    return [(u, k) for k in keys]


def beside_keys(u):
    turned, nxt = prep_keys(u + 1), prep_keys(u + 2) if linear_next(u) else []
    return nxt[:5] + turned + nxt[5:6] + [(u + 1, "gate")] + nxt[6:]


def step_keys(u):
    s = stage_of(u)
    own = lambda *names: [(u, n) for n in names]
    nxt = prep_keys(u + 1)
    if s == "attn":
        return (own("z0") + nxt[:2] + own("z1") if late_turn(u) else nxt[:2] + own("z0", "z1")) + nxt[2:]
    if s == "heads":
        end = lambda x: [(x, n) for n in ("r1", "z0", "z1")]
        return (end(u - 1) if same_last(u) else []) + nxt[:6] + own("r0") + nxt[6:] + ([] if same_next(u) else end(u))
    if s == "mlp":
        return own(*[f"up{m}" for m in range(KF)]) + own("z0") + nxt[:2] + own("z1") + nxt[2:]
    if s == "top1":
        return own("gate") + nxt + own("mT", "b0", "b1")
    if s == "linear" and u + 1 not in BESIDE:
        return own("kvm", "o0", "o1") + nxt + own("T2", "T3", "z0", "z1")
    if s == "linear":
        late = [] if linear_next(u) else prep_keys(u + 2)
        return own("kvm", "o0", "o1") + beside_keys(u) + own("T2", "T3", "z0", "z1") + [(u + 1, "rank")] + late
    return [] if u in BESIDE else own("gate", "rank")


def ring_plan():
    plan, used, bank = {}, [0, 0], 1
    for u in range(-1, STEPS):
        for key in prep_keys(0) if u < 0 else step_keys(u):
            bank = 0 if u >= 0 and stage_of(u) == "heads" else 1 - bank
            plan[key] = (len(plan), bank, used[bank])
            used[bank] += 1
    return plan, used


RING, RING_USES = ring_plan()


BANK1_USES = next(before for order, bank, before in sorted(RING.values()) if bank and order > RING[(4 * B, "r0")][0])


def first_item(u):
    return sum(ITEMS.get(stage_of(x), 0) for x in range(u))


def groups_of(u):
    if stage_of(u) == "attn":
        return [(0, 0, qt, [0]) for qt in range(TT)]
    return [(g, e, qt, [0, 1, 2, 3]) for g in range(KD) for qt in range(TT) for e in range(2)]


def items_of(u):
    return [(i, g, e, qt, j) for i, (g, e, qt, js) in enumerate(groups_of(u)) for j in js]


def first_group(u):
    return sum(len(groups_of(x)) for x in range(u) if stage_of(x) in ITEMS)


def norms_of(u):
    return 0 if u < B else 2 if stage_of(u) == "heads" else 1


def first_norm(u):
    return sum(norms_of(x) for x in NORM_ORDER[:NORM_ORDER.index(u)])


def xn_count(u):
    return NORM_ORDER.index(u) - 3 * B + 1


Y_FIRST = 5
YS = TT * E8 // 2


def weight_chunks():
    out = []
    qkv = lambda name, l, w, last: [(name, l, kk, w, "proj", kk * w, last) for kk in range(KD)]
    for l in range(LAYERS):
        out += qkv("attn_qkv", l, 3 * D, (l * B + B - 5, "v1") if l == 0 else (B - 1, "v1"))
        last = (2 * B - 1, "up7"), (2 * B - 1, "z1")
        out += [("wup", l, kk, FF, "wide", kk * FF, last[0]) for kk in range(KD)]
        out += [("wdown", l, i, 4 * D, "wide", KD * FF + i * 4 * D, last[1]) for i in range(2)]
    out += qkv("heads_qk", None, 4 * D, (3 * B - 1, "v1"))
    out += [("heads_v", None, 0, KD * D, "values", 0, (3 * B - 1, "z1"))]
    out += [("top1_t", None, i, 4 * D, "wide", i * 4 * D, (4 * B - 1, "z1")) for i in range(4)]
    out += qkv("lin_qkvu", None, 4 * D, (5 * B - 1, "v1"))
    return out


CHUNKS = weight_chunks()
SPLIT_AFTER = {"vector": {-1: [0, 1], 0: [2, 3], 1: [4, 5]},
               "gpsimd": {4: [6, 7], 8: [8, 9], 9: [10, 11], 12: [12, 13, 14], 18: [15, 16], 19: [17, 18], 20: [19, 20]}}
BASE = 16512
LATE = 15

SPLIT_BY = {("attn", 0): 2, ("up", 0): 4, ("down", 0): 6, ("attn", 1): 8, ("up", 1): 10, ("down", 1): 12,
            "heads": 15, "top1": 19, "linear": 21}

PAIRS = HEADS * TT // 2
NORM_AT = 8
AHEAD = 3


def in_body(u):
    if stage_of(u - 1) == "attn" and same_last(u - 1) or stage_of(u - 1) == "mlp":
        return True
    return stage_of(u - 2) == "heads" or u == 4 * B + 1 or stage_of(u - 2) == stage_of(u) == "top1"


def opening(u):
    return [] if same_last(u) else range(2 * AHEAD)


def ahead_of(u, k):
    i = 2 * (k + AHEAD)
    if i < 2 * PAIRS:
        return [(u, i), (u, i + 1)]
    return [(u + 1, i - 2 * PAIRS), (u + 1, i - 2 * PAIRS + 1)] if same_next(u) else []


def tower_kernel(nc, a):
    ctx = ExitStack()
    with ctx:
        place, at = {}, [BASE]

        def sb(name, shape, dt=F32):
            size = 1
            for n in shape[1:]:
                size *= n
            place[name] = at[0]
            at[0] += -(-size * (2 if dt == BF16 else 4) // 64) * 64
            return nc.alloc_sbuf_tensor_at(name, shape, dt, offset=place[name])

        def over(name, under, shape, dt=F32, skip=0):
            return nc.alloc_sbuf_tensor_at(name, shape, dt, offset=place[under] + 4 * skip)

        def sem(name):
            return ctx.enter_context(nc.semaphore(name))

        proj_hl = sb("proj_hl", [P, 2, 4 * KD * D], FR)
        wide_hl = sb("wide_hl", [P, 2, 2 * KD * FF], FR)
        out_w = sb("out_w", [P, 4, KD, D])
        rows = sb("rows", [P, LAYERS, 5, D])
        up_b = sb("up_b", [P, LAYERS, KF])
        gate8_b = sb("gate8_b", [P, E8])
        expert_b = sb("expert_b", [E8, D])
        gates_raw = sb("gates_raw", [P, KD, E8 + E16])
        gates_hl = sb("gates_hl", [P, 2, KD, E8 + E16], FR)
        part = lambda t, c0, k, n: [t[:, y, c0:c0 + k * n].rearrange("p (k n) -> p k n", k=k) for y in range(2)]
        values_hl = over("values_hl", "out_w", [P, 2, KD * D], FR)
        v_w = part(values_hl, 0, KD, D)
        qkv_w, lin_w = part(proj_hl, 0, KD, 3 * D), part(proj_hl, 0, KD, 4 * D)
        up_w, down_w = part(wide_hl, 0, KD, FF), part(wide_hl, KD * FF, KF, D)
        top1_w = part(wide_hl, 0, KD, E8 * D)
        W1 = [part(wide_hl, x * 2048, KD, DFF) for x in range(2)]
        W2 = [part(wide_hl, x * 2048 + 1024, KE, D) for x in range(2)]
        h = sb("h", [P, NT, D])
        xn = sb("xn", [P, 2, TT, D])
        xT_hl = sb("xT_hl", [P, 2, 2, KD, T], FR)
        qk = sb("qk", [P, 2, 2, KD, T])
        spare = sb("spare", [P, 2, KD, T])
        v = sb("v", [P, 2, TT, D])
        vodd = sb("vodd", [P, 2, TT, D])
        oT = sb("oT", [P, KD, T])
        hid_hl = sb("hid_hl", [P, 2, KF, T], FR)
        mh_q = [over("mh_q0", "qk", [P, HEADS // 4, T], FR), over("mh_q1", "hid_hl", [P, HEADS // 4, T], FR, skip=(KF + KD) * T)]
        mh_hi = [over("mh_hi0", "qk", [P, HEADS // 4, T], FR, skip=4 * T), over("mh_hi1", "wide_hl", [P, HEADS // 4, T], FR, skip=2048)]
        mh_lo = [over("mh_lo0", "qk", [P, HEADS // 4, T], FR, skip=8 * T), over("mh_lo1", "wide_hl", [P, HEADS // 4, T], FR, skip=4096 + 2048)]
        prob = over("prob", "hid_hl", [P, 8, T])
        probT = sb("probT", [P, 2, 4, T])
        relu = probT[:, 0, :, :]
        pos = spare[:, :, :, :].rearrange("p a k t -> p (a k t)")[:, 0:TT * D].rearrange("p (t d) -> p t d", t=TT)
        gate_u = spare[:, :, :, :].rearrange("p a k t -> p a (k t)").rearrange("p a (t d) -> p a t d", t=TT)
        lin_k = qk[:, 1, :, :, :].rearrange("p a k t -> p a (k t)").rearrange("p a (t d) -> p a t d", t=TT)
        lin_y = vodd
        early_raw = vodd[:, :, :, :].rearrange("p a t d -> p a (t d)")
        late_raw = rows[:, :, :, :].rearrange("p l r d -> p (l r d)")[:, 0:2048].rearrange("p (a n) -> p a n", a=2)
        lin_t = over("lin_t", "hid_hl", [P, 3, TT, D])
        srms = over("srms", "hid_hl", [P, 3, TT, HEADS], skip=6 * T)
        mwT = over("mwT", "hid_hl", [E8, T], skip=7 * T)
        xf = over("xf", "hid_hl", [P, NT, D], skip=KF * T)
        got_both = over("got", "hid_hl", [P, 2, NT, D])
        got = [got_both[:, 0], got_both[:, 1]]
        flatT = probT[:, :, :, :].rearrange("p a b t -> p (a b t)")
        xe = [flatT[:, x * 768:(x + 1) * 768].rearrange("p (t d) -> p t d", t=3) for x in range(2)]
        ye = [flatT[:, 1536 + x * 768:1536 + (x + 1) * 768].rearrange("p (t d) -> p t d", t=3) for x in range(2)]
        flat_x = xT_hl[:, :, :, :, :].rearrange("p s a k t -> p s (a k t)")
        xeT = [part(flat_x, x * 640, KD, CAP) for x in range(2)]
        flat_h = hid_hl[:, :, :, :].rearrange("p s m t -> p s (m t)")
        heT = [part(flat_h, x * KE * CAP, KE, CAP) for x in range(2)]
        gelu = [t[:, :, :, :].rearrange("p a b c -> p (a b c)")[:, 0:KE * CAP].rearrange("p (m t) -> p m t", m=KE)
                for t in (spare, v)]
        flat_q = qk[:, :, :, :, :].rearrange("p a b k t -> p (a b k t)")
        raw1 = [flat_q[:, x * 1024:(x + 1) * 1024] for x in range(2)]
        raw2 = [flat_q[:, 2048 + x * 1024:2048 + (x + 1) * 1024] for x in range(2)]
        kvm = sb("kvm", [P, 2, KD, P])
        zeros = kvm[:, :, :, :].rearrange("p a k n -> p (a k n)")
        ident = sb("ident", [P, P])
        ones_f = over("ones_f", "hid_hl", [P, P], skip=T)
        blockdiag = sb("blockdiag", [P, P])
        causal = sb("causal", [P, T])
        lowrow = sb("lowrow", [P, 2])
        before = sb("before", [P, P], BF16)
        ones_b = sb("ones_b", [P, P], BF16)
        tmp_b = prob[:, 0, 0:P]
        eps_c = sb("eps_c", [P, 1])
        iota16 = sb("iota16", [P, E16])
        iota_i = sb("iota_i", [P, E16], I32)
        first16 = sb("first16", [P, E16])
        base16 = sb("base16", [P, E16])
        ids = sb("ids", [P, NT], I32)
        idf = sb("idf", [P, 2, NT])
        idu = sb("idu", [P, NT], U32)
        stats = sb("stats", [P, 2, TT, 6])
        mv = sb("mv", [P, 2, TT, 2])
        sd = sb("sd", [P, 2, TT])
        rstd = sb("rstd", [P, 2, TT])
        negmax = sb("negmax", [P, 16])
        rsum = sb("rsum", [P, 2, TT])
        rinv = sb("rinv", [P, 2, TT])
        hsum = sb("hsum", [P, 2, TT * 8])
        hinv = sb("hinv", [P, 2, TT * 8])
        hinv_wide = over("hinv_wide", "hid_hl", [P, KD, T], skip=KF * T)
        lg = causal[:, 0:2 * TT * E16].rearrange("p (x t e) -> p x t e", x=2, t=TT)
        ga_ = over("ga_", "rows", [P, 6, TT, E16], skip=2048)
        small = over("small", "rows", [P, 12, TT], skip=2048 + 6 * TT * E16 + TT * E8)
        mw = over("mw", "rows", [P, TT, E8], skip=2048 + 6 * TT * E16)
        cnt = sb("cnt", [P, NT, E16], BF16)
        total = sb("total", [P, B, E16], BF16)
        wk = sb("wk", [P, TOPK, NT])
        slot_s = sb("slot_s", [P, TOPK, NT], U32)
        slot_g = idf[:, :, :].bitcast(U32)
        assert at[0] <= nc.sbuf_usable_end, at[0]

        ring = [ctx.enter_context(nc.psum_tensor(f"ring{i}", [P, T], F32)) for i in range(2)]
        s_bank = [ctx.enter_context(nc.psum_tensor(f"s_bank{i}", [P, T], F32)) for i in range(3)] + [ring[1]]
        pt_bank = [ctx.enter_context(nc.psum_tensor(f"pt_bank{i}", [P, T], F32)) for i in range(2)]
        o_bank = ctx.enter_context(nc.psum_tensor("o_bank", [P, T], F32))

        o_pair = [o_bank, s_bank[2]]
        up_bank = [s_bank[0], s_bank[1], s_bank[2], o_bank]

        y_bank = s_bank[0:3] + pt_bank + [o_bank]
        slots_x = nc.dram_tensor("slots_x", (SLOTS, D), F32, kind="Internal").ap()
        slots_y = nc.dram_tensor("slots_y", (SLOTS, D), F32, kind="Internal").ap()

        ids_in, pos_in, id_ready, const_p, const_v = sem("ids_in"), sem("pos_in"), sem("id_ready"), sem("const_p"), sem("const_v")
        emb_in = [sem(f"emb_in{b}") for b in range(B)]
        w_in = {n: sem(f"w_{n}") for n in ("out", "rows", "upb", "gates")}
        raw_in = [sem("raw_in0"), sem("raw_in1")]
        w_hi, w_split = sem("w_hi"), sem("w_split")
        gates_split = sem("gates_split")
        mh_part = sem("mh_part")
        xT_hi = sem("xT_hi")
        hid_hi, hid_split = sem("hid_hi"), sem("hid_split")
        zeroed = sem("zeroed")
        stats_ready, sd_ready, dve_step, norm_mid = sem("stats_ready"), sem("sd_ready"), sem("dve_step"), sem("norm_mid")
        xn_dve, xn_pool = sem("xn_dve"), sem("xn_pool")
        pool_step = sem("pool_step")
        ring_full = sem("ring_full")
        ring_drained = [sem("ring_drained0"), sem("ring_drained1")]
        s_full, masked, exped, inverted, widened = sem("s_full"), sem("masked"), sem("exped"), sem("inverted"), sem("widened")
        pt_full = sem("pt_full")
        pt_drained = [sem("pt_drained0"), sem("pt_drained1")]
        av_done, o_drained = sem("av_done"), sem("o_drained")
        odd_cleared = sem("odd_cleared")
        y_full, y_taken = sem("y_full"), sem("y_taken")
        gates, gexp, gmask = sem("gates"), sem("gexp"), sem("gmask")
        lin_step, lin_sd, lin_out = sem("lin_step"), sem("lin_sd"), sem("lin_out")
        counts, totals = sem("counts"), sem("totals")
        slots_set, kept = sem("slots_set"), sem("kept")
        scattered = sem("scattered")
        w1_in, w2_in, xe_in, ye_out = ([sem(f"w1_in{i}") for i in range(2)], [sem(f"w2_in{i}") for i in range(2)],
                                       [sem(f"xe_in{i}") for i in range(2)], [sem(f"ye_out{i}") for i in range(2)])
        e_turned, e_xhi, e_xT, e_up, e_gelu, e_hhi, e_hT, e_down, e_y = (sem(n) for n in (
            "e_turned", "e_xhi", "e_xT", "e_up", "e_gelu", "e_hhi", "e_hT", "e_down", "e_y"))
        w1_hi, w1_split, w2_hi, w2_split = sem("w1_hi"), sem("w1_split"), sem("w2_hi"), sem("w2_split")
        got_in = [sem(f"got_in{i}") for i in range(NT // 2)]
        mixed, mixed0, out_sent = sem("mixed"), sem("mixed0"), sem("out_sent")

        block = ctx.enter_context(nc.Block())

        def ring_free(eng, key):
            _, bank, before_it = RING[key]
            if before_it:
                eng.wait_ge(ring_drained[bank], before_it)
            return ring[bank]

        def filled(eng, key):
            eng.wait_ge(ring_full, RING[key][0] + 1)

        def ring_ready(eng, key):
            filled(eng, key)
            return ring[RING[key][1]]

        def ring_empty(key):
            return ring_drained[RING[key][1]]

        def drained(eng, key):
            eng.wait_ge(ring_drained[RING[key][1]], RING[key][2] + 1)

        def item_slot(u, i):
            return prob[:, (first_item(u) + i) % 8, :]

        def raw_slot(c):
            return (late_raw if c >= LATE else early_raw)[:, c % 2, 0:CHUNKS[c][3]]

        def split_weights(eng, c):
            _, _, _, width, region, c0, last_use = CHUNKS[c]
            dst = {"proj": proj_hl, "wide": wide_hl, "values": values_hl}[region]
            eng.wait_ge(raw_in[c % 2], 16 * (c // 2 + 1))
            if c:
                eng.wait_ge(w_split, c)
            if c >= 6:
                filled(eng, last_use)
            if c in (17, 18):
                eng.wait_ge(s_full, first_item(5 * B))
            eng.tensor_copy(dst[:, 0, c0:c0 + width], raw_slot(c)).then_inc(w_hi, 1)
            eng.wait_ge(w_hi, c + 1)
            eng.tensor_tensor(out=dst[:, 1, c0:c0 + width], in0=raw_slot(c),
                              in1=dst[:, 0, c0:c0 + width].bitcast(F32), op=ALU.subtract).then_inc(w_split, 1)

        def split_after(eng, name, u):
            for c in SPLIT_AFTER[name].get(u, []):
                split_weights(eng, c)

        def hidden_before(u):
            return KF * sum(stage_of(x) == "mlp" for x in range(u))
        def xT_of(p, kk, cols):
            return [xT_hl[:, y, p, kk, cols] for y in range(2)]

        def both(w, kk, cols):
            return [w[y][:, kk, cols] for y in range(2)]

        def w_all(which, y, x):
            c0 = x * 2048 + (which - 1) * 1024
            return wide_hl[:, y, c0:c0 + 1024]

        def last_out(u):
            return max(x for x in range(u) if stage_of(x) in ("attn", "heads", "linear"))

        def grid(t):
            return t.rearrange("(n p) d -> p n d", p=P)

        @block.sync
        def _(sync):
            sync.dma_start(ids[:, :], a["x_cols"]).then_inc(ids_in, 16)
            sync.dma_start(pos, grid(a["L0_tok_pos"])).then_inc(pos_in, 16)

            def load_chunk(c):
                name, l, i, width, _, _, _ = CHUNKS[c]
                if c >= 2:
                    sync.wait_ge(w_split, c - 1)
                if c == LATE:
                    sync.wait_ge(xn_dve, 2 * B)
                dst = raw_slot(c)
                if name == "wdown":
                    src = a["L0_tok_wdown"][l, i * 4 * P:(i + 1) * 4 * P, :].rearrange("(m p) n -> p m n", p=P)
                    dst = dst.rearrange("p (m n) -> p m n", m=4)
                elif name == "heads_v":
                    src = a["heads_v"].rearrange("(k p) n -> p k n", p=P)
                    dst = dst.rearrange("p (k n) -> p k n", k=KD)
                elif name == "wup":
                    src = a["L0_tok_wup"][l, i * P:(i + 1) * P, :]
                elif name == "attn_qkv":
                    src = a["attn_qkv"][l, i * P:(i + 1) * P, :]
                elif name == "top1_t":
                    src = a["top1_t"][i // 2 * P:(i // 2 + 1) * P, i % 2 * width:(i % 2 + 1) * width]
                else:
                    src = a[name][i * P:(i + 1) * P, :]
                sync.dma_start(dst, src).then_inc(raw_in[c % 2], 16)

            load_chunk(0)
            load_chunk(1)
            for i, w in enumerate((a["L0_tok_wo"][0], a["L0_tok_wo"][1], a["heads_proj"], a["lin_o_t"])):
                sync.dma_start(out_w[:, i, :, :], w.rearrange("(k p) n -> p k n", p=P)).then_inc(w_in["out"], 16)
            for m in range(LAYERS):
                for i, n in enumerate(("bdown", "ga", "ba", "gm", "bm")):
                    sync.dma_start(rows[:, m, i, :], a[f"L0_tok_{n}"][m:m + 1, :].to_broadcast([P, D]))\
                        .then_inc(w_in["rows"], 16)
            sync.dma_start(up_b[:, :, :], a["bup_cols"]).then_inc(w_in["upb"], 16)
            sync.dma_start(gates_raw[:, :, :], a["gates_t"].rearrange("(k p) n -> p k n", p=P)).then_inc(w_in["gates"], 16)
            sync.dma_start(gate8_b[:, :], a["router_b"].to_broadcast([P, E8])).then_inc(w_in["gates"], 16)
            sync.dma_start(expert_b[:, :], a["L0_ffn_expert_b"]).then_inc(w_in["gates"], 16)
            for c in range(2, 6):
                load_chunk(c)
            sync.wait_ge(const_p, 1)
            for i in range(ZEROINGS):
                sync.dma_start(slots_x[i * 256:(i + 1) * 256, :].rearrange("(p r) d -> p (r d)", p=P), zeros)\
                    .then_inc(zeroed, 16)
            for c in range(6, len(CHUNKS)):
                load_chunk(c)

            def weights1(e, x):
                sync.dma_start(raw1[x].rearrange("p (k f) -> p k f", k=KD),
                               a["w1_rows"][bass.ds(e * D, D), :].rearrange("(k p) f -> p k f", p=P)).then_inc(w1_in[x], 16)

            def weights2(e, x):
                sync.dma_start(raw2[x].rearrange("p (m d) -> p m d", m=KE),
                               a["w2_rows"][bass.ds(e * DFF, DFF), :].rearrange("(m p) d -> p m d", p=P)).then_inc(w2_in[x], 16)

            def tokens(e, x):
                src = slots_x[bass.ds(e * CAP, CAP), :]
                sync.dma_start(xe[x][:, 0:2, :], src[0:256, :].rearrange("(t p) d -> p t d", p=P)).then_inc(xe_in[x], 16)
                sync.dma_start(xe[x][0:LAST, 2, :], src[256:CAP, :]).then_inc(xe_in[x], 16)

            def results(e, x):
                dst = slots_y[bass.ds(e * CAP, CAP), :]
                sync.wait_ge(e_y, 2 * e + 2)
                sync.dma_start(dst[0:256, :].rearrange("(t p) d -> p t d", p=P), ye[x][:, 0:2, :]).then_inc(ye_out[x], 16)
                sync.dma_start(dst[256:CAP, :], ye[x][P - LAST:P, 2, :]).then_inc(ye_out[x], 16)

            def around(e, x, w1=True, w2=True, out=True):
                if w1:
                    sync.wait_ge(w1_split, e + 3)
                    weights1(e + 4, x)
                if w2:
                    sync.wait_ge(e_turned, 2 * e + 4)
                    tokens(e + 3, 1 - x)
                if out:
                    results(e - 1, 1 - x)
                if w2:
                    sync.wait_ge(w2_split, e + 2)
                    weights2(e + 3, 1 - x)

            filled(sync, (LAST_LINEAR, "o1"))
            for e in range(2):
                weights1(e, e)
                weights2(e, e)
            sync.wait_ge(scattered, 16 * TOPK * NT)
            for e in range(2):
                tokens(e, e)
            for e in range(2):
                sync.wait_ge(w1_split, e + 1)
                weights1(e + 2, e)
            sync.wait_ge(e_turned, 2)
            tokens(2, 0)
            sync.wait_ge(w2_split, 1)
            weights2(2, 0)
            around(0, 0, out=False)
            around(1, 1)
            with sync.Fori(1, E16 // 2 - 2) as j:
                for x in range(2):
                    around(2 * j + x, x)
            around(12, 0, w1=False)
            for e in range(13, 17):
                around(e, e % 2, w1=False, w2=False)
            out_v = a["out"].rearrange("b (t p) d -> b p t d", p=P)
            for i in range(NT // 2):
                sync.wait_ge(mixed, 2 * (i + 1))
                b, t = 2 * i // TT, 2 * i % TT
                sync.dma_start(out_v[b][:, t:t + 2, :], h[:, 2 * i:2 * i + 2, :]).then_inc(out_sent, 16)
            sync.wait_ge(out_sent, 16 * (NT // 2))

        @block.gpsimd
        def _(pool):
            done = {}

            def step(ins):
                ins.then_inc(pool_step, 1)
                done["n"] = done.get("n", 0) + 1

            def settle():
                pool.wait_ge(pool_step, done["n"])

            pool.memset(zeros, 0.0).then_inc(const_p, 1)
            step(pool.memset(ident[:, :], 0.0))
            step(pool.memset(ones_f[:, :], 1.0))
            step(pool.memset(causal[:, :], 0.0))
            step(pool.memset(ones_b[:, :], 1.0))
            step(pool.iota(iota_i[:, :], pattern=[[1, E16]], base=0, channel_multiplier=0))
            settle()
            step(pool.affine_select(out=ident[:, :], in_=ident[:, :], compare_op=ALU.not_equal, fill=1.0, base=0,
                                    pattern=[[-1, P]], channel_multiplier=1))
            step(pool.affine_select(out=causal[:, T - P:T], in_=causal[:, T - P:T], compare_op=ALU.is_ge, fill=FAR, base=0,
                                    pattern=[[-1, P]], channel_multiplier=1))
            step(pool.affine_select(out=tmp_b, in_=ones_f[:, :], compare_op=ALU.is_gt, fill=0.0, base=0,
                                    pattern=[[1, P]], channel_multiplier=-1))
            step(pool.affine_select(out=blockdiag[:, :], in_=ones_f[:, :], compare_op=ALU.is_ge, fill=0.0, base=0,
                                    pattern=[[-HD, P // HD], [0, HD]], channel_multiplier=1))
            step(pool.tensor_copy(iota16[:, :], iota_i[:, :]))
            settle()
            step(pool.affine_select(out=blockdiag[:, :], in_=blockdiag[:, :], compare_op=ALU.is_ge, fill=0.0, base=HD - 1,
                                    pattern=[[HD, P // HD], [0, HD]], channel_multiplier=-1))
            settle()
            pool.tensor_copy(before[:, :], tmp_b).then_inc(const_p, 1)

            pool.wait_ge(id_ready, 4)
            for t in range(NT):
                pool.indirect_dma_start(out=h[:, t, :], out_offset=None, in_=a["L0_tok_emb"],
                                        in_offset=bass.IndirectOffsetOnAxis(ap=idu[:, t:t + 1], axis=0))\
                    .then_inc(emb_in[t // TT], 16)

            def affine(u):
                p = u % 2
                l, r = ((u // B - 1) // 2, 1 if u // B % 2 == 1 else 3)
                if u == B:
                    pool.wait_ge(w_in["rows"], 160)
                pool.wait_ge(norm_mid, u - B + 1)
                row = lambda i: rows[:, l, i:i + 1, :].to_broadcast([P, TT, D])
                step(pool.tensor_tensor(out=xn[:, p, :, :], in0=xn[:, p, :, :], in1=row(r), op=ALU.mult))
                settle()
                pool.tensor_tensor(out=xn[:, p, :, :], in0=xn[:, p, :, :], in1=row(r + 1), op=ALU.add).then_inc(xn_pool, 1)

            for u in range(STEPS):
                if stage_of(u) == "heads":
                    for g in range(KD):
                        pool.wait_ge(inverted, KD * batch_of(u) + g + 1)
                        pool.tensor_copy(hinv_wide[:, g, :].rearrange("p (x d) -> p x d", d=HD),
                                         hinv[:, g, :].unsqueeze(2).to_broadcast([P, TT * 8, HD])).then_inc(widened, 1)
                if u == 3 * B + 1:
                    pool.wait_ge(av_done, first_group(4 * B))
                    pool.wait_ge(w_split, LATE)
                    pool.memset(v[:, :, :, :], 0.0).then_inc(odd_cleared, 1)
                    pool.memset(vodd[:, :, :, :], 0.0).then_inc(odd_cleared, 1)
                if B <= u + 2 < 4 * B:
                    affine(u + 2)
                split_after(pool, "gpsimd", u)
                if stage_of(u) == "route":
                    b = batch_of(u)
                    filled(pool, (5 * B - 1, "z1"))
                    for x in [u] if u < STEPS - 2 else [u, u + 1] if u == STEPS - 2 else []:
                        pool.wait_ge(xn_dve, xn_count(x))
                        y = batch_of(x)
                        pool.tensor_copy(xf[:, y * TT:(y + 1) * TT, :], xn[:, x % 2, :, :]).then_inc(kept, 1)
                    pool.wait_ge(kept, b + 1)
                    if b == 0:
                        pool.wait_ge(zeroed, 16 * ZEROINGS)
                    for k in range(TOPK):
                        pool.wait_ge(slots_set, 2 * TOPK * b + 2 * k + 2)
                        for t in range(b * TT, (b + 1) * TT):
                            pool.indirect_dma_start(out=slots_x,
                                                    out_offset=bass.IndirectOffsetOnAxis(ap=slot_s[:, k, t:t + 1], axis=0),
                                                    in_=xf[:, t, :], in_offset=None,
                                                    bounds_check=SLOTS - 1, oob_is_err=False).then_inc(scattered, 16)
            def low(e, x, w1=True, w2=True):
                if w1:
                    pool.wait_ge(w1_hi, e + 3)
                    pool.tensor_tensor(out=w_all(1, 1, x), in0=raw1[x], in1=w_all(1, 0, x).bitcast(F32), op=ALU.subtract)\
                        .then_inc(w1_split, 1)
                if w2:
                    pool.wait_ge(w2_hi, e + 2)
                    pool.tensor_tensor(out=w_all(2, 1, 1 - x), in0=raw2[1 - x], in1=w_all(2, 0, 1 - x).bitcast(F32),
                                       op=ALU.subtract).then_inc(w2_split, 1)

            low(-2, 0, w2=False)
            low(-1, 1)
            with pool.Fori(0, E16 // 2 - 1) as j:
                for x in range(2):
                    low(2 * j + x, x)
            low(E16 - 2, 0, w1=False)
            for x in range(2):
                pool.wait_ge(ye_out[x], 16 * E16)
            pool.wait_ge(scattered, 16 * TOPK * NT)
            for b in range(B):
                for t in range(b * TT, (b + 1) * TT):
                    for k in range(TOPK):
                        pool.indirect_dma_start(out=got[k][:, t, :], out_offset=None, in_=slots_y,
                                                in_offset=bass.IndirectOffsetOnAxis(ap=slot_g[:, k, t:t + 1], axis=0))\
                            .then_inc(got_in[t // 2], 16)

        @block.tensor
        def _(pe):
            def mm(out, lhsT, rhs, start, stop, **kw):
                return pe.matmul(out, lhsT, rhs, start=start, stop=stop, **kw)

            def chain(out, pairs):
                for i, (l, r) in enumerate(pairs):
                    ins = mm(out, l, r, i == 0, i == len(pairs) - 1)
                return ins

            def split_chain(out, pairs):
                for i, (l, r) in enumerate(pairs):
                    for y, z in ((0, 0), (0, 1), (1, 0)):
                        ins = mm(out, l[y], r[z], i == 0 and y + z == 0, i == len(pairs) - 1 and y == 1)
                return ins

            def project(u, key):
                p, s, l = u % 2, stage_of(u), layer_of(u)
                k = key[1]
                bank = ring_free(pe, key)
                if k[0] == "T":
                    c = int(k[1])
                    if c == 0:
                        if B <= u < 4 * B:
                            pe.wait_ge(xn_pool, u - B + 1)
                        else:
                            pe.wait_ge(xn_dve, u + 1 if u < B else xn_count(u))
                    for t in range(TT):
                        ins = pe.transpose(bank[:, t * P:(t + 1) * P], xn[:, p, t, c * P:(c + 1) * P], ident[:, :])
                    ins.then_inc(ring_full, 1)
                    return
                if k == "q0":
                    drained(pe, (u, "T0"))
                    drained(pe, (u, "T1"))
                    if batch_of(u) == 0:
                        pe.wait_ge(w_split, SPLIT_BY[("attn", l) if s == "attn" else s])
                w = lin_w if s == "linear" else qkv_w
                if s == "heads" and k[0] in "qk":
                    c0 = "qk".index(k[0]) * 2 * D + int(k[1]) * P
                    split_chain(bank[:, :], [(both(lin_w, kk, slice(c0, c0 + P)), xT_of(p, kk, slice(0, T)))
                                             for kk in range(KD)]).then_inc(ring_full, 1)
                elif k[0] in "qk" and k[1] != "v":
                    c0 = "qk".index(k[0]) * D + int(k[1]) * P
                    split_chain(bank[:, :], [(both(w, kk, slice(c0, c0 + P)), xT_of(p, kk, slice(0, T))) for kk in range(KD)])\
                        .then_inc(ring_full, 1)
                elif k[:2] == "kv":
                    t = int(k[2])
                    split_chain(bank[:, :], [(xT_of(p, kk, slice(t * P, (t + 1) * P)), both(w, kk, slice(D, 3 * D)))
                                             for kk in range(KD)]).then_inc(ring_full, 1)
                else:
                    if s == "heads":
                        w = v_w
                    c0 = 0 if s == "heads" else 2 * D if k[0] == "v" else 3 * D
                    for t in range(2):
                        tt = 2 * int(k[1]) + t
                        ins = split_chain(bank[:, t * D:(t + 1) * D],
                                          [(xT_of(p, kk, slice(tt * P, (tt + 1) * P)), both(w, kk, slice(c0, c0 + D)))
                                           for kk in range(KD)])
                    ins.then_inc(ring_full, 1)

            def prep(u):
                for key in prep_keys(u):
                    project(u, key)

            def scores(u, i):
                _, g, e, qt, j = items_of(u)[i]
                n0, p, w = first_item(u), u % 2, (qt + 1) * P
                if stage_of(u) == "attn":
                    if n0 + i >= 2:
                        pe.wait_ge(masked, n0 + max(i - 1, 0))
                    ins = chain(s_bank[i % 2][:, 0:w], [(qk[:, 0, p, kk, qt * P:w], qk[:, 1, p, kk, 0:w]) for kk in range(KD)])
                else:
                    pe.wait_ge(masked, n0 + max(i // 2 * 2 - 2, 0))
                    if i == 3 and not same_last(u):
                        pe.wait_ge(ring_drained[1], BANK1_USES)
                    r0, c = 32 * (2 * (j % 2) + e), 2 * g + j // 2
                    for y, keys in enumerate((mh_hi[p], mh_lo[p])):
                        ins = mm(s_bank[i % 4][:, 0:w], mh_q[p][r0:r0 + 32, c, qt * P:w], keys[r0:r0 + 32, c, 0:w],
                                 y == 0, y == 1, tile_position=(r0, 0))
                ins.then_inc(s_full, 1)

            def turn(u, i):
                qt, n = items_of(u)[i][3], first_item(u) + i
                pe.wait_ge(exped, n + 1)
                if n >= 2:
                    pe.wait_ge(pt_drained[n % 2], n // 2)
                for kt in range(qt + 1):
                    ins = pe.transpose(pt_bank[n % 2][:, kt * P:(kt + 1) * P], item_slot(u, i)[:, kt * P:(kt + 1) * P], ident[:, :])
                ins.then_inc(pt_full, 1)

            def weigh(u, i, o_use):
                p, m = u % 2, first_group(u) + i
                g, e, qt, js = groups_of(u)[i]
                last_n = first_item(u) + (i + 1) * len(js) - 1
                for x in range(2):
                    if last_n >= x:
                        pe.wait_ge(pt_drained[x], (last_n - x) // 2 + 1)
                if stage_of(u) == "attn" and o_use > 1:
                    pe.wait_ge(o_drained, o_use - 1)
                elif stage_of(u) == "heads" and qt == 0 and e == 0:
                    pe.wait_ge(o_drained, o_use)
                if stage_of(u) == "attn":
                    for c in range(KD):
                        for kt in range(qt + 1):
                            ins = mm(o_pair[qt % 2][:, c * P:(c + 1) * P], v[:, p, kt, c * P:(c + 1) * P],
                                     probT[:, m % 2, 0, kt * P:(kt + 1) * P], kt == 0, kt == qt)
                else:
                    vals = vodd if e else v
                    for kt in range(qt + 1):
                        for j in range(4):
                            c0 = g * P + 32 * j
                            ins = mm(o_bank[32 * j:32 * j + 32, qt * P:(qt + 1) * P], vals[:, p, kt, c0:c0 + 32],
                                     probT[:, m % 2, j, kt * P:(kt + 1) * P], e == 0 and kt == 0, e == 1 and kt == qt,
                                     tile_position=(0, 32 * j))
                ins.then_inc(av_done, 1)

            def widths(u, g):
                bank = ring_free(pe, (u, f"r{g}"))
                pe.wait_ge(widened, KD * batch_of(u) + g + 1)
                for qt in range(TT):
                    ins = pe.transpose(bank[:, qt * P:(qt + 1) * P], hinv_wide[:, g, qt * P:(qt + 1) * P], ident[:, :])
                ins.then_inc(ring_full, 1)

            def out_half(u, w, x):
                bank = ring_free(pe, (u, f"z{x}"))
                for t in range(2):
                    tt = 2 * x + t
                    ins = chain(bank[:, t * D:(t + 1) * D], [(oT[:, c, tt * P:(tt + 1) * P], w[:, c, :]) for c in range(KD)])
                ins.then_inc(ring_full, 1)

            def oT_stands(u):
                drained(pe, (u, "r0"))
                drained(pe, (u, "r1"))

            def out_proj(u, w):
                for x in range(2):
                    out_half(u, w, x)

            def linear_products(u):
                p = u % 2
                for k in ("q0", "q1", "kv0", "kv1", "kv2", "kv3", "g0", "g1"):
                    drained(pe, (u, k))
                bank = ring_free(pe, (u, "kvm"))
                for c in range(KD):
                    ins = chain(bank[:, c * P:(c + 1) * P],
                                [(lin_k[:, p, t, c * P:(c + 1) * P], v[:, p, t, c * P:(c + 1) * P]) for t in range(TT)])
                ins.then_inc(ring_full, 1)
                drained(pe, (u, "kvm"))
                for x in range(2):
                    bank = ring_free(pe, (u, f"o{x}"))
                    for t in range(2):
                        tt = 2 * x + t
                        for c in range(KD):
                            ins = mm(bank[:, t * D + c * P:t * D + (c + 1) * P], qk[:, 0, p, c, tt * P:(tt + 1) * P],
                                     kvm[:, p, c, :], True, True)
                    ins.then_inc(ring_full, 1)

            def linear_out(u):
                for c in range(KD):
                    bank = ring_free(pe, (u, f"T{2 + c}"))
                    pe.wait_ge(lin_out, batch_of(u) + 1)
                    for t in range(TT):
                        ins = pe.transpose(bank[:, t * P:(t + 1) * P], lin_y[:, u % 2, t, c * P:(c + 1) * P], ident[:, :])
                    ins.then_inc(ring_full, 1)
                drained(pe, (u, "T2"))
                drained(pe, (u, "T3"))
                out_proj(u, out_w[:, 3])

            def route_gate(u):
                drained(pe, (u, "T0"))
                drained(pe, (u, "T1"))
                bank = ring_free(pe, (u, "gate"))
                for t in range(TT):
                    ins = split_chain(bank[:, t * E16:(t + 1) * E16],
                                      [(xT_of(u % 2, kk, slice(t * P, (t + 1) * P)),
                                        [gates_hl[:, y, kk, slice(E8, E8 + E16)] for y in range(2)]) for kk in range(KD)])
                ins.then_inc(ring_full, 1)

            def route_ranks(u):
                bank = ring_free(pe, (u, "rank"))
                b = batch_of(u)
                pe.wait_ge(counts, b + 1)
                if b:
                    pe.wait_ge(totals, b)
                for t in range(TT):
                    tt = b * TT + t
                    ins = chain(bank[:, t * E16:(t + 1) * E16],
                                [(before[:, :], cnt[:, tt, :])] + [(ones_b[:, :], cnt[:, y, :]) for y in range(b * TT, tt)]
                                + ([(ones_b[:, :], total[:, b, :])] if b else []))
                ins.then_inc(ring_full, 1)

            o_uses = 0
            pe.wait_ge(const_p, 2)
            prep(0)
            for u in range(STEPS):
                s, p, l = stage_of(u), u % 2, layer_of(u)
                n0, m0 = first_item(u), first_group(u)
                if s == "attn":
                    if not same_last(u):
                        for key in prep_keys(u)[2:]:
                            drained(pe, key)
                        for i in range(TT):
                            scores(u, i)
                    else:
                        drained(pe, (u, "v0"))
                        drained(pe, (u, "v1"))
                    for i in range(TT):
                        turn(u, i)
                        if i:
                            weigh(u, i - 1, o_uses)
                            o_uses += 1
                    turned_keys = prep_keys(u + 1)[:2]
                    for key in [] if late_turn(u) else turned_keys:
                        project(u + 1, key)
                    weigh(u, TT - 1, o_uses)
                    o_uses += 1
                    pe.wait_ge(o_drained, o_uses)
                    if u == 0:
                        pe.wait_ge(w_in["out"], 64)
                    out_half(u, out_w[:, l], 0)
                    for key in turned_keys if late_turn(u) else []:
                        project(u + 1, key)
                    out_half(u, out_w[:, l], 1)
                    for key in prep_keys(u + 1)[2:]:
                        if key[1] == "v1":
                            for k in ("q0", "q1", "k0", "k1"):
                                drained(pe, (u + 1, k))
                            for i in range(TT):
                                scores(u + 1, i)
                        project(u + 1, key)
                elif s == "heads":
                    if not same_last(u):
                        for key in prep_keys(u)[2:]:
                            drained(pe, key)
                    else:
                        drained(pe, (u, "v0"))
                        drained(pe, (u, "v1"))
                    nxt = prep_keys(u + 1)
                    if not same_last(u):
                        pe.wait_ge(o_drained, o_uses)
                    for i in opening(u):
                        scores(u, i)
                    for k in range(PAIRS):
                        for x, i in ahead_of(u, k):
                            if x > u and i == 0:
                                for key in prep_keys(x)[2:-2]:
                                    drained(pe, key)
                            scores(x, i)
                        turn(u, 2 * k)
                        turn(u, 2 * k + 1)
                        if k >= 3 and k % 2 == 1:
                            weigh(u, (k - 3) // 2, o_uses)
                            if (k - 3) // 2 == 7:
                                o_uses += 1
                        if same_last(u):
                            if k == 1:
                                weigh(u - 1, PAIRS // 2 - 1, o_uses)
                                o_uses += 1
                            if k == 2:
                                widths(u - 1, 1)
                            if k == 4:
                                oT_stands(u - 1)
                            if k in (4, 6):
                                out_half(u - 1, out_w[:, 2], k // 2 - 2)
                        if k >= 7 and k % 2 == 1 and nxt:
                            project(u + 1, nxt.pop(0))
                        if k == 18:
                            widths(u, 0)
                    if not same_next(u):
                        weigh(u, PAIRS // 2 - 1, o_uses)
                        o_uses += 1
                        widths(u, 1)
                        oT_stands(u)
                        pe.wait_ge(masked, n0 + 2 * PAIRS)
                        out_proj(u, out_w[:, 2])
                elif s == "mlp":
                    drained(pe, (u, "T0"))
                    drained(pe, (u, "T1"))
                    if batch_of(u) == 0:
                        pe.wait_ge(w_split, SPLIT_BY["up", l])
                    for m in range(KF):
                        bank = ring_free(pe, (u, f"up{m}"))
                        split_chain(bank[:, :], [(both(up_w, kk, slice(m * P, (m + 1) * P)), xT_of(p, kk, slice(0, T)))
                                                 for kk in range(KD)])\
                            .then_inc(ring_full, 1)
                    if batch_of(u) == 0:
                        pe.wait_ge(w_split, SPLIT_BY["down", l])
                    for x in range(2):
                        bank = ring_free(pe, (u, f"z{x}"))
                        for t in range(2):
                            tt = 2 * x + t
                            for m in range(KF):
                                if tt == 0:
                                    pe.wait_ge(hid_split, hidden_before(u) + m + 1)
                                for y, z in ((0, 0), (0, 1), (1, 0)):
                                    ins = mm(bank[:, t * D:(t + 1) * D], hid_hl[:, y, m, tt * P:(tt + 1) * P], down_w[z][:, m, :],
                                             m == 0 and y + z == 0, m == KF - 1 and y == 1)
                        ins.then_inc(ring_full, 1)
                        for key in prep_keys(u + 1)[2:] if x else prep_keys(u + 1)[:2]:
                            project(u + 1, key)
                elif s == "top1":
                    drained(pe, (u, "T0"))
                    drained(pe, (u, "T1"))
                    if batch_of(u) == 0:
                        pe.wait_ge(w_in["gates"], 48)
                        pe.wait_ge(gates_split, 2)
                    bank = ring_free(pe, (u, "gate"))
                    for t in range(TT):
                        ins = split_chain(bank[:, t * E8:(t + 1) * E8],
                                          [(xT_of(p, kk, slice(t * P, (t + 1) * P)),
                                            [gates_hl[:, y, kk, slice(0, E8)] for y in range(2)]) for kk in range(KD)])
                    ins.then_inc(ring_full, 1)
                    if not same_last(u):
                        pe.wait_ge(masked, n0)
                        for x in range(2):
                            pe.wait_ge(pt_drained[x], n0 // 2)
                        pe.wait_ge(o_drained, o_uses)

                    def expert_pair(i):
                        t, e, n = i // (E8 // 2), i % (E8 // 2), YS * batch_of(u) + i
                        if n >= len(y_bank):
                            pe.wait_ge(y_taken, n - len(y_bank) + 1)
                        split_chain(y_bank[n % len(y_bank)][:, :],
                                    [(xT_of(p, kk, slice(t * P, (t + 1) * P)), both(top1_w, kk, slice(e * 2 * D, (e + 1) * 2 * D)))
                                     for kk in range(KD)]).then_inc(y_full, 1)

                    y_first = Y_FIRST if same_last(u) else 0
                    for i in range(y_first):
                        expert_pair(i)
                    prep(u + 1)
                    bank = ring_free(pe, (u, "mT"))
                    pe.wait_ge(gmask, batch_of(u) + 1)
                    for t in range(TT):
                        ins = pe.transpose(bank[0:E8, t * P:(t + 1) * P], mw[:, t, :], ident[:, :])
                    ins.then_inc(ring_full, 1)
                    drained(pe, (u, "mT"))
                    for x in range(2):
                        bank = ring_free(pe, (u, f"b{x}"))
                        for t in range(2):
                            tt = 2 * x + t
                            ins = mm(bank[:, t * D:(t + 1) * D], mwT[:, tt * P:(tt + 1) * P], expert_b[:, :], True, True)
                        ins.then_inc(ring_full, 1)
                    if not same_last(u):
                        pe.wait_ge(w_split, SPLIT_BY["top1"])
                    for i in range(y_first, YS):
                        expert_pair(i)
                elif s == "linear":
                    linear_products(u)
                    if u + 1 not in BESIDE:
                        prep(u + 1)
                    else:
                        for key in beside_keys(u):
                            if key[1] == "gate":
                                route_gate(u + 1)
                            else:
                                project(key[0], key)
                    linear_out(u)
                    if u + 1 in BESIDE:
                        route_ranks(u + 1)
                        if not linear_next(u):
                            prep(u + 2)
                elif u not in BESIDE:
                    route_gate(u)
                    route_ranks(u)
            for i in range(2):
                pe.wait_ge(ring_drained[i], RING_USES[i])
            pe.wait_ge(y_taken, YS * B)

            def turn_rows(e, x, m, begin=False):
                pe.wait_ge(xe_in[x], 32 * m + 32)
                for c in range(KD):
                    if not begin:
                        pe.wait_ge(e_xT, 2 * e - 1 + c)
                    for i, (t0, w) in enumerate(CAP_TILES):
                        ins = pe.transpose(pt_bank[c][:, t0:t0 + w], xe[x][0:w, i, c * P:(c + 1) * P], ident[0:w, 0:w])
                    ins.then_inc(e_turned, 1)

            def first(e, x, begin=False):
                pe.wait_ge(w1_split, e + 1)
                pe.wait_ge(e_xT, 2 * e + 2)
                for m in range(KE):
                    if not begin:
                        pe.wait_ge(e_gelu, KE * e - KE + m + 1)
                    split_chain(up_bank[m][:, 0:CAP], [(both(W1[x], kk, slice(m * P, (m + 1) * P)), both(xeT[x], kk, slice(0, CAP)))
                                                       for kk in range(KD)]).then_inc(e_up, 1)

            def second(e, x, begin=False):
                pe.wait_ge(w2_split, e + 1)
                pe.wait_ge(e_hT, KE * e + KE)
                for i, t0 in enumerate((0, P, CAP - P)):
                    bank = ring[i // 2]
                    if not begin and i != 1:
                        pe.wait_ge(e_y, 2 * e - 1 + i // 2)
                    ins = split_chain(bank[:, (i % 2) * D:(i % 2 + 1) * D],
                                      [(both(heT[x], m, slice(t0, t0 + P)), both(W2[x], m, slice(0, D))) for m in range(KE)])
                    if i:
                        ins.then_inc(e_down, 1)

            turn_rows(0, 0, 0, True)
            first(0, 0, True)
            turn_rows(1, 1, 0)
            first(1, 1)
            turn_rows(2, 0, 1)
            second(0, 0, True)
            with pe.Fori(1, E16 // 2 - 1) as j:
                for x in range(2):
                    e = 2 * j + x
                    first(e, x)
                    turn_rows(e + 1, 1 - x, j + x)
                    second(e - 1, 1 - x)
            first(E16 - 2, 0)
            turn_rows(E16 - 1, 1, E16 // 2 - 1)
            second(E16 - 3, 1)
            first(E16 - 1, 1)
            second(E16 - 2, 0)
            second(E16 - 1, 1)

        @block.scalar
        def _(act):
            def turned(u, dst, key):
                bank = ring_ready(act, key)
                act.activation(dst, bank[:, :], ACT.Copy).then_inc(ring_empty(key), 1)

            def root(u, w):
                n = first_norm(u) + w
                act.wait_ge(stats_ready, n + 1)
                act.activation(sd[:, n % 2, :], mv[:, n % 2, :, 1], ACT.Sqrt, bias=eps_c[:, 0:1]).then_inc(sd_ready, 1)

            def take(u, key):
                p, s, k = u % 2, stage_of(u), key[1]
                if k[0] == "T":
                    bank = ring_ready(act, key)
                    act.activation(xT_hl[:, 0, p, int(k[1]), :], bank[:, :], ACT.Copy).then_inc(xT_hi, 1)
                elif s == "heads" and k[0] in "qk":
                    c = int(k[1])
                    bank = ring_ready(act, key)
                    if k[0] == "q":
                        act.activation(mh_q[p][:, c, :], bank[:, :], ACT.Copy).then_inc(mh_part, 1)
                    else:
                        act.activation(mh_hi[p][:, c, :], bank[:, :], ACT.Copy, scale=MH_SCALE).then_inc(mh_part, 1)
                elif k[0] == "q":
                    bank = ring_ready(act, key)
                    dst = qk[:, 0, p, int(k[1]), :]
                    if s == "linear":
                        act.activation(dst, bank[:, :], ACT.Relu, scale=HD ** -0.5).then_inc(ring_empty(key), 1)
                    else:
                        act.activation(dst, bank[:, :], ACT.Copy, scale=-D ** -0.5).then_inc(ring_empty(key), 1)
                elif k in ("k0", "k1"):
                    bank = ring_ready(act, key)
                    c = int(k[1])
                    act.activation(qk[:, 1, p, c, :], bank[:, :], ACT.Copy).then_inc(ring_empty(key), 1)
                elif k[:2] == "kv":
                    t = int(k[2])
                    bank = ring_ready(act, key)
                    act.activation(lin_k[:, p, t, :], bank[:, 0:D], ACT.Relu, scale=HD ** -0.5)
                    act.activation(v[:, p, t, :], bank[:, D:2 * D], ACT.Copy).then_inc(ring_empty(key), 1)
                elif k[0] == "g":
                    x = int(k[1])
                    bank = ring_ready(act, key)
                    act.activation(gate_u[:, p, 2 * x:2 * x + 2, :].rearrange("p t d -> p (t d)"), bank[:, :], ACT.Silu)\
                        .then_inc(ring_empty(key), 1)

            def prep(u):
                for key in prep_keys(u):
                    take(u, key)

            def exp_item(u, i):
                _, g, e, qt, j = items_of(u)[i]
                n, w = first_item(u) + i, (qt + 1) * P
                total = rsum[:, u % 2, qt:qt + 1] if stage_of(u) == "attn" else hsum[:, g, qt * 8 + 2 * j + e:qt * 8 + 2 * j + e + 1]
                act.wait_ge(masked, n + 1)
                act.activation(item_slot(u, i)[:, 0:w], item_slot(u, i)[:, 0:w], ACT.Exp, scale=-1.0,
                               bias=negmax[:, n % 16:n % 16 + 1], accum_out=total).then_inc(exped, 1)

            def copy_item(u, i):
                m, _, _, qt, j = items_of(u)[i]
                n, mm = first_item(u) + i, first_group(u) + m
                if i == 0 and hidden_before(u):
                    act.wait_ge(hid_split, hidden_before(u))
                act.wait_ge(pt_full, n + 1)
                if mm >= 2:
                    act.wait_ge(av_done, mm - 1)
                act.activation(probT[:, mm % 2, j, 0:(qt + 1) * P], pt_bank[n % 2][:, 0:(qt + 1) * P], ACT.Copy)\
                    .then_inc(pt_drained[n % 2], 1)

            def o_take(u, g):
                act.wait_ge(av_done, first_group(u) + 8 * g + 8)
                filled(act, (last_out(u), "z1"))
                act.activation(oT[:, g, :], o_bank[:, :], ACT.Copy).then_inc(o_drained, 1)

            def choice_exp(u):
                act.wait_ge(gates, B + batch_of(u) + 1)
                act.activation(small[:, 2:4, :], small[:, 0:2, :], ACT.Exp, scale=-1.0).then_inc(gexp, 1)

            act.wait_ge(const_v, 2)
            act.activation(negmax[:, 15:16], eps_c[:, 0:1], ACT.Copy)
            prep(0)
            for u in range(STEPS):
                s, p, l = stage_of(u), u % 2, layer_of(u)
                n0 = first_item(u)
                if s == "attn":
                    if not same_last(u):
                        for i in range(TT):
                            exp_item(u, i)
                    copy_item(u, 0)
                    if same_last(u):
                        for w in range(norms_of(u + 1)):
                            root(u + 1, w)
                    copy_item(u, 2)
                    prep(u + 1)
                    if same_next(u):
                        for i in range(TT):
                            exp_item(u + 1, i)
                elif s == "heads":
                    nxt = prep_keys(u + 1)
                    for i in opening(u):
                        exp_item(u, i)
                    for k in range(PAIRS):
                        copy_item(u, 2 * k)
                        for x, i in ahead_of(u, k):
                            exp_item(x, i)
                        if k == 2 and same_last(u):
                            o_take(u - 1, 1)
                        if k >= 7 and k % 2 == 1 and nxt:
                            take(u + 1, nxt.pop(0))
                        if not same_last(u) and k in (0, 4):
                            root(u + 1, k // 4)
                        if k == NORM_AT + 1:
                            root(u + 2, 0)
                        if k == NORM_AT + 9 and norms_of(u + 2) == 2:
                            root(u + 2, 1)
                        if k == 18:
                            o_take(u, 0)
                    if not same_next(u):
                        o_take(u, 1)
                elif s == "mlp":
                    if u == B:
                        act.wait_ge(w_in["upb"], 16)
                    for m in range(KF):
                        key = (u, f"up{m}")
                        n = hidden_before(u) + m
                        if m == 0:
                            act.wait_ge(av_done, first_group(u))
                        if n >= 4:
                            act.wait_ge(hid_split, n - 3)
                        bank = ring_ready(act, key)
                        act.activation(relu[:, m % 4, :], bank[:, :], ACT.Relu, bias=up_b[:, l, m:m + 1]).then_inc(ring_empty(key), 1)
                        if m == 1 and in_body(u + 1):
                            root(u + 1, norms_of(u + 1) - 1)
                        if m == 5 and u == 4 * B - 2:
                            root(u + 2, 0)
                    prep(u + 1)
                elif s == "top1":
                    act.wait_ge(gates, batch_of(u) + 1)
                    act.activation(ga_[:, 1, :, 0:E8], ga_[:, 0, :, 0:E8], ACT.Exp).then_inc(gexp, 1)
                    prep(u + 1)
                    key = (u, "mT")
                    bank = ring_ready(act, key)
                    act.activation(mwT[:, :], bank[0:E8, :], ACT.Copy).then_inc(ring_empty(key), 1)
                elif s == "linear":
                    beside = u + 1 in BESIDE
                    if beside:
                        root(u + 1, 0)
                    for x in range(2):
                        key = (u, f"o{x}")
                        bank = ring_ready(act, key)
                        act.activation(lin_t[:, 0, 2 * x:2 * x + 2, :].rearrange("p t d -> p (t d)"), bank[:, :], ACT.Copy)\
                            .then_inc(ring_empty(key), 1)
                    for key in prep_keys(u + 1)[:4] if not beside else (beside_keys(u) if linear_next(u) else prep_keys(u + 1))[:4]:
                        take(key[0], key)
                    act.wait_ge(lin_step, batch_of(u) + 1)
                    act.activation(srms[:, 1, :, :], srms[:, 0, :, :], ACT.Sqrt, scale=1.0 / HD).then_inc(lin_sd, 1)
                    if not beside:
                        for key in prep_keys(u + 1)[4:]:
                            take(u + 1, key)
                    elif linear_next(u):
                        for key in beside_keys(u)[4:]:
                            if key[1] == "g0":
                                act.wait_ge(lin_out, batch_of(u) + 1)
                            if key[1] != "gate":
                                take(key[0], key)
                        choice_exp(u + 1)
                        if linear_next(u + 2):
                            root(u + 4, 0)
                    else:
                        choice_exp(u + 1)
                    filled(act, (last_out(u), "z1"))
                    for c in range(KD):
                        turned(u, oT[:, c, :], (u, f"T{2 + c}"))
                    if u == 6 * B:
                        root(u + 3, 0)
                    if beside and not linear_next(u):
                        root(u + 2, 0)
                        prep(u + 2)
                elif u not in BESIDE:
                    choice_exp(u)
                if s == "top1" and u + 2 < STEPS or s in ("attn", "mlp") and not in_body(u + 2):
                    for w in range(norms_of(u + 2)):
                        root(u + 2, w)

            def high_rows(e, x):
                for c in range(KD):
                    act.wait_ge(e_turned, 2 * e + c + 1)
                    act.activation(xeT[x][0][:, c, :], pt_bank[c][:, 0:CAP], ACT.Copy).then_inc(e_xhi, 1)

            def high1(x, m):
                act.wait_ge(w1_in[x], 16 * m + 16)
                act.activation(w_all(1, 0, x), raw1[x], ACT.Copy).then_inc(w1_hi, 1)

            def high2(x, m):
                act.wait_ge(w2_in[x], 16 * m + 16)
                act.activation(w_all(2, 0, x), raw2[x], ACT.Copy).then_inc(w2_hi, 1)

            def beside(e, x, m, rows_=True, w1=True, w2=True):
                for i in range(KE):
                    act.wait_ge(e_up, KE * e + i + 1)
                    act.activation(gelu[x][:, i, :], up_bank[i][:, 0:CAP], ACT.Gelu).then_inc(e_gelu, 1)
                if rows_:
                    high_rows(e + 1, 1 - x)
                if w1:
                    high1(x, m + 1)
                if w2:
                    if w2 != "begin":
                        act.wait_ge(e_down, 2 * e)
                    high2(1 - x, m + x)

            act.wait_ge(y_full, YS * B)
            high1(0, 0)
            high2(0, 0)
            high1(1, 0)
            high_rows(0, 0)
            beside(0, 0, 0, w2="begin")
            beside(1, 1, 0)
            with act.Fori(1, E16 // 2 - 1) as j:
                for x in range(2):
                    beside(2 * j + x, x, j)
            beside(E16 - 2, 0, E16 // 2 - 1, w1=False)
            beside(E16 - 1, 1, E16 // 2 - 1, rows_=False, w1=False, w2=False)

        @block.vector
        def _(dve):
            steps = [0]

            def step(ins):
                ins.then_inc(dve_step, 1)
                steps[0] += 1

            def settle():
                dve.wait_ge(dve_step, steps[0])

            dve.wait_ge(ids_in, 16)
            dve.tensor_scalar(idf[:, 0, :], ids[:, :], 0.0, float(VOCAB), ALU.is_lt, ALU.mult).then_inc(id_ready, 1)
            dve.wait_ge(id_ready, 1)
            dve.tensor_tensor(out=idf[:, 1, :], in0=ids[:, :], in1=idf[:, 0, :], op=ALU.add).then_inc(id_ready, 1)
            dve.wait_ge(id_ready, 2)
            dve.tensor_scalar(idf[:, 0, :], idf[:, 1, :], 0.0, float(VOCAB - 1), ALU.max, ALU.min).then_inc(id_ready, 1)
            dve.wait_ge(id_ready, 3)
            dve.tensor_copy(idu[:, :], idf[:, 0, :]).then_inc(id_ready, 1)
            dve.memset(eps_c[:, :], EPS).then_inc(const_v, 1)
            dve.wait_ge(const_p, 2)
            dve.wait_ge(const_v, 1)
            step(dve.tensor_scalar(first16[:, :], iota16[:, :], -1.0, float(E16), ALU.mult, ALU.add))
            step(dve.tensor_scalar(base16[:, :], iota16[:, :], float(CAP), None, ALU.mult))
            bd = blockdiag[:, :].rearrange("p (n two d) -> p two n d", two=2, d=HD)
            step(dve.tensor_reduce(lowrow[:, 1:2], bd[:, 1, :, 0:1], AX.XY, ALU.add))
            settle()
            dve.tensor_scalar(lowrow[:, 0:1], lowrow[:, 1:2], -1.0, None, ALU.mult).then_inc(const_v, 1)

            def normalise(u, w):
                n, b, p = first_norm(u) + w, batch_of(u), u % 2
                into_h = norms_of(u) == 2 and w == 0
                for t in range(TT):
                    step(dve.bn_stats(stats[:, n % 2, t, :], h[:, b * TT + t, :]))
                settle()
                for t in range(TT):
                    ins = dve.bn_aggr(mv[:, n % 2, t, :], stats[:, n % 2, t, :])
                    if t < TT - 1:
                        step(ins)
                    else:
                        ins.then_inc(stats_ready, 1)
                return n

            def scale_rows(u, w):
                n, b, p = first_norm(u) + w, batch_of(u), u % 2
                into_h = norms_of(u) == 2 and w == 0
                dve.wait_ge(sd_ready, n + 1)
                step(dve.reciprocal(rstd[:, n % 2, :], sd[:, n % 2, :]))
                settle()
                for t in range(TT):
                    dst = h[:, b * TT + t, :] if into_h else xn[:, p, t, :]
                    ins = dve.tensor_scalar(dst, h[:, b * TT + t, :], mv[:, n % 2, t, 0:1], rstd[:, n % 2, t:t + 1],
                                            ALU.subtract, ALU.mult)
                    if t < TT - 1 or into_h:
                        step(ins)
                    elif u < 4 * B:
                        ins.then_inc(norm_mid, 1)
                    else:
                        ins.then_inc(xn_dve, 1)

            def xn_free(u):
                if u >= 2:
                    filled(dve, (u - 2, "T1"))
                    if stage_of(u - 2) == "route":
                        dve.wait_ge(kept, batch_of(u - 2) + 1)
                    elif stage_of(u - 2) in ("attn", "mlp"):
                        drained(dve, (u - 2, "z1"))
                if u >= B:
                    settle()
                    if stage_of(last_step(u)) == "top1":
                        dve.wait_ge(y_taken, YS * (batch_of(u) + 1))
                    else:
                        drained(dve, (last_step(u), "z1"))

            def norm_part(u, n):
                hb = h[:, batch_of(u) * TT:(batch_of(u) + 1) * TT, :]
                row = lambda i: rows[:, 1, i:i + 1, :].to_broadcast([P, TT, D])
                if n == 4 * norms_of(u) - 4:
                    xn_free(u)
                elif n == 0:
                    drained(dve, (last_step(u), "z1"))
                if n % 4 == 0:
                    settle()
                    normalise(u, n // 4)
                elif n % 4 == 1:
                    scale_rows(u, n // 4)
                else:
                    settle()
                    step(dve.tensor_tensor(out=hb, in0=hb, in1=row(n + 1), op=ALU.mult if n == 2 else ALU.add))

            def front(u):
                if u >= STEPS:
                    return
                if u < B:
                    b, p = batch_of(u), u % 2
                    xn_free(u)
                    dve.wait_ge(emb_in[b], 16 * TT)
                    if u == 0:
                        dve.wait_ge(pos_in, 16)
                    dve.tensor_tensor(out=xn[:, p, :, :], in0=h[:, b * TT:(b + 1) * TT, :], in1=pos, op=ALU.add).then_inc(xn_dve, 1)
                    return
                for n in range(4 * norms_of(u) - 2):
                    norm_part(u, n)

            def take(u, key):
                p, s, k = u % 2, stage_of(u), key[1]
                if k[0] == "T":
                    c = int(k[1])
                    dve.wait_ge(xT_hi, KD * NORM_ORDER.index(u) + c + 1)
                    bank = ring_ready(dve, key)
                    dve.tensor_tensor(out=xT_hl[:, 1, p, c, :], in0=bank[:, :], in1=xT_hl[:, 0, p, c, :].bitcast(F32),
                                      op=ALU.subtract).then_inc(ring_empty(key), 1)
                elif s == "heads" and k[0] in "qk":
                    c = int(k[1])
                    dve.wait_ge(mh_part, HEADS // 2 * batch_of(u) + HEADS // 4 * "qk".index(k[0]) + c + 1)
                    bank = ring_ready(dve, key)
                    if k[0] == "q":
                        dve.scalar_tensor_tensor(out=mh_q[p][:, c, :], in0=mh_q[p][:, c, :].bitcast(F32), scalar=lowrow[:, 0:1],
                                                 in1=bank[:, :], op0=ALU.mult, op1=ALU.add).then_inc(ring_empty(key), 1)
                    else:
                        dve.scalar_tensor_tensor(out=mh_lo[p][:, c, :], in0=bank[:, :], scalar=MH_SCALE,
                                                 in1=mh_hi[p][:, c, :].bitcast(F32), op0=ALU.mult, op1=ALU.subtract)\
                            .then_inc(ring_empty(key), 1)
                elif k[0] == "v" and s == "attn":
                    x = int(k[1])
                    bank = ring_ready(dve, key)
                    dve.tensor_copy(v[:, p, 2 * x:2 * x + 2, :].rearrange("p t d -> p (t d)"), bank[:, :]).then_inc(ring_empty(key), 1)
                elif k[0] == "v":
                    x = int(k[1])
                    if u == 4 * B and x == 0:
                        dve.wait_ge(odd_cleared, 2)
                    bank = ring_ready(dve, key)
                    for e, dst in enumerate((v, vodd)):
                        cut = lambda y: y.rearrange("p (n two d) -> p two n d", two=2, d=HD)[:, e]
                        ins = dve.tensor_scalar(cut(dst[:, p, 2 * x:2 * x + 2, :].rearrange("p t d -> p (t d)")),
                                                cut(bank[:, :]), D ** -1.0, None, ALU.mult)
                    ins.then_inc(ring_empty(key), 1)

            def prep(u):
                for key in prep_keys(u):
                    take(u, key)

            def mask_item(u, i):
                n, w = first_item(u) + i, (items_of(u)[i][3] + 1) * P
                dve.wait_ge(s_full, n + 1)
                if i == 0 and hidden_before(u):
                    filled(dve, (2 * B * (1 + (u >= 4 * B)) - 1, "z1"))
                    dve.wait_ge(hid_split, hidden_before(u))
                if stage_of(u) == "attn":
                    bank = s_bank[i % 2]
                    if n >= 8:
                        dve.wait_ge(pt_full, n - 7)
                else:
                    bank = s_bank[i % 4]
                    dve.wait_ge(pt_full, max(n - 7, 0))
                dve.tensor_tensor_reduce(out=item_slot(u, i)[:, 0:w], in0=bank[:, 0:w], in1=causal[:, T - w:T],
                                         scale=1.0, scalar=3.0e38, op0=ALU.add, op1=ALU.min,
                                         accum_out=negmax[:, n % 16:n % 16 + 1]).then_inc(masked, 1)

            def copy_item(u, i):
                m, _, _, qt, j = items_of(u)[i]
                n, mm = first_item(u) + i, first_group(u) + m
                dve.wait_ge(pt_full, n + 1)
                if mm >= 2:
                    dve.wait_ge(av_done, mm - 1)
                dve.tensor_copy(probT[:, mm % 2, j, 0:(qt + 1) * P], pt_bank[n % 2][:, 0:(qt + 1) * P]).then_inc(pt_drained[n % 2], 1)

            def residual(u, base, parts=(0, 1)):
                b, p = batch_of(u), u % 2
                for x in parts:
                    key = (u, f"z{x}")
                    bank = ring_ready(dve, key)
                    r = slice(b * TT + 2 * x, b * TT + 2 * x + 2)
                    if stage_of(u) == "attn":
                        step(dve.scalar_tensor_tensor(out=h[:, r.start, :], in0=bank[:, 0:D], scalar=rinv[:, p, 2 * x:2 * x + 1],
                                                      in1=xn[:, p, 2 * x, :], op0=ALU.mult, op1=ALU.add))
                        dve.scalar_tensor_tensor(out=h[:, r.start + 1, :], in0=bank[:, D:2 * D],
                                                 scalar=rinv[:, p, 2 * x + 1:2 * x + 2], in1=xn[:, p, 2 * x + 1, :],
                                                 op0=ALU.mult, op1=ALU.add).then_inc(ring_empty(key), 1)
                        continue
                    src = xn[:, p, 2 * x:2 * x + 2, :] if base == "xn" else h[:, r, :]
                    dve.tensor_tensor(out=h[:, r, :], in0=bank[:, :].rearrange("p (t d) -> p t d", t=2), in1=src, op=ALU.add)\
                        .then_inc(ring_empty(key), 1)
                    if stage_of(u) == "mlp":
                        if u == B:
                            dve.wait_ge(w_in["rows"], 160)
                        drained(dve, key)
                        step(dve.tensor_tensor(out=h[:, r, :], in0=h[:, r, :],
                                               in1=rows[:, layer_of(u), 0:1, :].to_broadcast([P, 2, D]), op=ALU.add))

            def first_of(dst, vals, top, width):
                t1 = ga_[:, 4, :, 0:width]
                m = small[:, 8, :]
                wide = lambda y: y.unsqueeze(2).to_broadcast([P, TT, width])
                order = first16[:, 0:width].unsqueeze(1).to_broadcast([P, TT, width])
                step(dve.tensor_tensor(out=t1, in0=vals, in1=wide(top), op=ALU.is_ge))
                settle()
                step(dve.tensor_tensor(out=t1, in0=t1, in1=order, op=ALU.mult))
                settle()
                step(dve.tensor_reduce(m, t1, AX.X, ALU.max))
                settle()
                step(dve.tensor_tensor(out=dst, in0=t1, in1=wide(m), op=ALU.is_equal))
                settle()

            def o_take(u, qt):
                dve.wait_ge(av_done, first_group(u) + qt + 1)
                dve.tensor_copy(oT[:, :, qt * P:(qt + 1) * P], 
                                o_pair[qt % 2][:, 0:D].rearrange("p (c q) -> p c q", c=KD))\
                    .then_inc(o_drained, 1)

            def attention(u):
                if not same_last(u):
                    for i in range(TT):
                        mask_item(u, i)
                dve.wait_ge(exped, first_item(u) + TT)
                step(dve.reciprocal(rinv[:, u % 2, :], rsum[:, u % 2, :]))
                copy_item(u, 1)
                if same_last(u) and norms_of(u + 1):
                    norm_part(u + 1, 0)
                o_take(u, 0)
                if same_last(u):
                    if norms_of(u + 1):
                        norm_part(u + 1, 1)
                    else:
                        front(u + 1)
                o_take(u, 1)
                copy_item(u, 3)
                o_take(u, 2)
                turned_keys = prep_keys(u + 1)[:2]
                for key in [] if late_turn(u) else turned_keys:
                    take(u + 1, key)
                o_take(u, 3)
                settle()
                residual(u, "xn", [0])
                for key in turned_keys if late_turn(u) else []:
                    take(u + 1, key)
                residual(u, "xn", [1])
                for key in prep_keys(u + 1)[2:]:
                    if key[1] == "v1":
                        for i in range(TT):
                            mask_item(u + 1, i)
                    take(u + 1, key)

            def divide(u, g):
                key = (u, f"r{g}")
                bank = ring_ready(dve, key)
                dve.wait_ge(o_drained, LAYERS * B * TT + KD * batch_of(u) + g + 1)
                dve.tensor_tensor(out=oT[:, g, :], in0=bank[:, :], in1=oT[:, g, :], op=ALU.mult)\
                    .then_inc(ring_empty(key), 1)

            def many_heads(u):
                nxt = prep_keys(u + 1)
                for i in opening(u):
                    mask_item(u, i)
                for k in range(PAIRS):
                    for x, i in ahead_of(u, k):
                        mask_item(x, i)
                    copy_item(u, 2 * k + 1)
                    if same_last(u):
                        if k == 3:
                            divide(u - 1, 1)
                        if k in (5, 7):
                            residual(u - 1, "h", [k // 2 - 2])
                    if k == 19:
                        divide(u, 0)
                    if k >= 7 and k % 2 == 1 and nxt:
                        take(u + 1, nxt.pop(0))
                    if not same_last(u) and k < 6:
                        norm_part(u + 1, k)
                    if k >= NORM_AT and k % 2 == NORM_AT % 2 and (k - NORM_AT) // 2 < 4 * norms_of(u + 2) - 2:
                        norm_part(u + 2, (k - NORM_AT) // 2)
                    if k in (14, 30):
                        g = k // 16
                        dve.wait_ge(exped, first_item(u) + 32 * g + 32)
                        if batch_of(u) or g:
                            dve.wait_ge(widened, KD * batch_of(u) + g)
                        dve.reciprocal(hinv[:, g, :], hsum[:, g, :]).then_inc(inverted, 1)
                if not same_next(u):
                    divide(u, 1)
                    residual(u, "h")

            def feed_forward(u):
                n = hidden_before(u)

                def low(m):
                    dve.wait_ge(hid_hi, n + m + 1)
                    dve.tensor_tensor(out=hid_hl[:, 1, m, :], in0=relu[:, m % 4, :], in1=hid_hl[:, 0, m, :].bitcast(F32),
                                      op=ALU.subtract).then_inc(hid_split, 1)

                last_norm = 4 * norms_of(u + 1) - 4
                if in_body(u + 1):
                    norm_part(u + 1, last_norm)
                dve.wait_ge(pt_full, first_item(u))
                for m in range(KF):
                    drained(dve, (u, f"up{m}"))
                    dve.tensor_copy(hid_hl[:, 0, m, :], relu[:, m % 4, :]).then_inc(hid_hi, 1)
                    if m:
                        low(m - 1)
                    if m == 2 and in_body(u + 1):
                        norm_part(u + 1, last_norm + 1)
                    if m in (4, 6) and u == 4 * B - 2:
                        norm_part(u + 2, m // 2 - 2)
                low(KF - 1)
                if u == 4 * B - 2:
                    norm_part(u + 2, 2)
                    norm_part(u + 2, 3)
                residual(u, "xn", [0])
                for key in prep_keys(u + 1)[:2]:
                    take(u + 1, key)
                residual(u, "xn", [1])
                for key in prep_keys(u + 1)[2:]:
                    take(u + 1, key)

            def wide(y, n):
                return y.unsqueeze(2).to_broadcast([P, TT, n])

            def top1(u):
                b, p = batch_of(u), u % 2
                if b == 0:
                    dve.wait_ge(w_in["gates"], 48)
                key = (u, "gate")
                bank = ring_ready(dve, key)
                lgt, z, ez, oh = lg[:, p, :, 0:E8], ga_[:, 0, :, 0:E8], ga_[:, 1, :, 0:E8], ga_[:, 2, :, 0:E8]
                dve.tensor_tensor(out=lgt, in0=bank[:, 0:TT * E8].rearrange("p (t e) -> p t e", e=E8),
                                  in1=gate8_b[:, :].unsqueeze(1).to_broadcast([P, TT, E8]), op=ALU.add).then_inc(ring_empty(key), 1)
                drained(dve, key)
                step(dve.tensor_reduce(small[:, 0, :], lgt, AX.X, ALU.max))
                settle()
                dve.tensor_tensor(out=z, in0=lgt, in1=wide(small[:, 0, :], E8), op=ALU.subtract).then_inc(gates, 1)
                first_of(oh, lgt, small[:, 0, :], E8)
                dve.wait_ge(gexp, b + 1)
                step(dve.tensor_reduce(small[:, 1, :], ez, AX.X, ALU.add))
                settle()
                step(dve.reciprocal(small[:, 2, :], small[:, 1, :]))
                settle()
                dve.tensor_tensor(out=mw[:, :, :], in0=oh, in1=wide(small[:, 2, :], E8), op=ALU.mult).then_inc(gmask, 1)
                prep(u + 1)
                for x in range(2):
                    key = (u, f"b{x}")
                    bank = ring_ready(dve, key)
                    r = slice(b * TT + 2 * x, b * TT + 2 * x + 2)
                    dve.tensor_tensor(out=h[:, r, :], in0=bank[:, :].rearrange("p (t d) -> p t d", t=2), in1=h[:, r, :], op=ALU.add)\
                        .then_inc(ring_empty(key), 1)
                    drained(dve, key)
                dve.wait_ge(gmask, b + 1)
                for i in range(YS):
                    t, e, n = i // (E8 // 2), i % (E8 // 2), YS * b + i
                    dve.wait_ge(y_full, n + 1)
                    bank = y_bank[n % len(y_bank)]
                    ht = h[:, b * TT + t, :]
                    step(dve.scalar_tensor_tensor(out=ht, in0=bank[:, 0:D], scalar=mw[:, t, 2 * e:2 * e + 1], in1=ht,
                                                  op0=ALU.mult, op1=ALU.add))
                    settle()
                    dve.scalar_tensor_tensor(out=ht, in0=bank[:, D:2 * D], scalar=mw[:, t, 2 * e + 1:2 * e + 2], in1=ht,
                                             op0=ALU.mult, op1=ALU.add).then_inc(y_taken, 1)
                    dve.wait_ge(y_taken, n + 1)
                    if i in (YS // 2, 3 * YS // 4) and stage_of(u + 2) == "top1":
                        norm_part(u + 2, 4 * i // YS - 2)

            def linear(u):
                b, p = batch_of(u), u % 2
                beside = u + 1 in BESIDE
                key = (u, "kvm")
                bank = ring_ready(dve, key)
                if b == 0:
                    dve.wait_ge(zeroed, 16 * ZEROINGS)
                dve.tensor_tensor(out=kvm[:, p, :, :], in0=bank[:, 0:D].rearrange("p (c n) -> p c n", c=KD),
                                  in1=blockdiag[:, :].unsqueeze(1).to_broadcast([P, KD, P]), op=ALU.mult)\
                    .then_inc(ring_empty(key), 1)
                if beside:
                    front(u + 1)
                    if linear_next(u):
                        for key in prep_keys(u + 2)[:2]:
                            take(u + 2, key)
                else:
                    prep(u + 1)
                drained(dve, (u, "o0"))
                drained(dve, (u, "o1"))
                o, sq, gated = lin_t[:, 0], lin_t[:, 1], lin_t[:, 2]
                heads = lambda y: y.rearrange("p t (h d) -> p t h d", d=HD)
                step(dve.tensor_tensor(out=sq, in0=o, in1=o, op=ALU.mult))
                settle()
                dve.tensor_reduce(srms[:, 0, :, :], heads(sq), AX.X, ALU.add).then_inc(lin_step, 1)
                if beside:
                    prep(u + 1)
                step(dve.tensor_tensor(out=gated, in0=o, in1=gate_u[:, p, :, :], op=ALU.mult))
                dve.wait_ge(lin_sd, b + 1)
                step(dve.tensor_scalar(srms[:, 2, :, :], srms[:, 1, :, :], 1e-12, None, ALU.max))
                settle()
                step(dve.reciprocal(srms[:, 0, :, :], srms[:, 2, :, :]))
                settle()
                dve.tensor_tensor(out=heads(lin_y[:, p, :, :]), in0=heads(gated),
                                  in1=srms[:, 0, :, :].unsqueeze(3).to_broadcast([P, TT, HEADS, HD]), op=ALU.mult)\
                    .then_inc(lin_out, 1)
                if not beside:
                    residual(u, "h")
                    front(u + 3)
                    return
                gate_out(u + 1)
                if u - 1 in BESIDE:
                    route_slots(u - 1)
                route_choice(u + 1)
                if linear_next(u) and linear_next(u + 2):
                    front(u + 4)
                residual(u, "h")
                ranks_out(u + 1)
                if not linear_next(u):
                    front(u + 2)
                    prep(u + 2)
                    route_slots(u + 1)

            def gate_out(u):
                key = (u, "gate")
                bank = ring_ready(dve, key)
                dve.tensor_copy(lg[:, u % 2, :, :], bank[:, 0:TT * E16].rearrange("p (t e) -> p t e", e=E16))\
                    .then_inc(ring_empty(key), 1)

            def route_choice(u):
                b, p = batch_of(u), u % 2
                lgt, rest, oh = lg[:, p, :, :], ga_[:, 0, :, :], [ga_[:, 2, :, :], ga_[:, 3, :, :]]
                drained(dve, (u, "gate"))
                step(dve.tensor_reduce(small[:, 0, :], lgt, AX.X, ALU.max))
                settle()
                first_of(oh[0], lgt, small[:, 0, :], E16)
                step(dve.scalar_tensor_tensor(out=rest, in0=oh[0], scalar=-FAR, in1=lgt, op0=ALU.mult, op1=ALU.add))
                settle()
                dve.tensor_reduce(small[:, 1, :], rest, AX.X, ALU.max).then_inc(gates, 1)
                dve.wait_ge(gates, B + b + 1)
                first_of(oh[1], rest, small[:, 1, :], E16)
                r = slice(b * TT, (b + 1) * TT)
                dve.tensor_tensor(out=cnt[:, r, :], in0=oh[0], in1=oh[1], op=ALU.add).then_inc(counts, 1)
                if b < B - 1:
                    mine = ga_[:, 5, 0, :]
                    dve.wait_ge(counts, b + 1)
                    step(dve.tensor_reduce(mine, cnt[:, r, :].rearrange("p t e -> p e t"), AX.X, ALU.add))
                    settle()
                    if b:
                        dve.wait_ge(totals, b)
                        dve.tensor_tensor(out=total[:, b + 1, :], in0=total[:, b, :], in1=mine, op=ALU.add).then_inc(totals, 1)
                    else:
                        dve.tensor_copy(total[:, b + 1, :], mine).then_inc(totals, 1)
                dve.wait_ge(gexp, B + b + 1)
                step(dve.tensor_scalar(small[:, 4:6, :], small[:, 2:4, :], 1.0, None, ALU.add))
                settle()
                step(dve.reciprocal(small[:, 6:8, :], small[:, 4:6, :]))
                settle()
                step(dve.tensor_tensor(out=small[:, 9, :], in0=small[:, 6, :], in1=small[:, 7, :], op=ALU.add))
                settle()
                step(dve.tensor_scalar(small[:, 10, :], small[:, 9, :], 1e-6, None, ALU.add))
                settle()
                step(dve.reciprocal(small[:, 11, :], small[:, 10, :]))
                settle()
                step(dve.tensor_tensor(out=small[:, 6:8, :], in0=small[:, 6:8, :],
                                       in1=small[:, 11:12, :].to_broadcast([P, 2, TT]), op=ALU.mult))

            def ranks_out(u):
                key = (u, "rank")
                bank = ring_ready(dve, key)
                dve.tensor_copy(ga_[:, 1, :, :], bank[:, 0:TT * E16].rearrange("p (t e) -> p t e", e=E16))\
                    .then_inc(ring_empty(key), 1)

            def route_slots(u):
                b = batch_of(u)
                r = slice(b * TT, (b + 1) * TT)
                rk, t1, oh = ga_[:, 1, :, :], ga_[:, 5, :, :], [ga_[:, 2, :, :], ga_[:, 3, :, :]]
                settle()
                drained(dve, (u, "rank"))
                for k in range(TOPK):
                    rank, base, valid = small[:, 8, :], small[:, 9, :], small[:, 10, :]
                    step(dve.tensor_tensor(out=t1, in0=oh[k], in1=rk, op=ALU.mult))
                    settle()
                    step(dve.tensor_reduce(rank, t1, AX.X, ALU.add))
                    settle()
                    step(dve.tensor_tensor(out=t1, in0=oh[k], in1=base16[:, :].unsqueeze(1).to_broadcast([P, TT, E16]), op=ALU.mult))
                    settle()
                    step(dve.tensor_reduce(base, t1, AX.X, ALU.add))
                    step(dve.tensor_scalar(valid, rank, float(CAP), None, ALU.is_lt))
                    settle()
                    step(dve.tensor_tensor(out=wk[:, k, r], in0=small[:, 6 + k, :], in1=valid, op=ALU.mult))
                    step(dve.tensor_tensor(out=base, in0=base, in1=rank, op=ALU.add))
                    step(dve.tensor_scalar(small[:, 11, :], valid, -1048576.0, 1048576.0, ALU.mult, ALU.add))
                    settle()
                    dve.tensor_scalar(slot_g[:, k, r], base, float(SLOTS - 1), None, ALU.min).then_inc(slots_set, 1)
                    dve.tensor_tensor(out=slot_s[:, k, r], in0=base, in1=small[:, 11, :], op=ALU.add).then_inc(slots_set, 1)
                    dve.wait_ge(slots_set, 2 * TOPK * b + 2 * k + 2)

            def route(u):
                if u not in BESIDE:
                    gate_out(u)
                    route_choice(u)
                    ranks_out(u)
                    route_slots(u)

            bodies = {"attn": attention, "heads": many_heads, "mlp": feed_forward, "top1": top1, "linear": linear, "route": route}
            split_after(dve, "vector", -1)
            front(0)
            prep(0)
            front(1)
            for u in range(STEPS):
                bodies[stage_of(u)](u)
                if stage_of(u) not in ("linear", "route") and not in_body(u + 2):
                    front(u + 2)
                split_after(dve, "vector", u)
                if u == 1:
                    dve.wait_ge(w_in["gates"], 48)
                    dve.tensor_copy(gates_hl[:, 0, :, :], gates_raw[:, :, :]).then_inc(gates_split, 1)
                    dve.wait_ge(gates_split, 1)
                    dve.tensor_tensor(out=gates_hl[:, 1, :, :], in0=gates_raw[:, :, :], in1=gates_hl[:, 0, :, :].bitcast(F32),
                                      op=ALU.subtract).then_inc(gates_split, 1)

            def low_rows(e, x):
                for c in range(KD):
                    dve.wait_ge(e_xhi, 2 * e + c + 1)
                    dve.tensor_tensor(out=xeT[x][1][:, c, :], in0=pt_bank[c][:, 0:CAP], in1=xeT[x][0][:, c, :].bitcast(F32),
                                      op=ALU.subtract).then_inc(e_xT, 1)

            def split_hidden(e, x):
                def low(m):
                    dve.wait_ge(e_hhi, KE * e + m + 1)
                    dve.tensor_tensor(out=heT[x][1][:, m, :], in0=gelu[x][:, m, :], in1=heT[x][0][:, m, :].bitcast(F32),
                                      op=ALU.subtract).then_inc(e_hT, 1)

                for m in range(KE):
                    dve.wait_ge(e_gelu, KE * e + m + 1)
                    dve.tensor_copy(heT[x][0][:, m, :], gelu[x][:, m, :]).then_inc(e_hhi, 1)
                    if m:
                        low(m - 1)
                low(KE - 1)

            def results(e, x, m, begin=False):
                if not begin:
                    dve.wait_ge(ye_out[x], 32 * m)
                dve.wait_ge(e_down, 2 * e + 1)
                dve.tensor_copy(ye[x][:, 0:2, :].rearrange("p t d -> p (t d)"), ring[0][:, :]).then_inc(e_y, 1)
                dve.wait_ge(e_down, 2 * e + 2)
                dve.tensor_copy(ye[x][P - LAST:P, 2, :], ring[1][P - LAST:P, 0:D]).then_inc(e_y, 1)

            low_rows(0, 0)
            split_hidden(0, 0)
            low_rows(1, 1)
            split_hidden(1, 1)
            low_rows(2, 0)
            results(0, 0, 0, True)
            split_hidden(2, 0)
            low_rows(3, 1)
            results(1, 1, 0, True)
            split_hidden(3, 1)
            low_rows(4, 0)
            results(2, 0, 1)
            with dve.Fori(2, E16 // 2 - 1) as j:
                for x in range(2):
                    e = 2 * j + x
                    split_hidden(e, x)
                    low_rows(e + 1, 1 - x)
                    results(e - 1, 1 - x, j + x - 1)
            split_hidden(E16 - 2, 0)
            low_rows(E16 - 1, 1)
            results(E16 - 3, 1, E16 // 2 - 2)
            split_hidden(E16 - 1, 1)
            results(E16 - 2, 0, E16 // 2 - 1)
            results(E16 - 1, 1, E16 // 2 - 1)
            for i in range(NT // 2):
                dve.wait_ge(got_in[i], 16 * TOPK * 2)
                for t in (2 * i, 2 * i + 1):
                    dve.scalar_tensor_tensor(out=h[:, t, :], in0=got[0][:, t, :], scalar=wk[:, 0, t:t + 1], in1=h[:, t, :],
                                             op0=ALU.mult, op1=ALU.add).then_inc(mixed0, 1)
                for t in (2 * i, 2 * i + 1):
                    dve.wait_ge(mixed0, t + 1)
                    dve.scalar_tensor_tensor(out=h[:, t, :], in0=got[1][:, t, :], scalar=wk[:, 1, t:t + 1], in1=h[:, t, :],
                                             op0=ALU.mult, op1=ALU.add).then_inc(mixed, 1)


def kernel(**inputs):
    import numpy as np
    import concourse.bacc as bacc
    from concourse.bass_utils import run_bass_kernel_spmd

    x = {k: np.asarray(v) for k, v in inputs.items()}
    turned = lambda w: np.ascontiguousarray(np.swapaxes(x[w], -1, -2))
    arrays = {n: x[n] for n in x if n.startswith("L0_tok_")
              and n not in ("L0_tok_bup", "L0_tok_wq", "L0_tok_wk", "L0_tok_wv")}
    arrays["L0_ffn_expert_b"] = x["L0_ffn_expert_b"]
    arrays |= {
        "x_cols": np.ascontiguousarray(x["x"].reshape(NT, P).T),
        "bup_cols": np.ascontiguousarray(x["L0_tok_bup"].reshape(LAYERS, KF, P).transpose(2, 0, 1)),
        "attn_qkv": np.concatenate([x[f"L0_tok_w{n}"] for n in "qkv"], axis=2),
        "heads_qk": np.concatenate([np.repeat(turned(f"L0_attn_W_{n}").reshape(D, HEADS, 1, HD), 2, axis=2).reshape(D, 2 * D)
                                    for n in ("query", "key")], axis=1),
        "heads_v": turned("L0_attn_W_value"),
        "heads_proj": turned("L0_attn_W_proj"),
        "gates_t": np.concatenate([turned("L0_ffn_router_w"), turned("L1_ffn_gate_w")], axis=1),
        "router_b": x["L0_ffn_router_b"].reshape(1, E8),
        "top1_t": np.ascontiguousarray(x["L0_ffn_expert_w"].transpose(2, 0, 1).reshape(D, E8 * D)),
        "lin_qkvu": np.concatenate([turned(f"L1_attn_W{n}") for n in "qkvu"], axis=1), "lin_o_t": turned("L1_attn_Wo"),
        "w1_rows": x["L1_ffn_w1"].reshape(E16 * D, DFF), "w2_rows": x["L1_ffn_w2"].reshape(E16 * DFF, D),
    }
    nc = bacc.Bacc("TRN2", target_bir_lowering=False, num_devices=1)
    a, sent = {}, {}
    for name, array in arrays.items():
        sent[f"in_{name}"] = np.ascontiguousarray(array)
        a[name] = nc.dram_tensor(f"in_{name}", array.shape, mybir.dt.from_np(array.dtype), kind="ExternalInput").ap()
    a["out"] = nc.dram_tensor("out_0_dram", (B, T, D), F32, kind="ExternalOutput").ap()
    tower_kernel(nc, a)
    got = run_bass_kernel_spmd(nc, [sent], core_ids=[0])
    return got.results[0]["out_0_dram"]
```
